# Optimizing a Trainium2 kernel written in Bass

```python
import numpy as np
import jax
import jax.numpy as jnp

def _softmax(x, axis=-1):
    return jax.nn.softmax(x, axis=axis)

def _gelu(x):
    return jax.nn.gelu(x, approximate=True)

def _silu(x):
    return jax.nn.silu(x)

def _sigmoid(x):
    return jax.nn.sigmoid(x)

def _layernorm(x, axis=-1, eps=1e-05):
    m = jnp.mean(x, axis=axis, keepdims=True)
    v = jnp.var(x, axis=axis, keepdims=True)
    return (x - m) / jnp.sqrt(v + eps)

def _scatter_add(tgt, idx, src, axis=0):
    return tgt.at[idx].add(src)

def _segment_sum(src, seg, n):
    return jax.ops.segment_sum(src, seg, n)
kernel_name = 'mk_prb_d4_jaxref_r8_137457'

def setup_inputs(seed: int=0):
    np.random.seed(seed)
    _w = jnp.asarray

    def _L0_attn_setup():
        import jax, jax.numpy as jnp
        import numpy as np
        N_HEADS = 16
        BUCKETS = 32
        MAX_REL = 64
        ATT_SPAN = BUCKETS
        LN_EPS = 1e-07

        def make_log_bucket_position(relative_pos, bucket_size, max_position):
            sign = jnp.sign(relative_pos)
            mid = bucket_size // 2
            abs_pos = jnp.where((relative_pos < mid) & (relative_pos > -mid), mid - 1, jnp.abs(relative_pos))
            log_pos = jnp.ceil(jnp.log(abs_pos / mid) / jnp.log((max_position - 1) / mid) * (mid - 1)) + mid
            bucket_pos = jnp.where(abs_pos <= mid, abs_pos, log_pos * sign)
            return bucket_pos.astype(jnp.int32)

        def build_relative_position(q_size, k_size, bucket_size, max_position):
            rel = jnp.arange(q_size)[:, None] - jnp.arange(k_size)[None, :]
            rel = make_log_bucket_position(rel, bucket_size, max_position)
            return rel.astype(jnp.int32)
        key = jax.random.key(seed)
        ks = jax.random.split(key, 16)
        B, S, H = (4, 128, 128)
        std = 0.02
        inp = {'hidden_states': jax.random.normal(ks[0], (B, S, H), jnp.float32), 'attention_mask': jnp.ones((B, S), jnp.float32), 'rel_embeddings': jax.random.normal(ks[1], (2 * ATT_SPAN, H), jnp.float32) * std, 'Wq': jax.random.normal(ks[2], (H, H), jnp.float32) * std, 'bq': jnp.zeros((H,), jnp.float32), 'Wk': jax.random.normal(ks[3], (H, H), jnp.float32) * std, 'bk': jnp.zeros((H,), jnp.float32), 'Wv': jax.random.normal(ks[4], (H, H), jnp.float32) * std, 'bv': jnp.zeros((H,), jnp.float32), 'Wo': jax.random.normal(ks[5], (H, H), jnp.float32) * std, 'bo': jnp.zeros((H,), jnp.float32), 'ln_scale': jnp.ones((H,), jnp.float32), 'ln_bias': jnp.zeros((H,), jnp.float32)}
        return inp
    _L0_attn_in = _L0_attn_setup()

    def _L0_ffn_setup():
        import jax, jax.numpy as jnp
        import numpy as np
        key = jax.random.key(seed)
        kx, kw = jax.random.split(key)
        x = jax.random.normal(kx, (32, 512, 128), dtype=jnp.float32)
        weight = jax.random.normal(kw, (128, 128), dtype=jnp.float32) * 0.01
        return {'x': x, 'weight': weight}
    _L0_ffn_in = _L0_ffn_setup()

    def _L1_attn_setup():
        import jax, jax.numpy as jnp
        import numpy as np

        def _logcumsumexp(x, axis):
            return jax.lax.associative_scan(jnp.logaddexp, x, axis=axis)

        def _log_g(x):
            return jnp.where(x >= 0, jnp.log(jax.nn.relu(x) + 0.5), -jax.nn.softplus(-x))

        def _min_gru(x, Wz, bz, Wh, bh):
            k = x @ Wz + bz
            log_z = -jax.nn.softplus(-k)
            log_coeffs = -jax.nn.softplus(k)
            log_tilde_h = _log_g(x @ Wh + bh)
            a_star = jnp.cumsum(log_coeffs, axis=1)
            log_h = a_star + _logcumsumexp(log_z + log_tilde_h - a_star, axis=1)
            return jnp.exp(log_h)
        key = jax.random.key(seed)
        ks = jax.random.split(key, 7)
        B, S, D, H = (4, 512, 128, 128)
        s_in = 1.0 / np.sqrt(D)
        s_cat = 1.0 / np.sqrt(2 * H)
        return {'x': jax.random.normal(ks[0], (B, S, D), jnp.float32), 'Wz_f': jax.random.normal(ks[1], (D, H), jnp.float32) * s_in, 'bz_f': jnp.zeros((H,), jnp.float32), 'Wh_f': jax.random.normal(ks[2], (D, H), jnp.float32) * s_in, 'bh_f': jnp.zeros((H,), jnp.float32), 'Wz_b': jax.random.normal(ks[3], (D, H), jnp.float32) * s_in, 'bz_b': jnp.zeros((H,), jnp.float32), 'Wh_b': jax.random.normal(ks[4], (D, H), jnp.float32) * s_in, 'bh_b': jnp.zeros((H,), jnp.float32), 'W_out': jax.random.normal(ks[5], (2 * H, H), jnp.float32) * s_cat, 'b_out': jnp.zeros((H,), jnp.float32)}
    _L1_attn_in = _L1_attn_setup()

    def _L1_ffn_setup():
        import jax, jax.numpy as jnp
        import numpy as np
        NUM_EXPERTS = 8
        NUM_SELECTED = 2
        EXPERT_CAPACITY = 64
        NUM_GROUPS = 8

        def _routing(xg, w_router):
            G, T, H = xg.shape
            logits = jnp.einsum('gth,he->gte', xg, w_router)
            probs = jax.nn.softmax(logits, axis=-1)
            _gate, idx = jax.lax.top_k(probs, NUM_SELECTED)
            idx_kt = jnp.swapaxes(idx, 1, 2).reshape(G, -1)
            expert_mask = jax.nn.one_hot(idx_kt, NUM_EXPERTS, dtype=jnp.int32)
            priority = jnp.cumsum(expert_mask, axis=1) * expert_mask - 1
            priority = priority.reshape(G, NUM_SELECTED, T, NUM_EXPERTS)
            priority = jnp.swapaxes(priority, 1, 2).max(axis=2)
            dispatch = jax.nn.one_hot(priority, EXPERT_CAPACITY, dtype=xg.dtype)
            combine = probs[..., None] * dispatch
            return (dispatch, combine)
        key = jax.random.key(seed)
        k1, k2, k3, k4 = jax.random.split(key, 4)
        B, S, H, F = (8, 256, 128, 512)
        return {'x': jax.random.normal(k1, (B, S, H), jnp.float32), 'w_router': jax.random.normal(k2, (H, NUM_EXPERTS), jnp.float32) * 0.02, 'wi': jax.random.normal(k3, (NUM_EXPERTS, H, F), jnp.float32) * 0.02, 'wo': jax.random.normal(k4, (NUM_EXPERTS, F, H), jnp.float32) * 0.02}
    _L1_ffn_in = _L1_ffn_setup()

    def _L2_attn_setup():
        import jax, jax.numpy as jnp
        import numpy as np
        HEADS = 8
        DIM_HEAD = 128
        ATTN_MATRIX_SCALE = 1.5
        SCALE = DIM_HEAD ** (-0.5)

        def _split_heads(t):
            b, n, _ = t.shape
            t = t.reshape(b, n, HEADS, DIM_HEAD)
            return t.transpose(2, 0, 1, 3).reshape(HEADS, b * n, DIM_HEAD)
        key = jax.random.key(seed)
        ks = jax.random.split(key, 7)
        b, n, m = (2, 256, 256)
        qd, cd, inner = (128, 96, HEADS * DIM_HEAD)
        x = jax.random.normal(ks[0], (b, n, qd), dtype=jnp.float32)
        context = jax.random.normal(ks[1], (b, m, cd), dtype=jnp.float32)
        Wq = jax.random.normal(ks[2], (qd, inner), dtype=jnp.float32) * qd ** (-0.5)
        Wk = jax.random.normal(ks[3], (cd, inner), dtype=jnp.float32) * cd ** (-0.5)
        Wv = jax.random.normal(ks[4], (cd, inner), dtype=jnp.float32) * cd ** (-0.5)
        Wout = jax.random.normal(ks[5], (inner, qd), dtype=jnp.float32) * inner ** (-0.5)
        bout = jnp.zeros((qd,), dtype=jnp.float32)
        return {'x': x, 'context': context, 'Wq': Wq, 'Wk': Wk, 'Wv': Wv, 'Wout': Wout, 'bout': bout}
    _L2_attn_in = _L2_attn_setup()

    def _L2_ffn_setup():
        import jax, jax.numpy as jnp
        import numpy as np
        DIM = 128

        def _reference_tuple_inner(x, W_r, W_k, W_v, mu_r, mu_k):
            B, T, C = x.shape
            x_prev = jnp.concatenate([jnp.zeros((B, 1, C), x.dtype), x[:, :-1, :]], axis=1)
            xr = mu_r * x + (1.0 - mu_r) * x_prev
            xk = mu_k * x + (1.0 - mu_k) * x_prev
            r = jax.nn.sigmoid(jnp.einsum('btc,dc->btd', xr, W_r))
            k = jnp.einsum('btc,dc->btd', xk, W_k)
            k_act = jnp.square(jax.nn.relu(k))
            out = r * jnp.einsum('btc,dc->btd', k_act, W_v)
            new_state = x[:, -1, :]
            return (out, new_state)
        key = jax.random.key(seed)
        ks = jax.random.split(key, 6)
        B, T, C = (8, 256, DIM)
        x = jax.random.normal(ks[0], (B, T, C), dtype=jnp.float32)
        s = 1.0 / np.sqrt(C)
        W_r = jax.random.uniform(ks[1], (C, C), jnp.float32, -s, s)
        W_k = jax.random.uniform(ks[2], (C, C), jnp.float32, -s, s)
        W_v = jax.random.uniform(ks[3], (C, C), jnp.float32, -s, s)
        mu_r = jax.random.uniform(ks[4], (C,), jnp.float32)
        mu_k = jax.random.uniform(ks[5], (C,), jnp.float32)
        return {'x': x, 'W_r': W_r, 'W_k': W_k, 'W_v': W_v, 'mu_r': mu_r, 'mu_k': mu_k}
    _L2_ffn_in = _L2_ffn_setup()

    def _L3_attn_setup():
        import jax, jax.numpy as jnp
        import numpy as np
        EPS = 1e-05

        def _layernorm(x, gamma, beta):
            m = jnp.mean(x, axis=-1, keepdims=True)
            v = jnp.mean(jnp.square(x - m), axis=-1, keepdims=True)
            return (x - m) * jax.lax.rsqrt(v + EPS) * gamma + beta
        key = jax.random.key(seed)
        B, Q, C, H = (4, 512, 128, 16)
        hd = C // H
        ks = jax.random.split(key, 8)
        s_in = 1.0 / np.sqrt(C)
        return {'x': jax.random.normal(ks[0], (B, Q, C), jnp.float32), 'qkv_w': jax.random.normal(ks[1], (3 * C, C), jnp.float32) * s_in, 'qkv_b': jnp.zeros((3 * C,), jnp.float32), 'kn_g': jnp.ones((hd,), jnp.float32), 'kn_b': jnp.zeros((hd,), jnp.float32), 'vn_g': jnp.ones((hd,), jnp.float32), 'vn_b': jnp.zeros((hd,), jnp.float32), 'temperature': jnp.ones((H, 1, 1), jnp.float32), 'attn_bias': jnp.zeros((H, hd, hd), jnp.float32), 'p1_w': jax.random.normal(ks[2], (C, C), jnp.float32) * s_in, 'p1_b': jnp.zeros((C,), jnp.float32), 'p2_w': jax.random.normal(ks[3], (C, C), jnp.float32) * s_in, 'p2_b': jnp.zeros((C,), jnp.float32)}
    _L3_attn_in = _L3_attn_setup()

    def _L3_ffn_setup():
        import jax, jax.numpy as jnp
        import numpy as np
        B, N, D = (4, 512, 128)
        E, S, F = (16, 64, 256)
        DO = 128
        EPS = 1e-05

        def _layernorm(x, g, b):
            mu = jnp.mean(x, axis=-1, keepdims=True)
            var = jnp.mean(jnp.square(x - mu), axis=-1, keepdims=True)
            return (x - mu) * jax.lax.rsqrt(var + EPS) * g + b
        key = jax.random.key(seed)
        ks = jax.random.split(key, 8)
        d = {'x': jax.random.normal(ks[0], (B, N, D), dtype=jnp.float32), 'norm_g': jnp.ones((D,), jnp.float32), 'norm_b': jnp.zeros((D,), jnp.float32), 'slot_g': jnp.ones((D,), jnp.float32), 'slot_b': jnp.zeros((D,), jnp.float32), 'scale': jnp.ones((1,), jnp.float32), 'slot_embeds': jax.random.normal(ks[1], (E, S, D), jnp.float32) / np.sqrt(D), 'Wg': jax.random.normal(ks[2], (E, D, F), jnp.float32) * np.sqrt(2.0 / (D + F)), 'bg': jnp.zeros((E, F), jnp.float32), 'Wu': jax.random.normal(ks[3], (E, D, F), jnp.float32) * np.sqrt(2.0 / (D + F)), 'bu': jnp.zeros((E, F), jnp.float32), 'Wd': jax.random.normal(ks[4], (E, F, DO), jnp.float32) * np.sqrt(2.0 / (F + DO)), 'bd': jnp.zeros((E, DO), jnp.float32)}
        return d
    _L3_ffn_in = _L3_ffn_setup()
    _d = {'L0_attn_hidden_states': _L0_attn_in['hidden_states'], 'L0_attn_attention_mask': _L0_attn_in['attention_mask'], 'L0_attn_rel_embeddings': _L0_attn_in['rel_embeddings'], 'L0_attn_Wq': _L0_attn_in['Wq'], 'L0_attn_bq': _L0_attn_in['bq'], 'L0_attn_Wk': _L0_attn_in['Wk'], 'L0_attn_bk': _L0_attn_in['bk'], 'L0_attn_Wv': _L0_attn_in['Wv'], 'L0_attn_bv': _L0_attn_in['bv'], 'L0_attn_Wo': _L0_attn_in['Wo'], 'L0_attn_bo': _L0_attn_in['bo'], 'L0_attn_ln_scale': _L0_attn_in['ln_scale'], 'L0_attn_ln_bias': _L0_attn_in['ln_bias'], 'L0_ffn_weight': _L0_ffn_in['weight'], 'L1_attn_Wz_f': _L1_attn_in['Wz_f'], 'L1_attn_bz_f': _L1_attn_in['bz_f'], 'L1_attn_Wh_f': _L1_attn_in['Wh_f'], 'L1_attn_bh_f': _L1_attn_in['bh_f'], 'L1_attn_Wz_b': _L1_attn_in['Wz_b'], 'L1_attn_bz_b': _L1_attn_in['bz_b'], 'L1_attn_Wh_b': _L1_attn_in['Wh_b'], 'L1_attn_bh_b': _L1_attn_in['bh_b'], 'L1_attn_W_out': _L1_attn_in['W_out'], 'L1_attn_b_out': _L1_attn_in['b_out'], 'L1_ffn_w_router': _L1_ffn_in['w_router'], 'L1_ffn_wi': _L1_ffn_in['wi'], 'L1_ffn_wo': _L1_ffn_in['wo'], 'L2_attn_context': _L2_attn_in['context'], 'L2_attn_Wq': _L2_attn_in['Wq'], 'L2_attn_Wk': _L2_attn_in['Wk'], 'L2_attn_Wv': _L2_attn_in['Wv'], 'L2_attn_Wout': _L2_attn_in['Wout'], 'L2_attn_bout': _L2_attn_in['bout'], 'L2_ffn_W_r': _L2_ffn_in['W_r'], 'L2_ffn_W_k': _L2_ffn_in['W_k'], 'L2_ffn_W_v': _L2_ffn_in['W_v'], 'L2_ffn_mu_r': _L2_ffn_in['mu_r'], 'L2_ffn_mu_k': _L2_ffn_in['mu_k'], 'L3_attn_qkv_w': _L3_attn_in['qkv_w'], 'L3_attn_qkv_b': _L3_attn_in['qkv_b'], 'L3_attn_kn_g': _L3_attn_in['kn_g'], 'L3_attn_kn_b': _L3_attn_in['kn_b'], 'L3_attn_vn_g': _L3_attn_in['vn_g'], 'L3_attn_vn_b': _L3_attn_in['vn_b'], 'L3_attn_temperature': _L3_attn_in['temperature'], 'L3_attn_attn_bias': _L3_attn_in['attn_bias'], 'L3_attn_p1_w': _L3_attn_in['p1_w'], 'L3_attn_p1_b': _L3_attn_in['p1_b'], 'L3_attn_p2_w': _L3_attn_in['p2_w'], 'L3_attn_p2_b': _L3_attn_in['p2_b'], 'L3_ffn_norm_g': _L3_ffn_in['norm_g'], 'L3_ffn_norm_b': _L3_ffn_in['norm_b'], 'L3_ffn_slot_g': _L3_ffn_in['slot_g'], 'L3_ffn_slot_b': _L3_ffn_in['slot_b'], 'L3_ffn_scale': _L3_ffn_in['scale'], 'L3_ffn_slot_embeds': _L3_ffn_in['slot_embeds'], 'L3_ffn_Wg': _L3_ffn_in['Wg'], 'L3_ffn_bg': _L3_ffn_in['bg'], 'L3_ffn_Wu': _L3_ffn_in['Wu'], 'L3_ffn_bu': _L3_ffn_in['bu'], 'L3_ffn_Wd': _L3_ffn_in['Wd'], 'L3_ffn_bd': _L3_ffn_in['bd']}
    _x0 = _d['L0_attn_hidden_states']
    _d['L0_attn_hidden_states'] = jax.random.normal(jax.random.fold_in(jax.random.key(seed), 1), (8, 512, 128), dtype=_x0.dtype)
    del _x0
    return _d

def reference(L0_attn_hidden_states, L0_attn_attention_mask, L0_attn_rel_embeddings, L0_attn_Wq, L0_attn_bq, L0_attn_Wk, L0_attn_bk, L0_attn_Wv, L0_attn_bv, L0_attn_Wo, L0_attn_bo, L0_attn_ln_scale, L0_attn_ln_bias, L0_ffn_weight, L1_attn_Wz_f, L1_attn_bz_f, L1_attn_Wh_f, L1_attn_bh_f, L1_attn_Wz_b, L1_attn_bz_b, L1_attn_Wh_b, L1_attn_bh_b, L1_attn_W_out, L1_attn_b_out, L1_ffn_w_router, L1_ffn_wi, L1_ffn_wo, L2_attn_context, L2_attn_Wq, L2_attn_Wk, L2_attn_Wv, L2_attn_Wout, L2_attn_bout, L2_ffn_W_r, L2_ffn_W_k, L2_ffn_W_v, L2_ffn_mu_r, L2_ffn_mu_k, L3_attn_qkv_w, L3_attn_qkv_b, L3_attn_kn_g, L3_attn_kn_b, L3_attn_vn_g, L3_attn_vn_b, L3_attn_temperature, L3_attn_attn_bias, L3_attn_p1_w, L3_attn_p1_b, L3_attn_p2_w, L3_attn_p2_b, L3_ffn_norm_g, L3_ffn_norm_b, L3_ffn_slot_g, L3_ffn_slot_b, L3_ffn_scale, L3_ffn_slot_embeds, L3_ffn_Wg, L3_ffn_bg, L3_ffn_Wu, L3_ffn_bu, L3_ffn_Wd, L3_ffn_bd):

    def _L0_attn_ref(hidden_states, attention_mask, rel_embeddings, Wq, bq, Wk, bk, Wv, bv, Wo, bo, ln_scale, ln_bias):
        import jax, jax.numpy as jnp
        import numpy as np
        N_HEADS = 16
        BUCKETS = 32
        MAX_REL = 64
        ATT_SPAN = BUCKETS
        LN_EPS = 1e-07

        def make_log_bucket_position(relative_pos, bucket_size, max_position):
            sign = jnp.sign(relative_pos)
            mid = bucket_size // 2
            abs_pos = jnp.where((relative_pos < mid) & (relative_pos > -mid), mid - 1, jnp.abs(relative_pos))
            log_pos = jnp.ceil(jnp.log(abs_pos / mid) / jnp.log((max_position - 1) / mid) * (mid - 1)) + mid
            bucket_pos = jnp.where(abs_pos <= mid, abs_pos, log_pos * sign)
            return bucket_pos.astype(jnp.int32)

        def build_relative_position(q_size, k_size, bucket_size, max_position):
            rel = jnp.arange(q_size)[:, None] - jnp.arange(k_size)[None, :]
            rel = make_log_bucket_position(rel, bucket_size, max_position)
            return rel.astype(jnp.int32)
        B, S, H = hidden_states.shape
        nH = N_HEADS
        d = H // nH

        def split_heads(x):
            return jnp.transpose(x.reshape(B, S, nH, d), (0, 2, 1, 3))
        q = split_heads(hidden_states @ Wq + bq)
        k = split_heads(hidden_states @ Wk + bk)
        v = split_heads(hidden_states @ Wv + bv)
        scale_factor = 3
        scale = jnp.sqrt(jnp.asarray(d * scale_factor, hidden_states.dtype))
        scores = jnp.einsum('bhqd,bhkd->bhqk', q, k) / scale
        rel = build_relative_position(S, S, BUCKETS, MAX_REL)
        pos_k = (rel_embeddings @ Wk + bk).reshape(2 * ATT_SPAN, nH, d)
        pos_k = jnp.transpose(pos_k, (1, 0, 2))
        c2p_att = jnp.einsum('bhqd,hpd->bhqp', q, pos_k)
        c2p_pos = jnp.clip(rel + ATT_SPAN, 0, 2 * ATT_SPAN - 1)
        c2p = jnp.take_along_axis(c2p_att, jnp.broadcast_to(c2p_pos[None, None], (B, nH, S, S)), axis=-1)
        p2c_pos = jnp.clip(-rel + ATT_SPAN, 0, 2 * ATT_SPAN - 1)
        p2c_att = jnp.einsum('bhkd,hpd->bhkp', k, pos_k)
        p2c = jnp.take_along_axis(p2c_att, jnp.broadcast_to(p2c_pos[None, None], (B, nH, S, S)), axis=-1)
        p2c = jnp.swapaxes(p2c, -1, -2)
        scores = scores + (c2p + p2c) / scale
        probs = jax.nn.softmax(scores, axis=-1)
        ctx = jnp.einsum('bhqk,bhkd->bhqd', probs, v)
        ctx = jnp.transpose(ctx, (0, 2, 1, 3)).reshape(B, S, H)
        out = ctx @ Wo + bo + hidden_states
        mu = jnp.mean(out, axis=-1, keepdims=True)
        var = jnp.mean(jnp.square(out - mu), axis=-1, keepdims=True)
        out = (out - mu) * jax.lax.rsqrt(var + LN_EPS) * ln_scale + ln_bias
        return out

    def _L0_ffn_ref(x, weight):
        import jax, jax.numpy as jnp
        import numpy as np
        b_weight = jnp.sign(weight)
        return jnp.einsum('bsi,oi->bso', x, b_weight)

    def _L1_attn_ref(x, Wz_f, bz_f, Wh_f, bh_f, Wz_b, bz_b, Wh_b, bh_b, W_out, b_out):
        import jax, jax.numpy as jnp
        import numpy as np

        def _logcumsumexp(x, axis):
            return jax.lax.associative_scan(jnp.logaddexp, x, axis=axis)

        def _log_g(x):
            return jnp.where(x >= 0, jnp.log(jax.nn.relu(x) + 0.5), -jax.nn.softplus(-x))

        def _min_gru(x, Wz, bz, Wh, bh):
            k = x @ Wz + bz
            log_z = -jax.nn.softplus(-k)
            log_coeffs = -jax.nn.softplus(k)
            log_tilde_h = _log_g(x @ Wh + bh)
            a_star = jnp.cumsum(log_coeffs, axis=1)
            log_h = a_star + _logcumsumexp(log_z + log_tilde_h - a_star, axis=1)
            return jnp.exp(log_h)
        x_rev = jnp.flip(x, axis=1)
        out_fwd = _min_gru(x, Wz_f, bz_f, Wh_f, bh_f)
        out_bwd = _min_gru(x_rev, Wz_b, bz_b, Wh_b, bh_b)
        concat = jnp.concatenate([out_fwd, out_bwd], axis=2)
        return concat @ W_out + b_out

    def _L1_ffn_ref(x, w_router, wi, wo):
        import jax, jax.numpy as jnp
        import numpy as np
        NUM_EXPERTS = 8
        NUM_SELECTED = 2
        EXPERT_CAPACITY = 64
        NUM_GROUPS = 8

        def _routing(xg, w_router):
            G, T, H = xg.shape
            logits = jnp.einsum('gth,he->gte', xg, w_router)
            probs = jax.nn.softmax(logits, axis=-1)
            _gate, idx = jax.lax.top_k(probs, NUM_SELECTED)
            idx_kt = jnp.swapaxes(idx, 1, 2).reshape(G, -1)
            expert_mask = jax.nn.one_hot(idx_kt, NUM_EXPERTS, dtype=jnp.int32)
            priority = jnp.cumsum(expert_mask, axis=1) * expert_mask - 1
            priority = priority.reshape(G, NUM_SELECTED, T, NUM_EXPERTS)
            priority = jnp.swapaxes(priority, 1, 2).max(axis=2)
            dispatch = jax.nn.one_hot(priority, EXPERT_CAPACITY, dtype=xg.dtype)
            combine = probs[..., None] * dispatch
            return (dispatch, combine)
        B, S, H = x.shape
        T = B * S // NUM_GROUPS
        xg = x.reshape(NUM_GROUPS, T, H)
        dispatch, combine = _routing(xg, w_router)
        expert_in = jnp.einsum('gth,gtec->gech', xg, dispatch)
        h = jax.nn.gelu(jnp.einsum('gech,ehf->gecf', expert_in, wi))
        expert_out = jnp.einsum('gecf,efh->gech', h, wo)
        out = jnp.einsum('gech,gtec->gth', expert_out, combine)
        return out.reshape(B, S, H)

    def _L2_attn_ref(x, context, Wq, Wk, Wv, Wout, bout):
        import jax, jax.numpy as jnp
        import numpy as np
        HEADS = 8
        DIM_HEAD = 128
        ATTN_MATRIX_SCALE = 1.5
        SCALE = DIM_HEAD ** (-0.5)

        def _split_heads(t):
            b, n, _ = t.shape
            t = t.reshape(b, n, HEADS, DIM_HEAD)
            return t.transpose(2, 0, 1, 3).reshape(HEADS, b * n, DIM_HEAD)
        b, n, _ = x.shape
        qh = _split_heads(jnp.einsum('bnq,qi->bni', x, Wq))
        kh = _split_heads(jnp.einsum('bmc,ci->bmi', context, Wk))
        vh = _split_heads(jnp.einsum('bmc,ci->bmi', context, Wv))
        sim = jnp.einsum('hid,hjd->hij', qh, kh) * SCALE
        mean = jnp.mean(sim, axis=-1, keepdims=True)
        sim = (sim - mean) * ATTN_MATRIX_SCALE + mean
        attn = jax.nn.softmax(sim, axis=-1)
        out = jnp.einsum('hij,hjd->hid', attn, vh)
        out = out.reshape(HEADS, b, n, DIM_HEAD).transpose(1, 2, 0, 3)
        out = out.reshape(b, n, HEADS * DIM_HEAD)
        return jnp.einsum('bni,iq->bnq', out, Wout) + bout

    def _L2_ffn_ref(x, W_r, W_k, W_v, mu_r, mu_k):
        import jax, jax.numpy as jnp
        import numpy as np
        DIM = 128

        def _reference_tuple_inner(x, W_r, W_k, W_v, mu_r, mu_k):
            B, T, C = x.shape
            x_prev = jnp.concatenate([jnp.zeros((B, 1, C), x.dtype), x[:, :-1, :]], axis=1)
            xr = mu_r * x + (1.0 - mu_r) * x_prev
            xk = mu_k * x + (1.0 - mu_k) * x_prev
            r = jax.nn.sigmoid(jnp.einsum('btc,dc->btd', xr, W_r))
            k = jnp.einsum('btc,dc->btd', xk, W_k)
            k_act = jnp.square(jax.nn.relu(k))
            out = r * jnp.einsum('btc,dc->btd', k_act, W_v)
            new_state = x[:, -1, :]
            return (out, new_state)
        return _reference_tuple_inner(x, W_r, W_k, W_v, mu_r, mu_k)[0]

    def _L3_attn_ref(x, qkv_w, qkv_b, kn_g, kn_b, vn_g, vn_b, temperature, attn_bias, p1_w, p1_b, p2_w, p2_b):
        import jax, jax.numpy as jnp
        import numpy as np
        EPS = 1e-05

        def _layernorm(x, gamma, beta):
            m = jnp.mean(x, axis=-1, keepdims=True)
            v = jnp.mean(jnp.square(x - m), axis=-1, keepdims=True)
            return (x - m) * jax.lax.rsqrt(v + EPS) * gamma + beta
        B, Q, C = x.shape
        H = temperature.shape[0]
        hd = C // H
        qkv = (x @ qkv_w.T + qkv_b).reshape(B, Q, 3, H, hd)
        qkv = jnp.transpose(qkv, (2, 0, 3, 1, 4))
        q, k, v = (qkv[0], qkv[1], qkv[2])
        k = _layernorm(k, kn_g, kn_b)
        v = _layernorm(v, vn_g, vn_b)
        kv = jnp.einsum('bhqd,bhqe->bhde', k, v) / Q * temperature + attn_bias
        att = jnp.einsum('bhqd,bhde->bhqe', q, kv)
        att = jnp.transpose(att, (0, 2, 1, 3)).reshape(B, Q, C) + x
        h = jax.nn.gelu(att @ p1_w.T + p1_b, approximate=False)
        return h @ p2_w.T + p2_b + x

    def _L3_ffn_ref(x, norm_g, norm_b, slot_g, slot_b, scale, slot_embeds, Wg, bg, Wu, bu, Wd, bd):
        import jax, jax.numpy as jnp
        import numpy as np
        B, N, D = (4, 512, 128)
        E, S, F = (16, 64, 256)
        DO = 128
        EPS = 1e-05

        def _layernorm(x, g, b):
            mu = jnp.mean(x, axis=-1, keepdims=True)
            var = jnp.mean(jnp.square(x - mu), axis=-1, keepdims=True)
            return (x - mu) * jax.lax.rsqrt(var + EPS) * g + b
        x = _layernorm(x, norm_g, norm_b)
        se = _layernorm(slot_embeds, slot_g, slot_b) * scale
        logits = jnp.einsum('bnd,esd->bnes', x, se)
        dispatch = jax.nn.softmax(logits, axis=1)
        combine = jax.nn.softmax(logits.reshape(x.shape[0], x.shape[1], -1), axis=-1)
        slots = jnp.einsum('bnd,bnes->besd', x, dispatch)
        gate = jax.nn.gelu(jnp.einsum('besd,edf->besf', slots, Wg) + bg[None, :, None, :], approximate=False)
        up = jnp.einsum('besd,edf->besf', slots, Wu) + bu[None, :, None, :]
        eout = jnp.einsum('besf,efo->beso', gate * up, Wd) + bd[None, :, None, :]
        eout = eout.reshape(eout.shape[0], -1, eout.shape[-1])
        return jnp.einsum('bns,bso->bno', combine, eout)
    x = L0_attn_hidden_states
    xn = _layernorm(x, axis=-1)
    x = x + _L0_attn_ref(xn, L0_attn_attention_mask, L0_attn_rel_embeddings, L0_attn_Wq, L0_attn_bq, L0_attn_Wk, L0_attn_bk, L0_attn_Wv, L0_attn_bv, L0_attn_Wo, L0_attn_bo, L0_attn_ln_scale, L0_attn_ln_bias) + _L0_ffn_ref(xn, L0_ffn_weight)
    xn = _layernorm(x, axis=-1)
    x = x + _L1_attn_ref(xn, L1_attn_Wz_f, L1_attn_bz_f, L1_attn_Wh_f, L1_attn_bh_f, L1_attn_Wz_b, L1_attn_bz_b, L1_attn_Wh_b, L1_attn_bh_b, L1_attn_W_out, L1_attn_b_out) + _L1_ffn_ref(xn, L1_ffn_w_router, L1_ffn_wi, L1_ffn_wo)
    xn = _layernorm(x, axis=-1)
    x = x + _L2_attn_ref(xn, L2_attn_context, L2_attn_Wq, L2_attn_Wk, L2_attn_Wv, L2_attn_Wout, L2_attn_bout) + _L2_ffn_ref(xn, L2_ffn_W_r, L2_ffn_W_k, L2_ffn_W_v, L2_ffn_mu_r, L2_ffn_mu_k)
    xn = _layernorm(x, axis=-1)
    x = x + _L3_attn_ref(xn, L3_attn_qkv_w, L3_attn_qkv_b, L3_attn_kn_g, L3_attn_kn_b, L3_attn_vn_g, L3_attn_vn_b, L3_attn_temperature, L3_attn_attn_bias, L3_attn_p1_w, L3_attn_p1_b, L3_attn_p2_w, L3_attn_p2_b) + _L3_ffn_ref(xn, L3_ffn_norm_g, L3_ffn_norm_b, L3_ffn_slot_g, L3_ffn_slot_b, L3_ffn_scale, L3_ffn_slot_embeds, L3_ffn_Wg, L3_ffn_bg, L3_ffn_Wu, L3_ffn_bu, L3_ffn_Wd, L3_ffn_bd)
    return x

_drawn_inputs = setup_inputs


def setup_inputs(seed=0):
    import zlib

    import numpy as np

    out = dict(_drawn_inputs(seed))
    spreads = {'L0_attn_bq': (0.0, 0.8),
     'L0_attn_bk': (0.0, 0.8),
     'L0_attn_bv': (0.0, 0.8),
     'L0_attn_bo': (0.0, 0.8),
     'L0_attn_ln_scale': (1.0, 0.6),
     'L0_attn_ln_bias': (0.0, 0.8),
     'L1_attn_bz_f': (0.0, 2.0),
     'L1_attn_bh_f': (0.0, 2.0),
     'L1_attn_bz_b': (0.0, 2.0),
     'L1_attn_bh_b': (0.0, 2.0),
     'L1_attn_b_out': (0.0, 0.8),
     'L2_attn_bout': (0.0, 2.0),
     'L3_attn_qkv_b': (0.0, 2.0),
     'L3_attn_kn_g': (1.0, 0.6),
     'L3_attn_kn_b': (0.0, 2.0),
     'L3_attn_vn_g': (1.0, 0.6),
     'L3_attn_vn_b': (0.0, 2.0),
     'L3_attn_temperature': (1.0, 0.6),
     'L3_attn_attn_bias': (0.0, 2.0),
     'L3_attn_p1_b': (0.0, 2.0),
     'L3_attn_p2_b': (0.0, 2.0),
     'L3_ffn_norm_g': (1.0, 0.6),
     'L3_ffn_norm_b': (0.0, 2.0),
     'L3_ffn_slot_g': (1.0, 0.6),
     'L3_ffn_slot_b': (0.0, 2.0),
     'L3_ffn_bg': (0.0, 2.0),
     'L3_ffn_bu': (0.0, 2.0),
     'L3_ffn_bd': (0.0, 2.0)}
    factors = {'L0_attn_rel_embeddings': 8.0,
     'L0_attn_Wq': 8.0,
     'L0_attn_Wk': 8.0,
     'L0_attn_Wv': 8.0,
     'L0_attn_Wo': 8.0,
     'L1_attn_Wz_f': 4.469,
     'L1_attn_Wz_b': 4.874,
     'L1_ffn_w_router': 8.0,
     'L1_ffn_wi': 8.0,
     'L1_ffn_wo': 8.0,
     'L2_attn_context': 16.662,
     'L2_attn_Wq': 10.695,
     'L2_attn_Wk': 10.662,
     'L2_attn_Wv': 10.362,
     'L2_attn_Wout': 10.452,
     'L2_ffn_W_r': 8.0,
     'L2_ffn_W_k': 8.0,
     'L2_ffn_W_v': 7.888,
     'L2_ffn_mu_r': 8.0,
     'L2_ffn_mu_k': 8.0,
     'L3_attn_qkv_w': 8.0,
     'L3_attn_p1_w': 8.0,
     'L3_attn_p2_w': 8.0,
     'L3_ffn_slot_embeds': 8.0,
     'L3_ffn_Wg': 8.0,
     'L3_ffn_Wu': 8.0,
     'L3_ffn_Wd': 8.0}
    for name, (base, spread) in spreads.items():
        noise = np.random.default_rng([zlib.crc32(name.encode()), seed]).standard_normal(out[name].shape)
        drawn = base * np.exp(spread * noise) if base else spread * noise
        out[name] = jnp.asarray(drawn.astype(out[name].dtype))
    for name, factor in factors.items():
        out[name] = (out[name] * factor).astype(out[name].dtype)
    return out
```

```python
import numpy as np
from contextlib import ExitStack
import concourse.bass as bass
from concourse import mybir

F32 = mybir.dt.float32
ACT = mybir.ActivationFunctionType
ALU = mybir.AluOpType
AX = mybir.AxisListType


class Queues:
    ENG = ("tensor", "vector", "scalar", "gpsimd", "sync")

    def __init__(self, nc, ctx):
        self.nc, self.ctx = nc, ctx
        self.q = {e: [] for e in self.ENG}
        self.sem = {e: ctx.enter_context(nc.semaphore("s_" + e)) for e in self.ENG}
        self.n = {e: 0 for e in self.ENG}
        self.seen = {e: {} for e in self.ENG}
        self.dsem, self.dn = {}, {}

    def _waits(self, e, waits):
        flat = []

        def walk(w):
            if w is None:
                return
            if isinstance(w, tuple) and w and isinstance(w[0], str):
                flat.append(w)
            else:
                for x in w:
                    walk(x)
        walk(waits)
        most = {}
        for name, sem, v in flat:
            if v > most.get(name, (None, 0))[1]:
                most[name] = (sem, v)
        for name, (sem, v) in most.items():
            if self.seen[e].get(name, 0) < v:
                self.seen[e][name] = v
                self.q[e].append(("w", sem, v))

    def op(self, e, fn, *waits):
        self._waits(e, waits)
        self.n[e] += 1
        self.q[e].append(("i", fn, self.sem[e], 1))
        return (e, self.sem[e], self.n[e])

    def dma(self, e, name, out, in_, *waits):
        self._waits(e, waits)
        if name not in self.dsem:
            self.dsem[name] = self.ctx.enter_context(self.nc.semaphore("d_" + name))
            self.dn[name] = 0
        self.dn[name] += 16
        self.q[e].append(("i", lambda g: g.dma_start(out, in_), self.dsem[name], 16))
        return (name, self.dsem[name], self.dn[name])

    def last(self):
        return [(e, self.sem[e], self.n[e]) for e in self.ENG if self.n[e]]

    def alldma(self):
        return [(n, self.dsem[n], self.dn[n]) for n in self.dsem]

    def emit(self, block):
        def run(e):
            def body(g):
                for item in self.q[e]:
                    if item[0] == "w":
                        g.wait_ge(item[1], item[2])
                    else:
                        item[1](g).then_inc(item[2], item[3])
            return body
        block.tensor(run("tensor"))
        block.vector(run("vector"))
        block.scalar(run("scalar"))
        block.gpsimd(run("gpsimd"))
        block.sync(run("sync"))


class Ring:

    def __init__(self, bufs, free=()):
        self.bufs, self.free, self.i = bufs, [list(free) for _ in bufs], 0

    def take(self):
        k = self.i % len(self.bufs)
        self.i += 1
        free, self.free[k] = self.free[k], None
        assert free is not None, "the buffer is still in use"
        return k, self.bufs[k], free

    def done(self, k, *tokens):
        self.free[k] = list(tokens)


NB, NT, NH = 8, 32, 16
SEQ = 512
SLOTS = 6
PITCH = 256
SLOT = 512 * PITCH + 256

_FAR = [0] + [1] * 6 + [2] * 5 + [3] * 5 + [4] * 4 + [5] * 4 + [6] * 3 + [7] * 3 + [8] * 3 + [9] * 3
_FAR += [10] * 2 + [11] * 2 + [12] * 2 + [13] * 2 + [14] * 2 + [15]


def buckets(near, edge):
    out = {}
    for n, f in enumerate(_FAR):
        r = -64 + n
        out[r] = f
        out[-r] = min(64 - f, 63)
    for r in range(-15, 16):
        out[r] = near
    out[16] = out[-16] = edge
    return out


def constants():
    c = {}
    c["ident"] = np.eye(128, dtype=np.float32)
    i = np.arange(128)
    c["tric"] = (i[None, :] < i[:, None]).astype(np.float32)
    c["trid"] = (i[None, :] > i[:, None]).astype(np.float32)
    c["trile"] = (i[:, None] <= i[None, :]).astype(np.float32)
    oc, od = np.zeros((64, 128), np.float32), np.zeros((64, 128), np.float32)
    bc, bd = buckets(47, 48), buckets(17, 16)
    oc[63, 0] = od[63, 0] = 1
    oc[0, 0] = od[0, 0] = -1
    for s in range(1, 128):
        r = 64 - s
        oc[bc[r], s] += 1
        oc[63 if r > 0 else 0, s] -= 1
        r = s - 64
        od[bd[r], s] += 1
        od[63 if r > 0 else 0, s] -= 1
    ends = np.zeros((64, 2), np.float32)
    ends[63, 0] = 1
    ends[0, 1] = 1
    c["oh"] = np.concatenate([oc, od, ends], axis=1)
    c["iota"] = np.tile(np.arange(64, dtype=np.float32)[None, :], (128, 1))
    c["rev"] = np.tile(np.arange(8, 0, -1).astype(np.float32)[None, :], (128, 1))
    head = i // 8
    c["bdmask"] = (head[:, None] == head[None, :]).astype(np.float32)
    return c


def program(nc, a, out):
    ctx = ExitStack()
    with ctx:
        def sb(name, shape):
            return ctx.enter_context(nc.sbuf_tensor(name, shape, F32))

        X = sb("X", [128, NT, 128])
        XN = sb("XN", [128, NT, 128])
        XT = sb("XT", [128, NT * 128])
        ident = sb("ident", [128, 128])
        ones = sb("ones", [1, 512])
        ARENA = 38600
        AR = sb("AR", [128, ARENA])
        PS = ctx.enter_context(nc.psum_tensor("PS", [128, 8, 512], F32))
        scr = nc.dram_tensor("scr", [2 * SLOTS, SLOT], F32, kind="Internal").ap()
        Q = Queues(nc, ctx)
        top = [0]

        def take(*dims, rows=128):
            n = int(np.prod(dims))
            ap = AR[0:rows, top[0]:top[0] + n]
            top[0] += n
            assert top[0] <= ARENA, top[0]
            if len(dims) == 1:
                return ap
            names = "abcd"[:len(dims)]
            spec = {names[i]: dims[i] for i in range(1, len(dims))}
            return ap.rearrange(f"p ({' '.join(names)}) -> p {' '.join(names)}", **spec)

        def barrier():
            now = Q.last() + Q.alldma()
            for e in Q.ENG:
                Q._waits(e, now)
            top[0] = 0

        def M(out, lhsT, rhs, start, stop, *w):
            return Q.op("tensor", lambda e: e.matmul(out, lhsT, rhs, start=start, stop=stop), *w)

        def TR(out, in_, *w):
            k = in_.shape[0]
            return Q.op("tensor", lambda e: e.transpose(out, in_, ident[0:k, 0:k]), *w)

        def act(out, in_, func, *w, bias=0.0, scale=1.0, accum=None):
            return Q.op("scalar", lambda e: e.activation(out, in_, func, bias=bias, scale=scale, accum_out=accum), *w)

        def tt(e, out, in0, in1, op, *w):
            return Q.op(e, lambda g: g.tensor_tensor(out, in0, in1, op), *w)

        def ts(e, out, in0, s1, s2, op0, op1, *w):
            if op1 is None:
                return Q.op(e, lambda g: g.tensor_scalar(out, in0, s1, None, op0), *w)
            return Q.op(e, lambda g: g.tensor_scalar(out, in0, s1, s2, op0, op1), *w)

        def stt(out, in0, s, in1, op0, op1, *w):
            return Q.op("vector", lambda g: g.scalar_tensor_tensor(out, in0, s, in1, op0, op1), *w)

        def red(out, in_, op, *w):
            return Q.op("vector", lambda g: g.tensor_reduce(out, in_, AX.X, op), *w)

        def rec(out, in_, *w):
            return Q.op("vector", lambda g: g.reciprocal(out, in_), *w)

        def cp(e, out, in_, *w):
            if e == "scalar":
                return act(out, in_, ACT.Copy, *w)
            return Q.op(e, lambda g: g.tensor_copy(out, in_), *w)

        def memset(e, out, v, *w):
            return Q.op(e, lambda g: g.memset(out, v), *w)

        def load(dst, name, *w, e="sync"):
            return Q.dma(e, "in_" + name, dst, a[name], *w)

        def bc(ap, shape):
            return ap.to_broadcast(shape)

        def rsqrt(y, v, tmp, *w):
            t = act(tmp, v, ACT.Sqrt, *w)
            t = rec(y, tmp, t)
            t = tt("vector", tmp, y, y, ALU.mult, t)
            t = tt("vector", tmp, tmp, v, ALU.mult, t)
            t = ts("vector", tmp, tmp, -0.5, 1.5, ALU.mult, ALU.add, t)
            return tt("vector", y, y, tmp, ALU.mult, t)

        def stats(src, n, eps, mv, st, y, v, tmp, *w):
            for i in range(n):
                t = Q.op("vector", lambda g, i=i: g.bn_stats(st[:, i, :], src[:, i, :]), *w)
                t = Q.op("vector", lambda g, i=i: g.bn_aggr(mv[:, i, :], st[:, i, :]), t)
            t = ts("vector", v, mv[:, 0:n, 1], eps, None, ALU.add, None, t)
            return rsqrt(y, v, tmp, t)

        t_id = load(ident[:, :], "ident")
        t_on = memset("vector", ones[:, :], 1.0)
        t_z = [memset("vector", PS[:, k, :], 0.0) for k in range(8)]
        t_x = Q.dma("scalar", "x", X[:, :, :], a["x"])

        def norm_top(*w):
            o = top[0]
            st, mv = take(NT, 6), take(NT, 2)
            y, v, tmp = take(NT), take(NT), take(NT)
            R = Ring([PS[:, k, :] for k in range(8)], [*w])
            t = stats(X, NT, 1e-5, mv, st, y, v, tmp, *w)
            tn = []
            for i in range(NT):
                e = "vector" if i % 2 else "gpsimd"
                tn.append(Q.op(e, lambda g, i=i: g.tensor_scalar(XN[:, i, :], X[:, i, :], mv[:, i, 0:1], y[:, i:i + 1],
                                                                 ALU.subtract, ALU.mult), t, *w))
            done = []
            for k in range(NT // 4):
                r, ps, free = R.take()
                for j in range(4):
                    t = TR(ps[:, j * 128:j * 128 + 128], XN[:, 4 * k + j, :], tn[4 * k + j], free, t_id)
                t = cp("scalar", XT[:, k * 512:k * 512 + 512], ps, t)
                R.done(r, t)
                done.append(t)
            return tn + done
        ptb = take(5, 4, 512)
        wqk = take(3, 512)
        wks = ptb[:, 0, 0:3, :]
        wv, wo, sw = take(128), take(128), take(128)
        relT = take(64)
        rowb = take(3 * 512 + 256, rows=1)
        colb = take(12)
        oh = take(258, rows=64)
        lnsc, lnb = take(128), take(128)
        tric, trid = take(128), take(128)
        t_w = [load(wqk, "wqk", e="scalar"), load(wks, "wks", e="scalar"), load(wv, "l0_wv"), load(wo, "l0_wo"), load(sw, "l0_sw"), load(relT, "relT"),
               load(rowb, "l0_rows"), load(colb, "l0_cols"), load(oh, "oh"), load(lnsc, "l0_lnsc"),
               load(lnb, "l0_lnb"), load(tric, "tric"), load(trid, "trid")]
        t_sw = act(sw, sw, ACT.Sign, t_w)
        posk = ptb[0:64, 1, 0:3, :]
        PGC, PGD = take(4, 128), take(4, 128)
        BIAS = take(3, 4)
        QP, KL, KU = take(4, 512), take(4, 512), take(4, 512)
        VA = [take(4, 16, 9) for _ in range(2)]
        PTB = Ring([ptb[:, k, :, :] for k in range(5)])
        GC = [take(4, 128) for _ in range(3)]
        GD = [take(4, 128) for _ in range(3)]
        CB = [take(4, PITCH) for _ in range(3)]
        DB = [take(4, PITCH) for _ in range(3)]
        PB = Ring([take(512) for _ in range(4)])
        TMP = take(4, 128)
        OS, CTT = take(512), take(512)
        CT = take(4, 4, 4, 8)
        RD = take(4, 4)
        MX, NBI = take(8, 2), take(8, 2)
        T1 = take(4, 128)
        lst, lmv, ly, lv, ltmp = take(4, 6), take(4, 2), take(4), take(4), take(4)
        save = top[0]

        zt = memset("vector", QP.rearrange("p a b -> p (a b)"), 0.0)
        t_scr = [Q.dma("sync", f"z{k}", scr[k, :].rearrange("(p n) -> p n", p=128),
                       QP.rearrange("p a b -> p (a b)")[:, 0:SLOT // 128], zt) for k in range(2 * SLOTS)]
        t_cb = [memset("gpsimd", CB[k], 0.0) for k in range(3)] + [memset("gpsimd", DB[k], 0.0) for k in range(3)]
        t_va = [memset("gpsimd", VA[k], 1.0) for k in range(2)]
        t_n = norm_top(t_x, t_z)
        top[0] = save
        RS = Ring([PS[:, 0:2, :], PS[:, 2:4, :]], t_n)
        R = Ring([PS[:, k, :] for k in (4, 5, 6)], t_n)
        OB = PS[:, 7, :]

        tp = []
        for k in range(3):
            r, ps, free = R.take()
            M(ps[0:64, :], relT, wks[:, k, :], True, False, free, t_w)
            t = M(ps[0:64, :], ones[0:1, 0:64], rowb[0:1, 512 * k:512 * k + 512], False, True, t_on)
            t = cp("scalar", posk[:, k, :], ps[0:64, :], t)
            R.done(r, t)
            tp.append(t)
        for k, dst in ((0, PGC), (1, PGD)):
            r, ps, free = R.take()
            for g in range(4):
                t = M(ps[:, g * 128:g * 128 + 128], posk[:, k, g * 128:g * 128 + 128], oh[:, 128 * k:128 * k + 128],
                      True, True, free, tp)
            t = cp("vector", dst.rearrange("p a b -> p (a b)"), ps, t)
            R.done(r, t)
            tp.append(t)
        r, ps, free = R.take()
        for g in range(4):
            gs = slice(g * 128, g * 128 + 128)
            M(ps[:, g:g + 1], posk[:, 1, gs], oh[:, 256:257], True, False, free, tp)
            M(ps[:, g:g + 1], posk[:, 2, gs], oh[:, 257:258], False, True)
            M(ps[:, 4 + g:5 + g], posk[:, 0, gs], oh[:, 256:257], True, True)
            t = M(ps[:, 8 + g:9 + g], posk[:, 0, gs], oh[:, 257:258], True, True)
        t = tt("vector", BIAS.rearrange("p a b -> p (a b)"), ps[:, 0:12], colb, ALU.add, t)
        R.done(r, t)
        t_pos = tp + [t]
        PTB.free = [t_pos for _ in range(5)]

        SC = float(1.0 / np.sqrt(np.float32(24.0)))
        st = {"slice": [t_scr] * 4, "opq": {}, "g": {}, "c": {}, "d": {}, "rd": {}, "s": {}, "pt": {}, "va": [[], []],
              "tv": {}, "cfree": [[], [], []], "dfree": [[], [], []], "gfree": [[], [], []], "ofree": [t_n], "ctfree": [],
              "mx": [[] for _ in range(8)], "cttfree": [], "t1free": [], "tmpfree": []}

        def proj(b, g):
            gs = slice(g * 128, g * 128 + 128)
            toks = []
            for k, (w, dst) in enumerate(((0, QP), (1, KL), (2, KU))):
                r, ps, free = R.take()
                t = M(ps, wqk[:, w, gs], XT[:, b * SEQ:b * SEQ + SEQ], True, True, free, t_w, t_n)
                if k % 2:
                    t = ts("vector", dst[:, g, :], ps, BIAS[:, k, g:g + 1], None, ALU.add, None, t, st["slice"][g], t_pos)
                else:
                    t = act(dst[:, g, :], ps, ACT.Identity, t, st["slice"][g], t_pos, bias=BIAS[:, k, g:g + 1])
                R.done(r, t)
                toks.append(t)
            st["opq"][b, g] = toks
            if g == 0:
                r, ps, free = R.take()
                for q in range(4):
                    o = ps[:, q * 128:q * 128 + 128]
                    M(o, XT[:, (b * 4 + q) * 128:(b * 4 + q) * 128 + 128], wv, True, False, free)
                    t = M(o, ones[0:1, 0:128], rowb[0:1, 1536:1664], False, True)
                t = cp("vector", VA[b % 2][:, :, :, 0:8], ps.rearrange("p (q h d) -> p q h d", q=4, h=16), t, t_va,
                       st["va"][b % 2])
                R.done(r, t)
                st["tv"][b] = t

        def emit_g(n):
            b, h = divmod(n, 16)
            g, hh = divmod(h, 4)
            if hh == 0:
                proj(b, g)
            k = n % 3
            rows = slice(32 * hh, 32 * hh + 32)
            toks = []
            for src, pg, dst, e in ((QP, PGC, GC[k], "scalar"), (KL, PGD, GD[k], "vector")):
                r, ps, free = R.take()
                for q in range(4):
                    t = M(ps[:, q * 128:q * 128 + 128], src[rows, g, q * 128:q * 128 + 128], pg[rows, g, :], True, True,
                          free, st["opq"][b, g])
                t = cp(e, dst.rearrange("p a b -> p (a b)"), ps, t, st["gfree"][k])
                R.done(r, t)
                toks.append(t)
            s = n % SLOTS
            wr = []
            for x, src in enumerate((GC[k], GD[k])):
                dst = bass.AP(scr.tensor, (x * SLOTS + s) * SLOT + 129, [[PITCH, 128], [128 * PITCH, 4], [1, 127]])
                wr.append(Q.dma("sync", f"w{x}{s}", dst, src[:, :, 1:128], toks[x], st["rd"].get(n - SLOTS, []), t_scr))
            st["g"][n] = (toks, wr)

        def emit_r(n):
            s, k = n % SLOTS, n % 3
            toks, wr = st["g"][n]
            reads, res = [], []
            for x, buf in enumerate((CB[k], DB[k])):
                fr = st["cfree"][k] if x == 0 else st["dfree"][k]
                base = (x * SLOTS + s) * SLOT + 128
                lo = bass.AP(scr.tensor, base, [[PITCH - 1, 64], [128 * PITCH, 4], [1, 192]])
                hi = bass.AP(scr.tensor, base + 64 * (PITCH - 1) + 64, [[PITCH - 1, 64], [128 * PITCH, 4], [1, 192]])
                r1 = Q.dma("sync", f"r{x}{k}l", buf[0:64, :, 0:192], lo, wr[x], fr, t_cb)
                r2 = Q.dma("sync", f"r{x}{k}h", buf[64:128, :, 64:256], hi, wr[x], fr, t_cb)
                reads.append((r1, r2))
            for x, (buf, tri, G) in enumerate(((CB[k], tric, GC[k]), (DB[k], trid, GD[k]))):
                t = tt("gpsimd", TMP, bc(tri.unsqueeze(1), [128, 4, 128]), bc(G[:, :, 0:1], [128, 4, 128]), ALU.mult,
                       toks[x], t_w, st["tmpfree"])
                t = tt("gpsimd", buf[:, :, 64:192], buf[:, :, 64:192], TMP, ALU.add, t, reads[x])
                st["tmpfree"] = [t]
                res.append((t,) + reads[x])
            st["gfree"][k] = [t] + wr
            st["rd"][n] = [r for p in reads for r in p]
            st["c"][n], st["d"][n] = res

        def emit_s(n, half):
            b, h = divmod(n, 16)
            g, hh = divmod(h, 4)
            k = n % 3
            rows = slice(32 * hh, 32 * hh + 32)
            r, S, free = RS.take()
            for t_ in range(2):
                ib = 2 * half + t_
                q = QP[rows, g, ib * 128:ib * 128 + 128]
                if ib:
                    M(S[:, t_, 0:128 * ib], q, KL[rows, g, 0:128 * ib], True, False, free)
                M(S[:, t_, 128 * ib:512], q, KU[rows, g, 128 * ib:512], ib == 0, False, free)
                if ib:
                    jb = ib - 1
                    M(S[0:64, t_, 128 * jb + 64:128 * jb + 128], DB[k][64:128, jb, 192:256], ident[64:128, 64:128],
                      False, False, st["d"][n])
                if ib < 3:
                    jb = ib + 1
                    M(S[64:128, t_, 128 * jb:128 * jb + 64], DB[k][0:64, jb, 0:64], ident[0:64, 0:64], False, False,
                      st["d"][n])
                tS = M(S[:, t_, 128 * ib:128 * ib + 128], DB[k][:, ib, 64:192], ident[:, :], False, True, st["d"][n])
                lo, hi = max(0, 128 * ib - 64), min(512, 128 * ib + 192)
                o = 64 - 128 * ib
                t = tt("vector", S[:, t_, lo:hi], S[:, t_, lo:hi], CB[k][:, ib, lo + o:hi + o], ALU.add, tS, st["c"][n])
            if half:
                st["cfree"][k], st["dfree"][k] = [t], [tS]
                if hh == 3:
                    st["slice"][g] = [tS]
            m = (2 * n + half) % 8
            t = red(MX[:, m, :], S, ALU.max, t, st["mx"][m])
            t = ts("vector", NBI[:, m, :], MX[:, m, :], -SC, None, ALU.mult, None, t)
            for t_ in range(2):
                kp, P, fp = PB.take()
                te = act(P, S[:, t_, :], ACT.Exp, t, fp, bias=NBI[:, m, t_:t_ + 1], scale=SC)
                st["s"][n, half, t_] = (te, kp, P)
            st["mx"][m] = [te]
            RS.done(r, te)

        def emit_pt(n, half):
            b, h = divmod(n, 16)
            g, hh = divmod(h, 4)
            if half == 0:
                st["ptk", n] = PTB.take()
                st["pte", n] = []
            kb, PT, fpt = st["ptk", n]
            for t_ in range(2):
                ib = 2 * half + t_
                te, kp, P = st["s"][n, half, t_]
                r, ps, free = R.take()
                for jb in range(4):
                    t = TR(ps[:, jb * 128:jb * 128 + 128], P[:, jb * 128:jb * 128 + 128], te, free)
                PB.done(kp, t)
                e = "scalar" if t_ == 0 else "vector"
                t = cp(e, PT[:, :, ib * 128:ib * 128 + 128], ps.rearrange("p (a b) -> p a b", a=4), t, fpt)
                R.done(r, t)
                st["pte", n].append(t)
            if half == 1 and hh == 3:
                emit_pv(b, g)

        def emit_pv(b, g):
            ns = [b * 16 + g * 4 + hh for hh in range(4)]
            for jb in range(4):
                for hh in range(4):
                    kb, PT, _ = st["ptk", ns[hh]]
                    t = M(OB[32 * hh:32 * hh + 9, :], VA[b % 2][:, jb, g * 4 + hh, :], PT[:, jb, :], jb == 0, jb == 3,
                          st["pte", ns[hh]], st["tv"][b], st["ofree"])
            for hh in range(4):
                PTB.done(st["ptk", ns[hh]][0], t)
            if g == 3:
                st["va"][b % 2] = [t]
            t = cp("scalar", OS, OB, t)
            st["ofree"] = [t]
            r, ps, free = R.take()
            for q in range(4):
                t2 = TR(ps[:, q * 128:q * 128 + 128], OS[:, q * 128:q * 128 + 128], t, free)
            st["ofree"].append(t2)
            v = ps.rearrange("p (q h r) -> p q h r", q=4, h=4)
            t = rec(RD, v[:, :, :, 8], t2)
            t = tt("vector", CT[:, :, g, :, :], v[:, :, :, 0:8], bc(RD.unsqueeze(3), [128, 4, 4, 8]), ALU.mult, t,
                   st["ctfree"])
            R.done(r, t)
            if g == 3:
                tail(b, t)

        def tail(b, tc):
            r, ps, free = R.take()
            for q in range(4):
                t = TR(ps[:, q * 128:q * 128 + 128], CT[:, q, :, :, :].rearrange("p g h d -> p (g h d)"), tc, free)
            st["ctfree"] = [t]
            t = cp("scalar", CTT, ps, t)
            R.done(r, t)
            r, ps, free = R.take()
            r2, ps2, free2 = R.take()
            for q in range(4):
                o = ps[:, q * 128:q * 128 + 128]
                M(o, CTT[:, q * 128:q * 128 + 128], wo, True, False, t, free)
                t1 = M(o, ones[0:1, 0:128], rowb[0:1, 1664:1792], False, True)
                i = b * 4 + q
                t2 = M(ps2[:, q * 128:q * 128 + 128], XT[:, i * 128:i * 128 + 128], sw, True, True, free2, t_sw)
            xs = slice(b * 4, b * 4 + 4)
            v4 = lambda p: p.rearrange("p (q c) -> p q c", q=4)
            t = tt("vector", T1, v4(ps), XN[:, xs, :], ALU.add, t1)
            R.done(r, t)
            tx = tt("vector", X[:, xs, :], v4(ps2), X[:, xs, :], ALU.add, t2)
            R.done(r2, tx)
            t = stats(T1, 4, 1e-7, lmv, lst, ly, lv, ltmp, t)
            for q in range(4):
                t3 = ts("vector", T1[:, q, :], T1[:, q, :], lmv[:, q, 0:1], ly[:, q:q + 1], ALU.subtract, ALU.mult, t)
            t = tt("vector", T1, T1, bc(lnsc.unsqueeze(1), [128, 4, 128]), ALU.mult, t3)
            t = tt("vector", T1, T1, bc(lnb.unsqueeze(1), [128, 4, 128]), ALU.add, t)
            tt("vector", X[:, xs, :], X[:, xs, :], T1, ALU.add, t, tx)

        NBH = NB * NH
        LG, LR = 3, 1
        for n in range(LG):
            emit_g(n)
        for n in range(LR):
            emit_r(n)
        for n in range(NBH):
            if n + LG < NBH:
                emit_g(n + LG)
            if n + LR < NBH:
                emit_r(n + LR)
            emit_s(n, 0)
            if n:
                emit_pt(n - 1, 1)
            emit_s(n, 1)
            emit_pt(n, 0)
        emit_pt(NBH - 1, 1)

        barrier()
        names = ["wz_f", "wh_f", "wz_b", "wh_b"]
        w1 = [take(128) for _ in names]
        c1 = take(4)
        wout, bout = take(2, 128), take(128, rows=1)
        router = take(8)
        trile, iota, rev = take(128), take(64), take(8)
        wi, wo2 = take(8, 512), take(8, 4, 128)
        t_w = [load(w1[k], names[k]) for k in range(4)] + [load(c1, "l1_cols"), load(wout, "l1_wout"), load(bout, "l1_bout"),
               load(router, "router"), load(trile, "trile"), load(iota, "iota"), load(rev, "rev")]
        t_wi, t_wo2 = load(wi, "wi", e="scalar"), load(wo2, "wo2", e="scalar")
        ones128 = take(128)
        t_o = memset("gpsimd", ones128, 1.0)
        c1x = take(4)
        t_c = None
        for k in range(4):
            t_c = ts("vector", c1x[:, k:k + 1], c1[:, k:k + 1], 1.0 if k % 2 else -1.0, 0.5 if k % 2 else 0.0, ALU.mult,
                     ALU.add, t_w)
        PRI, PROB = take(NT, 8), take(NT, 8)
        big = top[0]
        t_n = norm_top()
        top[0] = big
        R = Ring([PS[:, k, :] for k in range(8)], t_n)

        L, L2, E1, E2, W_ = (take(NT, 8) for _ in range(5))
        m8, s8 = take(NT), take(NT)
        full = [128, NT, 8]
        col = lambda v: bc(v.unsqueeze(2), full)
        r, ps, free = R.take()
        for i in range(NT):
            t = M(ps[:, i * 8:i * 8 + 8], XT[:, i * 128:i * 128 + 128], router, True, True, free, t_w)
        t = cp("vector", L.rearrange("p a b -> p (a b)"), ps[:, 0:256], t)
        R.done(r, t)
        tL = t
        t = red(m8, L, ALU.max, tL)
        t = tt("vector", PROB, L, col(m8), ALU.subtract, t)
        t = act(PROB, PROB, ACT.Exp, t)
        t = red(s8, PROB, ALU.add, t)
        t = rec(s8, s8, t)
        tP = tt("vector", PROB, PROB, col(s8), ALU.mult, t)
        revb = bc(rev.unsqueeze(1), full)

        def first_max(dst, src, t):
            t = red(m8, src, ALU.max, t)
            t = tt("vector", W_, src, col(m8), ALU.is_equal, t)
            t = tt("vector", W_, W_, revb, ALU.mult, t)
            t = red(m8, W_, ALU.max, t)
            return tt("vector", dst, W_, col(m8), ALU.is_equal, t)
        t1 = first_max(E1, L, tP)
        t = stt(L2, E1, -3.0e38, L, ALU.mult, ALU.add, t1)
        t2 = first_max(E2, L2, t)
        v1, v2 = (E.rearrange("p (b q) e -> p b q e", q=4) for E in (E1, E2))
        r, ps, free = R.take()
        for k, (E, v) in enumerate(((E1, v1), (E2, v2))):
            o = ps[:, 256 * k:256 * k + 256]
            ov = o.rearrange("p (b q e) -> p b q e", q=4, e=8)
            for q in range(4):
                prev = [(v, j) for j in range(q)] + ([(v1, j) for j in range(4)] if k else [])
                t = M(ov[:, :, q, :], trile, v[:, :, q, :], True, not prev, free, t1, t2, t_w)
                for x, (pv, j) in enumerate(prev):
                    t = M(ov[:, :, q, :], ones128, pv[:, :, j, :], False, x == len(prev) - 1, t_o)
        ps_v = ps.rearrange("p (k n e) -> p k n e", k=2, e=8)
        ta = tt("vector", E1, E1, ps_v[:, 0], ALU.mult, t)
        tb = tt("vector", E2, E2, ps_v[:, 1], ALU.mult, t)
        R.done(r, tb)
        t = tt("vector", PRI, E1, E2, ALU.max, ta, tb)
        tPRI = ts("vector", PRI, PRI, -1.0, None, ALU.add, None, t)

        top[0] = big
        A_ = Ring([take(512) for _ in range(3)], [tPRI])
        Z_ = Ring([take(512) for _ in range(3)], [tPRI])
        G_ = Ring([take(512) for _ in range(3)], [tPRI])
        H_ = Ring([take(512) for _ in range(4)], [tPRI])

        def scan_unit(b, d):
            toks = []
            for k in range(2):
                r, ps, free = R.take()
                t = M(ps, w1[2 * d + k], XT[:, b * SEQ:b * SEQ + SEQ], True, True, free, t_w)
                toks.append((r, ps, t))
            (r0, p0, tz), (r1, p1, th) = toks
            ka, A, fa = A_.take()
            kz, Z, fz = Z_.take()
            kg, G, fg = G_.take()
            kh, H, fh = H_.take()
            t_a = act(A, p0, ACT.Sigmoid, tz, fa, t_c, bias=c1x[:, 2 * d:2 * d + 1], scale=-1.0)
            t_z = act(Z, p0, ACT.Sigmoid, fz, bias=c1[:, 2 * d:2 * d + 1])
            R.done(r0, t_z)
            t_g = act(G, p1, ACT.Sigmoid, th, fg, bias=c1[:, 2 * d + 1:2 * d + 2])
            t = stt(G, p1, c1x[:, 2 * d + 1:2 * d + 2], G, ALU.add, ALU.max, t_g)
            R.done(r1, t)
            t = tt("gpsimd", G, G, Z, ALU.mult, t, t_z)
            Z_.done(kz, t)
            rv = slice(None, None, -1) if d else slice(None)
            t = Q.op("vector", lambda g: g.tensor_tensor_scan(H, A[:, rv], G[:, rv], 0.0, ALU.mult, ALU.add), t, t_a, fh)
            A_.done(ka, t)
            G_.done(kg, t)
            return kh, H, t

        def scan_out(b, hs):
            r, ps, free = R.take()
            for q in range(4):
                o = ps[:, q * 128:q * 128 + 128]
                sl = slice(q * 128, q * 128 + 128)
                M(o, hs[0][1][:, sl], wout[:, 0, :], True, False, hs[0][2], free)
                M(o, hs[1][1][:, sl], wout[:, 1, :], False, False, hs[1][2])
                t = M(o, ones[0:1, 0:128], bout, False, True)
            for kh, _, _ in hs:
                H_.done(kh, t)
            xs = slice(b * 4, b * 4 + 4)
            t = tt("vector", X[:, xs, :], X[:, xs, :], ps.rearrange("p (q c) -> p q c", q=4), ALU.add, t)
            R.done(r, t)
            return t
        hs = None
        tX = []
        for b in range(NB):
            cur = [scan_unit(b, d) for d in range(2)]
            if b:
                tX.append(scan_out(b - 1, hs))
            hs = cur
        tX.append(scan_out(NB - 1, hs))

        for e in ("vector", "gpsimd", "scalar"):
            Q._waits(e, Q.last())
        top[0] = big
        XIN = take(8, 8, 64)
        EO = take(4, 8, 128)
        HT = Ring([take(4, 512) for _ in range(2)])
        DD = Ring([take(8, 64) for _ in range(5)])
        iob = bc(iota.unsqueeze(1), [128, 8, 64])
        t_in = []
        for g in range(8):
            r, ps, free = R.take()
            for q in range(4):
                i = g * 4 + q
                kd, D, fd = DD.take()
                t = tt("vector", D, iob, bc(PRI[:, i, :].unsqueeze(2), [128, 8, 64]), ALU.is_equal, fd)
                t = M(ps, XN[:, i, :], D.rearrange("p a b -> p (a b)"), q == 0, q == 3, t, free)
                DD.done(kd, t)
            t = cp("scalar", XIN[:, :, g, :], ps.rearrange("p (e c) -> p e c", e=8), t)
            R.done(r, t)
            t_in.append(t)
        t_eo = []
        R1 = Ring([PS[:, k, :] for k in range(4)], Q.last())
        R2 = Ring([PS[:, 4:6, :], PS[:, 6:8, :]], Q.last())

        def down(e, kh, H, toks):
            r, ps, free = R2.take()
            rows = slice(64 * (e % 2), 64 * (e % 2) + 64)
            pv = ps.rearrange("p k (g c) -> p (k g) c", c=128)
            for g in range(8):
                for f in range(4):
                    t = M(pv[rows, g, :], H[:, f, g * 64:g * 64 + 64], wo2[:, e, f, :], f == 0, f == 3, toks, free, t_wo2)
            HT.done(kh, t)
            t = cp("vector", EO[rows, e // 2, :, :], pv[rows, :, :], t)
            R2.done(r, t)
            t_eo.append(t)
        prev = None
        for e in range(8):
            kh, H, fh = HT.take()
            toks = []
            for f in range(4):
                r, ps, free = R1.take()
                t = M(ps, wi[:, e, f * 128:f * 128 + 128], XIN[:, e, :, :].rearrange("p g c -> p (g c)"), True, True,
                      t_in, free, t_wi)
                t = act(H[:, f, :], ps, ACT.Gelu_apprx_tanh, t, fh)
                R1.done(r, t)
                toks.append(t)
            if prev:
                down(*prev)
            prev = (e, kh, H, toks)
        down(*prev)
        R = Ring([PS[:, k, :] for k in range(8)], Q.last())
        CTB = Ring([take(4, 128) for _ in range(2)])

        def comb_a(i):
            kd, D, fd = DD.take()
            for e in range(8):
                t = ts("vector", D[:, e, :], iota, PRI[:, i, e:e + 1], PROB[:, i, e:e + 1], ALU.is_equal, ALU.mult, fd)
            r, ps, free = R.take()
            Df = D.rearrange("p a b -> p (a b)")
            for c in range(4):
                t2 = TR(ps[:, c * 128:c * 128 + 128], Df[:, c * 128:c * 128 + 128], t, free)
            DD.done(kd, t2)
            kc, CB_, fc = CTB.take()
            t = cp("scalar", CB_, ps.rearrange("p (a b) -> p a b", a=4), t2, fc)
            R.done(r, t)
            return i, kc, CB_, t

        def comb_b(i, kc, CB_, t):
            r, ps, free = R.take()
            for c in range(4):
                t = M(ps[:, 0:128], CB_[:, c, :], EO[:, c, i // 4, :], c == 0, c == 3, t, t_eo, free)
            CTB.done(kc, t)
            t = tt("vector", X[:, i, :], X[:, i, :], ps[:, 0:128], ALU.add, t)
            R.done(r, t)
        prev = None
        for i in range(NT):
            cur = comb_a(i)
            if prev:
                comb_b(*prev)
            prev = cur
        comb_b(*prev)

        barrier()
        ctxT, wk_, wv_ = take(512, rows=96), take(1024, rows=96), take(1024, rows=96)
        wqT, wout2 = take(8, 128), take(8, 128)
        bout2 = take(128, rows=1)
        w3, mu, mu1 = take(3, 128), take(2), take(2)
        t_w = [load(ctxT, "ctxT"), load(wk_, "l2_wk"), load(wv_, "l2_wv", e="scalar"), load(wqT, "l2_wqT"),
               load(wout2, "l2_wout", e="scalar"), load(bout2, "l2_bout"), load(w3, "l2_w"), load(mu, "l2_mu")]
        MH, VW = take(8, 512), take(8, 4, 128)
        XR, XK = take(NB, SEQ), take(NB, SEQ)
        KA = Ring([take(512) for _ in range(2)])
        RG = Ring([take(512) for _ in range(2)])
        SVK = Ring([take(512) for _ in range(2)])
        BO = take(128)
        base = top[0]
        R = Ring([PS[:, k, :] for k in range(4)])
        t_v = []
        for h in range(8):
            hs_ = slice(h * 128, h * 128 + 128)
            for w, kind in ((wk_, 0), (wv_, 1)):
                r, ps, free = R.take()
                t = M(ps, w[:, hs_], ctxT, True, True, free, t_w)
                k, S_, fs = SVK.take()
                t = cp("scalar" if kind else "vector", S_, ps, t, fs)
                R.done(r, t)
                r, ps, free = R.take()
                if kind == 0:
                    t = M(ps, wqT[:, h, :], S_, True, True, t, free)
                    SVK.done(k, t)
                    t = cp("scalar", MH[:, h, :], ps, t)
                else:
                    for j in range(4):
                        t = M(ps[:, j * 128:j * 128 + 128], S_[:, j * 128:j * 128 + 128], wout2[:, h, :], True, True, t, free)
                    SVK.done(k, t)
                    t = cp("vector", VW[:, h, :, :], ps.rearrange("p (j c) -> p j c", j=4), t)
                R.done(r, t)
                t_v.append(t)
        r, ps, free = R.take()
        t = M(ps[:, 0:128], ones[0:1, 0:128], bout2, True, True, free, t_w)
        t_bo = cp("scalar", BO, ps[:, 0:128], t)
        R.done(r, t_bo)
        Q._waits("tensor", Q.last())
        Q._waits("scalar", Q.last())
        t_n = norm_top(Q.last())
        top[0] = base
        R = Ring([PS[:, k, :] for k in range(8)], t_n)
        t_mu = ts("vector", mu1, mu, -1.0, 1.0, ALU.mult, ALU.add, t_w)
        XTb = XT[:, :].rearrange("p (b t) -> p b t", b=NB)
        t_x = tt("gpsimd", X[:, :, :], X[:, :, :], bc(BO.unsqueeze(1), [128, NT, 128]), ALU.add, t_bo, t_n)
        t_f = []
        for b in range(NB):
            toks = []
            for k, dst in enumerate((XR, XK)):
                t0 = memset("gpsimd", dst[:, b, 0:1], 0.0)
                t = act(dst[:, b, 1:], XTb[:, b, 0:SEQ - 1], ACT.Copy, t_n, t_mu, scale=mu1[:, k:k + 1])
                toks.append(stt(dst[:, b, :], XTb[:, b, :], mu[:, k:k + 1], dst[:, b, :], ALU.mult, ALU.add, t, t0))
            r, ps, free = R.take()
            t = M(ps, w3[:, 1, :], XK[:, b, :], True, True, toks[1], free)
            k, K_, fk = KA.take()
            t = act(K_, ps, ACT.Relu, t, fk)
            R.done(r, t)
            t = act(K_, K_, ACT.Square, t)
            r, ps, free = R.take()
            r2, ps2, free2 = R.take()
            for q in range(4):
                sl = slice(q * 128, q * 128 + 128)
                tr = M(ps[:, sl], XR[:, b, sl], w3[:, 0, :], True, True, toks[0], free)
            for q in range(4):
                sl = slice(q * 128, q * 128 + 128)
                tv = M(ps2[:, sl], K_[:, sl], w3[:, 2, :], True, True, t, free2)
            KA.done(k, tv)
            k, G, fg = RG.take()
            t = act(G, ps, ACT.Sigmoid, tr, fg)
            R.done(r, t)
            t = tt("vector", G, G, ps2, ALU.mult, t, tv)
            R.done(r2, t)
            xs = slice(b * 4, b * 4 + 4)
            t = tt("gpsimd", X[:, xs, :], X[:, xs, :], G.rearrange("p (q c) -> p q c", q=4), ALU.add, t, t_x)
            RG.done(k, t)
            t_f.append(t)
        for e in ("vector", "scalar", "gpsimd"):
            Q._waits(e, Q.last())
        top[0] = base
        now = Q.last()
        RS = Ring([PS[:, 0:2, :], PS[:, 2:4, :]], now)
        R = Ring([PS[:, 4, :], PS[:, 5, :]], now)
        RO = Ring([PS[:, 6, :], PS[:, 7, :]], now)
        PB = Ring([take(512) for _ in range(6)])
        PT = Ring([take(512) for _ in range(4)])
        MXR = Ring([take(2) for _ in range(4)])
        NBR = Ring([take(2) for _ in range(4)])
        DNR = Ring([take(8) for _ in range(3)])
        C = 1.5 * 128 ** -0.5
        pend = {}

        def att_s(i, p):
            r, S, free = RS.take()
            for x in range(2):
                t = M(S[:, x, :], XT[:, i * 128:i * 128 + 128], MH[:, 2 * p + x, :], True, True, free, t_v)
            km, MX_, fm = MXR.take()
            kn, NB_, fn = NBR.take()
            t = red(MX_, S, ALU.max, t, fm)
            t = ts("vector", NB_, MX_, -C, None, ALU.mult, None, t, fn)
            MXR.done(km, t)
            if p == 0:
                pend["d", i] = DNR.take()
            kd, DN, fd = pend["d", i]
            es = []
            for x in range(2):
                kp, P, fp = PB.take()
                te = act(P, S[:, x, :], ACT.Exp, t, fp, fd, bias=NB_[:, x:x + 1], scale=C,
                         accum=DN[:, 2 * p + x:2 * p + x + 1])
                es.append((te, kp, P))
            NBR.done(kn, te)
            RS.done(r, te)
            pend[i, p] = es

        def att_t(i, p):
            res = []
            for x, (te, kp, P) in enumerate(pend[i, p]):
                r, ps, free = R.take()
                for j in range(4):
                    t = TR(ps[:, j * 128:j * 128 + 128], P[:, j * 128:j * 128 + 128], te, free)
                PB.done(kp, t)
                kt, T_, ft = PT.take()
                t = cp("vector" if x else "scalar", T_, ps, t, ft)
                R.done(r, t)
                res.append((kt, T_, t))
            pend["t", i, p] = res

        def att_v(i, p):
            if p % 2 == 0:
                pend["o", i, p // 2] = RO.take()
            ro, O, fo = pend["o", i, p // 2]
            for x, (kt, T_, t) in enumerate(pend["t", i, p]):
                h = 2 * p + x
                for j in range(4):
                    tv = M(O[:, (h % 4) * 128:(h % 4) * 128 + 128], T_[:, j * 128:j * 128 + 128], VW[:, h, j, :], j == 0,
                           j == 3, t, fo)
                PT.done(kt, tv)
            if p % 2:
                kd, DN, _ = pend["d", i]
                half = slice(2 * p - 2, 2 * p + 2)
                t = rec(DN[:, half], DN[:, half], tv)
                for h in range(2 * p - 2, 2 * p + 2):
                    t = stt(X[:, i, :], O[:, (h % 4) * 128:(h % 4) * 128 + 128], DN[:, h:h + 1], X[:, i, :], ALU.mult,
                            ALU.add, t)
                RO.done(ro, t)
                if p == 3:
                    DNR.done(kd, t)
        seq = [(i, p) for i in range(NT) for p in range(4)]
        for n in range(len(seq) + 2):
            if n < len(seq):
                att_s(*seq[n])
            if 1 <= n < len(seq) + 1:
                att_t(*seq[n - 1])
            if n >= 2:
                att_v(*seq[n - 2])

        barrier()
        wqkv, rows3, cols3 = take(384), take(384, rows=1), take(3)
        gb, ab, pw, bdm = take(2, 256), take(128), take(2, 128), take(128)
        ng, nb_, sg, sbb, scl = take(128), take(128), take(128), take(128), take(1)
        fb, bd = take(16, 2, 2), take(2048, rows=1)
        SE = take(8, 128)
        t_w = [load(wqkv, "l3_qkv"), load(rows3, "l3_rows"), load(cols3, "l3_cols"), load(gb, "l3_gb", e="scalar"),
               load(ab, "l3_ab"), load(pw, "l3_p"), load(bdm, "bdmask", e="scalar"), load(ng, "l3_ng"), load(nb_, "l3_nb"),
               load(sg, "l3_sg"), load(sbb, "l3_sb"), load(scl, "l3_scale"), load(fb, "l3_fb", e="scalar"),
               load(bd, "l3_bd"), load(SE, "slots", e="scalar")]
        SET = take(1024)
        SLT = take(16, NB, 64)
        base = top[0]
        t_n = norm_top()
        top[0] = base
        R = Ring([PS[:, k, :] for k in range(8)], t_n)
        QT = Ring([take(512) for _ in range(2)])
        KV = Ring([take(4, 256) for _ in range(2)])
        SQ = Ring([take(4, 256) for _ in range(2)])
        S1, V1, T2, Y1 = (Ring([take(128) for _ in range(2)]) for _ in range(4))
        KVM = Ring([take(128) for _ in range(2)])
        AT = Ring([take(512) for _ in range(2)])
        HB = Ring([take(512) for _ in range(2)])
        t_tc = ts("vector", cols3[:, 2:3], cols3[:, 2:3], 1.0 / 512, None, ALU.mult, None, t_w)

        def heads_ln(b):
            rq, pq, fq = R.take()
            t = M(pq, wqkv[:, 0:128], XT[:, b * SEQ:b * SEQ + SEQ], True, True, fq, t_w)
            kq, QT_, f = QT.take()
            tq = act(QT_, pq, ACT.Identity, t, f, bias=cols3[:, 0:1])
            R.done(rq, tq)
            kk, KV_, f = KV.take()
            for x in range(2):
                r, ps, free = R.take()
                for y in range(2):
                    q = 2 * x + y
                    o = ps[:, y * 256:y * 256 + 256]
                    i = b * 4 + q
                    M(o, XT[:, i * 128:i * 128 + 128], wqkv[:, 128:384], True, False, free)
                    t = M(o, ones[0:1, 0:128], rows3[0:1, 0:256], False, True)
                t = cp("scalar", KV_[:, 2 * x:2 * x + 2, :], ps.rearrange("p (y c) -> p y c", y=2), t, f)
                R.done(r, t)
            v = KV_.rearrange("p q (h d) -> p (q h) d", d=8)
            ks, SQ_, fs = SQ.take()
            sv = SQ_.rearrange("p q (h d) -> p (q h) d", d=8)
            k1, s1, f1 = S1.take()
            k2, v1, f2 = V1.take()
            k3, tm, f3 = T2.take()
            k4, y1, f4 = Y1.take()
            wide = lambda z: bc(z.unsqueeze(2), [128, 128, 8])
            t = red(s1, v, ALU.add, t, f1)
            t = ts("vector", s1, s1, 0.125, None, ALU.mult, None, t)
            t = tt("gpsimd", v, v, wide(s1), ALU.subtract, t)
            S1.done(k1, t)
            tc_ = t
            t = act(SQ_, KV_, ACT.Square, t, fs)
            t = red(v1, sv, ALU.add, t, f2)
            SQ.done(ks, t)
            t = ts("vector", v1, v1, 0.125, 1e-5, ALU.mult, ALU.add, t)
            t = rsqrt(y1, v1, tm, t, f3, f4)
            V1.done(k2, t)
            T2.done(k3, t)
            t = tt("vector", v, v, wide(y1), ALU.mult, t, tc_)
            Y1.done(k4, t)
            t = tt("gpsimd", KV_, KV_, bc(gb[:, 0, :].unsqueeze(1), [128, 4, 256]), ALU.mult, t, t_w)
            t = tt("gpsimd", KV_, KV_, bc(gb[:, 1, :].unsqueeze(1), [128, 4, 256]), ALU.add, t)
            return b, kq, QT_, tq, kk, KV_, t

        def linear(b, kq, QT_, tq, kk, KV_, tkv):
            r, ps, free = R.take()
            for q in range(4):
                t = M(ps[:, 0:128], KV_[:, q, 0:128], KV_[:, q, 128:256], q == 0, q == 3, tkv, free)
            KV.done(kk, t)
            km, KM, f = KVM.take()
            t = stt(KM, ps[:, 0:128], cols3[:, 2:3], bdm, ALU.mult, ALU.mult, t, t_tc, f)
            R.done(r, t)
            t = tt("vector", KM, KM, ab, ALU.add, t)
            r, ps, free = R.take()
            t = M(ps, KM, QT_, True, True, t, tq, free)
            KVM.done(km, t)
            QT.done(kq, t)
            ka, A, f = AT.take()
            t = tt("vector", A, ps, XT[:, b * SEQ:b * SEQ + SEQ], ALU.add, t, f)
            R.done(r, t)
            r, ps, free = R.take()
            t = M(ps, pw[:, 0, :], A, True, True, t, free)
            AT.done(ka, t)
            kh, H, f = HB.take()
            t = act(H, ps, ACT.Gelu, t, f, bias=cols3[:, 1:2])
            R.done(r, t)
            r, ps, free = R.take()
            for q in range(4):
                o = ps[:, q * 128:q * 128 + 128]
                M(o, H[:, q * 128:q * 128 + 128], pw[:, 1, :], True, False, t, free)
                t2 = M(o, ones[0:1, 0:128], rows3[0:1, 256:384], False, True)
            HB.done(kh, t2)
            xs = slice(b * 4, b * 4 + 4)
            t = tt("vector", X[:, xs, :], X[:, xs, :], ps.rearrange("p (q c) -> p q c", q=4), ALU.add, t2)
            R.done(r, t)
            return tt("gpsimd", X[:, xs, :], X[:, xs, :], XN[:, xs, :], ALU.add, t)
        prev = None
        for b in range(NB):
            cur = heads_ln(b)
            if prev:
                linear(*prev)
            prev = cur
        linear(*prev)

        for e in ("vector", "scalar", "gpsimd", "tensor"):
            Q._waits(e, Q.last())
        top[0] = base
        st3, mv3 = take(NT, 6), take(NT, 2)
        y3, v3, tm3 = take(NT), take(NT), take(NT)
        R = Ring([PS[:, k, :] for k in range(8)], Q.last())

        def norm_affine(src, n, g_, b_, dstT, extra):
            t = stats(src, n, 1e-5, mv3, st3, y3[:, 0:n], v3[:, 0:n], tm3[:, 0:n], Q.last())
            for i in range(n):
                tl = ts("vector", src[:, i, :], src[:, i, :], mv3[:, i, 0:1], y3[:, i:i + 1], ALU.subtract, ALU.mult, t)
            t = tt("gpsimd", src, src, bc(g_.unsqueeze(1), [128, n, 128]), ALU.mult, tl, t_w)
            t = tt("gpsimd", src, src, bc(b_.unsqueeze(1), [128, n, 128]), ALU.add, t)
            if extra is not None:
                t = ts("vector", src, src, extra, None, ALU.mult, None, t)
            res = []
            for k in range(n // 4):
                r, ps, free = R.take()
                for j in range(4):
                    tr = TR(ps[:, j * 128:j * 128 + 128], src[:, 4 * k + j, :], t, free)
                tr = cp("scalar", dstT[:, k * 512:k * 512 + 512], ps, tr)
                R.done(r, tr)
                res.append(tr)
            return res + [t]
        t_se = norm_affine(SE, 8, sg, sbb, SET, scl)
        t_x2 = norm_affine(XN[:, :, :], NT, ng, nb_, XT, None)
        top[0] = base
        for e in ("vector", "scalar", "gpsimd"):
            Q._waits(e, Q.last())
        now = Q.last()
        RS = Ring([PS[:, 0:2, :], PS[:, 2:4, :]], now)
        R = Ring([PS[:, 4, :], PS[:, 5, :]], now)
        RO = Ring([PS[:, 6, :], PS[:, 7, :]], now)
        PB = Ring([take(512) for _ in range(6)])
        PT = Ring([take(512) for _ in range(6)])
        MXR = Ring([take(2) for _ in range(4)])
        DNR = Ring([take(2) for _ in range(6)])
        SLK = Ring([take(2, 128) for _ in range(2)])
        pend = {}

        def pair_s(key, lhs, rhs, joint):
            r, S, free = RS.take()
            for x in range(2):
                t = M(S[:, x, :], lhs[x], rhs[x], True, True, free)
            km, MX_, fm = MXR.take()
            if joint:
                t = red(MX_[:, 0:1], S.rearrange("p a b -> p (a b)"), ALU.max, t, fm)
                t = ts("vector", MX_[:, 1:2], MX_[:, 0:1], -1.0, None, ALU.mult, None, t)
                nb2 = [MX_[:, 1:2], MX_[:, 1:2]]
            else:
                t = red(MX_, S, ALU.max, t, fm)
                t = ts("vector", MX_, MX_, -1.0, None, ALU.mult, None, t)
                nb2 = [MX_[:, 0:1], MX_[:, 1:2]]
            kd, DN, fd = DNR.take()
            es = []
            for x in range(2):
                kp, P, fp = PB.take()
                te = act(P, S[:, x, :], ACT.Exp, t, fp, fd, bias=nb2[x], accum=DN[:, x:x + 1])
                es.append((te, kp, P))
            MXR.done(km, te)
            RS.done(r, te)
            pend["e", key] = es, kd, DN

        def pair_t(key):
            es, kd, DN = pend["e", key]
            res = []
            for x, (te, kp, P) in enumerate(es):
                r, ps, free = R.take()
                for j in range(4):
                    t = TR(ps[:, j * 128:j * 128 + 128], P[:, j * 128:j * 128 + 128], te, free)
                PB.done(kp, t)
                kt, T_, ft = PT.take()
                t = cp("vector" if x else "scalar", T_, ps, t, ft)
                R.done(r, t)
                res.append((kt, T_, t))
            pend["t", key] = res

        def slot_v(key):
            b, p = key
            _, kd, DN = pend["e", key]
            ro, O, fo = RO.take()
            for x, (kt, T_, t) in enumerate(pend["t", key]):
                for j in range(4):
                    tv = M(O[:, x * 128:x * 128 + 128], T_[:, j * 128:j * 128 + 128], XN[:, b * 4 + j, :], j == 0, j == 3,
                           t, fo)
                PT.done(kt, tv)
            t = rec(DN, DN, tv)
            ks, S_, fs = SLK.take()
            t = tt("vector", S_, O[:, 0:256].rearrange("p (x c) -> p x c", x=2), bc(DN.unsqueeze(2), [128, 2, 128]),
                   ALU.mult, t, fs)
            DNR.done(kd, t)
            for x in range(2):
                tr = TR(O[:, 256 + x * 128:384 + x * 128], S_[:, x, :], t)
            SLK.done(ks, tr)
            t = cp("scalar", SLT[:, 4 * p:4 * p + 4, b, :], O[:, 256:512].rearrange("p (e s) -> p e s", e=4), tr)
            RO.done(ro, t)
            return t
        seq = [(b, p) for b in range(NB) for p in range(4)]
        for n in range(len(seq) + 2):
            if n < len(seq):
                b, p = seq[n]
                xb = XT[:, b * SEQ:b * SEQ + SEQ]
                pair_s((b, p), [SET[:, (2 * p + x) * 128:(2 * p + x) * 128 + 128] for x in range(2)], [xb, xb], False)
            if 1 <= n < len(seq) + 1:
                pair_t(seq[n - 1])
            if n >= 2:
                t_sl = slot_v(seq[n - 2])

        for e in ("vector", "scalar", "gpsimd", "tensor"):
            Q._waits(e, Q.last())
        top[0] = base
        EO = take(8, NB, 128)
        WG = Ring([take(2, 256) for _ in range(3)])
        WD = Ring([take(2, 128) for _ in range(3)])
        GB = Ring([take(2, 512) for _ in range(2)])
        now = Q.last()
        R1 = Ring([PS[:, k, :] for k in range(4)], now)
        R2 = Ring([PS[:, 4:6, :], PS[:, 6:8, :]], now)

        def up(e):
            kw, W, fw = WG.take()
            kd, D, fd = WD.take()
            tw = Q.dma("sync", f"wg{kw}", W, a["wgu"][:, e, :, :], fw, now)
            td = Q.dma("sync", f"wd{kd}", D, a["wd"][:, e, :, :], fd, now)
            kg, G, fg = GB.take()
            toks = []
            rhs = SLT[:, e, :, :].rearrange("p b s -> p (b s)")
            for f in range(2):
                r, ps, free = R1.take()
                t = M(ps, W[:, 0, f * 128:f * 128 + 128], rhs, True, True, tw, free)
                r2, ps2, free2 = R1.take()
                t2 = M(ps2, W[:, 1, f * 128:f * 128 + 128], rhs, True, True, free2)
                t = act(G[:, f, :], ps, ACT.Gelu, t, fg, bias=fb[:, e, 0, f:f + 1])
                R1.done(r, t)
                t = stt(G[:, f, :], ps2, fb[:, e, 1, f:f + 1], G[:, f, :], ALU.add, ALU.mult, t, t2)
                R1.done(r2, t)
                toks.append(t)
            WG.done(kw, t2)
            return e, kd, D, td, kg, G, toks

        def dn(e, kd, D, td, kg, G, toks):
            r, ps, free = R2.take()
            rows = slice(64 * (e % 2), 64 * (e % 2) + 64)
            pv = ps.rearrange("p k (g c) -> p (k g) c", c=128)
            for g in range(8):
                for f in range(2):
                    M(pv[rows, g, :], G[:, f, g * 64:g * 64 + 64], D[:, f, :], f == 0, False, toks, td, free)
                t = M(pv[rows, g, :], ones[0:1, 0:64], bd[0:1, e * 128:e * 128 + 128], False, True)
            WD.done(kd, t)
            GB.done(kg, t)
            t = cp("vector" if e % 2 else "scalar", EO[rows, e // 2, :, :], pv[rows, :, :], t)
            R2.done(r, t)
            return t
        prev = None
        t_eo = []
        for e in range(16):
            cur = up(e)
            if prev:
                t_eo.append(dn(*prev))
            prev = cur
        t_eo.append(dn(*prev))

        for e in ("vector", "scalar", "gpsimd", "tensor"):
            Q._waits(e, Q.last())
        now = Q.last()
        RS = Ring([PS[:, 0:2, :], PS[:, 2:4, :]], now)
        R = Ring([PS[:, 4, :], PS[:, 5, :]], now)
        RO = Ring([PS[:, 6, :], PS[:, 7, :]], now)
        PB = Ring([take(512) for _ in range(6)])
        PT = Ring([take(512) for _ in range(6)])
        MXR = Ring([take(2) for _ in range(4)])
        DNR = Ring([take(2) for _ in range(6)])
        pend.clear()

        def comb_v(i):
            _, kd, DN = pend["e", i]
            ro, O, fo = RO.take()
            for x, (kt, T_, t) in enumerate(pend["t", i]):
                for j in range(4):
                    tv = M(O[:, 0:128], T_[:, j * 128:j * 128 + 128], EO[:, 4 * x + j, i // 4, :], x + j == 0,
                           x + j == 4, t, fo)
                PT.done(kt, tv)
            t = tt("vector", DN[:, 0:1], DN[:, 0:1], DN[:, 1:2], ALU.add, tv)
            t = rec(DN[:, 0:1], DN[:, 0:1], t)
            t = stt(X[:, i, :], O[:, 0:128], DN[:, 0:1], X[:, i, :], ALU.mult, ALU.add, t)
            DNR.done(kd, t)
            RO.done(ro, t)
        for n in range(NT + 2):
            if n < NT:
                xt = XT[:, n * 128:n * 128 + 128]
                pair_s(n, [xt, xt], [SET[:, 0:512], SET[:, 512:1024]], True)
            if 1 <= n < NT + 1:
                pair_t(n - 1)
            if n >= 2:
                comb_v(n - 2)

        Q.dma("sync", "out", out, X[:, :, :], Q.last())
        Q._waits("sync", Q.alldma())
        block = ctx.enter_context(nc.Block())
        Q.emit(block)


def layout(inp):
    f = {k: np.asarray(v) for k, v in inp.items()}
    d = constants()

    def heads(w, *at):
        w = w.reshape(w.shape[0], 16, 8)
        o = np.zeros((w.shape[0], 16, 32), w.dtype)
        for x in at:
            o[:, :, x:x + 8] = w
        return o.reshape(w.shape[0], 512)

    d["x"] = f["L0_attn_hidden_states"].reshape(NT, 128, 128).transpose(1, 0, 2)
    wq, wk = f["L0_attn_Wq"], f["L0_attn_Wk"]
    bq, bk = f["L0_attn_bq"][None], f["L0_attn_bk"][None]
    d["wqk"] = np.stack([heads(wq, 0), heads(wk, 0, 8), heads(wk, 0, 16)], 1)
    d["wks"] = np.stack([heads(wk, 0), heads(wk, 8), heads(wk, 16)], 1)
    d["l0_wv"], d["l0_wo"] = f["L0_attn_Wv"], f["L0_attn_Wo"]
    d["l0_sw"] = f["L0_ffn_weight"].T
    d["relT"] = f["L0_attn_rel_embeddings"].T
    d["l0_rows"] = np.concatenate([heads(bk, 0)[0], heads(bk, 8)[0], heads(bk, 16)[0], f["L0_attn_bv"],
                                   f["L0_attn_bo"]])[None]
    cols = [heads(bq, 0), heads(bk, 0, 8), heads(bk, 0, 16)]
    d["l0_cols"] = np.concatenate([c.reshape(4, 128).T for c in cols], axis=1)
    rep = lambda v: np.tile(np.asarray(v)[None, :], (128, 1))
    d["l0_lnsc"], d["l0_lnb"] = rep(f["L0_attn_ln_scale"]), rep(f["L0_attn_ln_bias"])
    for s in "fb":
        d["wz_" + s], d["wh_" + s] = f["L1_attn_Wz_" + s], f["L1_attn_Wh_" + s]
    d["l1_cols"] = np.stack([f["L1_attn_bz_f"], f["L1_attn_bh_f"], f["L1_attn_bz_b"], f["L1_attn_bh_b"]], 1)
    d["l1_wout"] = f["L1_attn_W_out"].reshape(2, 128, 128).transpose(1, 0, 2)
    d["l1_bout"] = f["L1_attn_b_out"][None]
    d["router"] = f["L1_ffn_w_router"]
    d["wi"] = f["L1_ffn_wi"].transpose(1, 0, 2)
    d["wo2"] = f["L1_ffn_wo"].reshape(8, 4, 128, 128).transpose(2, 0, 1, 3)
    d["ctxT"] = f["L2_attn_context"].reshape(512, 96).T
    d["l2_wqT"] = f["L2_attn_Wq"].reshape(128, 8, 128).transpose(2, 1, 0)
    d["l2_wk"], d["l2_wv"] = f["L2_attn_Wk"], f["L2_attn_Wv"]
    d["l2_wout"] = f["L2_attn_Wout"].reshape(8, 128, 128).transpose(1, 0, 2)
    d["l2_bout"] = f["L2_attn_bout"][None]
    d["l2_w"] = np.stack([f["L2_ffn_W_r"].T, f["L2_ffn_W_k"].T, f["L2_ffn_W_v"].T], 1)
    d["l2_mu"] = np.stack([f["L2_ffn_mu_r"], f["L2_ffn_mu_k"]], 1)
    qkv = f["L3_attn_qkv_w"].T
    d["l3_qkv"] = qkv
    qb = f["L3_attn_qkv_b"]
    d["l3_rows"] = np.concatenate([qb[128:], f["L3_attn_p2_b"]])[None]
    d["l3_cols"] = np.stack([qb[:128], f["L3_attn_p1_b"], np.repeat(f["L3_attn_temperature"].reshape(16), 8)], 1)
    g = np.stack([np.tile(f["L3_attn_kn_g"], 16), np.tile(f["L3_attn_vn_g"], 16)])
    b = np.stack([np.tile(f["L3_attn_kn_b"], 16), np.tile(f["L3_attn_vn_b"], 16)])
    d["l3_gb"] = np.tile(np.stack([g, b])[None].reshape(1, 2, 256), (128, 1, 1))
    ab = np.zeros((16, 8, 16, 8), np.float32)
    for h in range(16):
        ab[h, :, h, :] = f["L3_attn_attn_bias"][h]
    d["l3_ab"] = ab.reshape(128, 128)
    d["l3_p"] = np.stack([f["L3_attn_p1_w"].T, f["L3_attn_p2_w"].T], 1)
    d["l3_ng"], d["l3_nb"] = rep(f["L3_ffn_norm_g"]), rep(f["L3_ffn_norm_b"])
    d["l3_sg"], d["l3_sb"] = rep(f["L3_ffn_slot_g"]), rep(f["L3_ffn_slot_b"])
    d["l3_scale"] = np.tile(f["L3_ffn_scale"][None], (128, 1))
    d["slots"] = f["L3_ffn_slot_embeds"].reshape(8, 128, 128).transpose(1, 0, 2)
    d["wgu"] = np.stack([f["L3_ffn_Wg"], f["L3_ffn_Wu"]], 1).transpose(2, 0, 1, 3)
    d["wd"] = f["L3_ffn_Wd"].reshape(16, 2, 128, 128).transpose(2, 0, 1, 3)
    d["l3_fb"] = np.stack([f["L3_ffn_bg"].reshape(16, 2, 128), f["L3_ffn_bu"].reshape(16, 2, 128)], 1).transpose(3, 0, 1, 2)
    d["l3_bd"] = f["L3_ffn_bd"].reshape(1, 2048)
    return {k: np.ascontiguousarray(v) for k, v in d.items()}


def kernel(**inputs):
    import concourse.bacc as bacc
    from concourse.bass_utils import run_bass_kernel_spmd

    nc = bacc.Bacc("TRN2", target_bir_lowering=False, num_devices=1)
    arrays = layout(inputs)
    a = {k: nc.dram_tensor("in_" + k, v.shape, mybir.dt.from_np(v.dtype), kind="ExternalInput").ap()
         for k, v in arrays.items()}
    out = nc.dram_tensor("out", (128, NT, 128), F32, kind="ExternalOutput").ap()
    program(nc, a, out)
    r = run_bass_kernel_spmd(nc, [{"in_" + k: v for k, v in arrays.items()}], core_ids=[0])
    y = r.results[0]["out"]
    return np.ascontiguousarray(y.transpose(1, 0, 2)).reshape(8, 512, 128)
```

```python
import numpy as np
from contextlib import ExitStack
import concourse.bass as bass
from concourse import mybir

F32 = mybir.dt.float32
BF = mybir.dt.bfloat16
ACT = mybir.ActivationFunctionType
ALU = mybir.AluOpType
AX = mybir.AxisListType


class Queues:
    ENG = ("tensor", "vector", "scalar", "gpsimd", "sync")

    def __init__(self, nc, ctx):
        self.nc, self.ctx = nc, ctx
        self.q = {e: [] for e in self.ENG}
        self.sem = {e: ctx.enter_context(nc.semaphore("s_" + e)) for e in self.ENG}
        self.n = {e: 0 for e in self.ENG}
        self.seen = {e: {} for e in self.ENG}
        self.dsem, self.dn = {}, {}

    def _waits(self, e, waits):
        flat = []

        def walk(w):
            if w is None:
                return
            if isinstance(w, tuple) and w and isinstance(w[0], str):
                flat.append(w)
            else:
                for x in w:
                    walk(x)
        walk(waits)
        most = {}
        for name, sem, v in flat:
            if v > most.get(name, (None, 0))[1]:
                most[name] = (sem, v)
        for name, (sem, v) in most.items():
            if self.seen[e].get(name, 0) < v:
                self.seen[e][name] = v
                self.q[e].append(("w", sem, v))

    def op(self, e, fn, *waits):
        self._waits(e, waits)
        self.n[e] += 1
        self.q[e].append(("i", fn, self.sem[e], 1))
        return (e, self.sem[e], self.n[e])

    def dma(self, e, name, out, in_, *waits):
        self._waits(e, waits)
        if name not in self.dsem:
            self.dsem[name] = self.ctx.enter_context(self.nc.semaphore("d_" + name))
            self.dn[name] = 0
        self.dn[name] += 16
        self.q[e].append(("i", lambda g: g.dma_start(out, in_), self.dsem[name], 16))
        return (name, self.dsem[name], self.dn[name])

    def last(self):
        return [(e, self.sem[e], self.n[e]) for e in self.ENG if self.n[e]]

    def alldma(self):
        return [(n, self.dsem[n], self.dn[n]) for n in self.dsem]

    def emit(self, block):
        def run(e):
            def body(g):
                for item in self.q[e]:
                    if item[0] == "w":
                        g.wait_ge(item[1], item[2])
                    else:
                        item[1](g).then_inc(item[2], item[3])
            return body
        block.tensor(run("tensor"))
        block.vector(run("vector"))
        block.scalar(run("scalar"))
        block.gpsimd(run("gpsimd"))
        block.sync(run("sync"))


class Ring:

    def __init__(self, bufs, free=()):
        self.bufs, self.free = bufs, [list(free) for _ in bufs]
        self.queue = list(range(len(bufs)))

    def take(self):
        assert self.queue, "all buffers are in use"
        k = self.queue.pop(0)
        return k, self.bufs[k], self.free[k]

    def done(self, k, *tokens):
        self.free[k] = list(tokens)
        self.queue.append(k)


NB, NT, NH = 8, 32, 16
SEQ = 512
SLOTS = 6
PITCH = 256
SLOT = 4 * 128 * PITCH + 128
QSZ = 2 * 16 * 48 * 512 + 16 * 12 * 512
PBN = 6
NRS = 4
NCD = 4
VEC_PT = (1,)

_FAR = [0] + [1] * 6 + [2] * 5 + [3] * 5 + [4] * 4 + [5] * 4 + [6] * 3 + [7] * 3 + [8] * 3 + [9] * 3
_FAR += [10] * 2 + [11] * 2 + [12] * 2 + [13] * 2 + [14] * 2 + [15]


def buckets(near, edge):
    out = {}
    for n, f in enumerate(_FAR):
        r = -64 + n
        out[r] = f
        out[-r] = min(64 - f, 63)
    for r in range(-15, 16):
        out[r] = near
    out[16] = out[-16] = edge
    return out


def constants():
    c = {}
    c["ident"] = np.eye(128, dtype=np.float32)
    i = np.arange(128)
    c["tri"] = np.stack([i[None, :] < i[:, None], i[None, :] > i[:, None]], 1).astype(np.float32)
    c["trile"] = (i[:, None] <= i[None, :]).astype(np.float32)
    oc, od = np.zeros((64, 128), np.float32), np.zeros((64, 128), np.float32)
    bc, bd = buckets(47, 48), buckets(17, 16)
    oc[63, 0] = od[63, 0] = 1
    oc[0, 0] = od[0, 0] = -1
    for s in range(1, 128):
        r = 64 - s
        oc[bc[r], s] += 1
        oc[63 if r > 0 else 0, s] -= 1
        r = s - 64
        od[bd[r], s] += 1
        od[63 if r > 0 else 0, s] -= 1
    ends = np.zeros((64, 2), np.float32)
    ends[63, 0] = 1
    ends[0, 1] = 1
    c["oh"] = np.concatenate([oc, od, ends], axis=1)
    c["iota"] = np.tile(np.arange(64, dtype=np.float32)[None, :], (128, 1))
    c["rev"] = np.tile(np.arange(8, 0, -1).astype(np.float32)[None, :], (128, 1))
    head = i // 8
    pat = np.zeros((128, 3), np.float32)
    pat[54:57, 0] = 1
    pat[48:51, 1] = 1
    pat[51:54, 2] = 1
    c["pat"] = pat
    c["mask16"] = (head[:, None] == i[None, :16]).astype(np.float32)
    c["bdmask"] = (head[:, None] == head[None, :]).astype(np.float32)
    return c


def program(nc, a, out):
    ctx = ExitStack()
    with ctx:
        def sb(name, shape):
            return ctx.enter_context(nc.sbuf_tensor(name, shape, F32))

        X = sb("X", [128, NT, 128])
        XN = sb("XN", [128, NT, 128])
        XT = sb("XT", [128, NT * 128])
        ident = sb("ident", [128, 128])
        ARENA = 40700
        AR = sb("AR", [128, ARENA])
        PS = ctx.enter_context(nc.psum_tensor("PS", [128, 8, 512], F32))
        scr = nc.dram_tensor("scr", [2 * SLOTS, SLOT], F32, kind="Internal").ap()
        qsc = nc.dram_tensor("qsc", [2 * QSZ], BF, kind="Internal").ap()
        pgd = nc.dram_tensor("pgd", [128, 3, 256], BF, kind="Internal").ap()
        Q = Queues(nc, ctx)
        top = [0]

        def take(*dims, rows=128):
            n = int(np.prod(dims))
            ap = AR[0:rows, top[0]:top[0] + n]
            top[0] += n
            assert top[0] <= ARENA, top[0]
            if len(dims) == 1:
                return ap
            names = "abcd"[:len(dims)]
            spec = {names[i]: dims[i] for i in range(1, len(dims))}
            return ap.rearrange(f"p ({' '.join(names)}) -> p {' '.join(names)}", **spec)

        def barrier():
            now = Q.last() + Q.alldma()
            for e in Q.ENG:
                Q._waits(e, now)
            top[0] = 0

        def M(out, lhsT, rhs, start, stop, *w):
            return Q.op("tensor", lambda e: e.matmul(out, lhsT, rhs, start=start, stop=stop), *w)

        def TR(out, in_, *w):
            k = in_.shape[0]
            return Q.op("tensor", lambda e: e.transpose(out, in_, ident[0:k, 0:k]), *w)

        def act(out, in_, func, *w, bias=0.0, scale=1.0, accum=None):
            return Q.op("scalar", lambda e: e.activation(out, in_, func, bias=bias, scale=scale, accum_out=accum), *w)

        def tt(e, out, in0, in1, op, *w):
            return Q.op(e, lambda g: g.tensor_tensor(out, in0, in1, op), *w)

        def ts(e, out, in0, s1, s2, op0, op1, *w):
            if op1 is None:
                return Q.op(e, lambda g: g.tensor_scalar(out, in0, s1, None, op0), *w)
            return Q.op(e, lambda g: g.tensor_scalar(out, in0, s1, s2, op0, op1), *w)

        def stt(out, in0, s, in1, op0, op1, *w):
            return Q.op("vector", lambda g: g.scalar_tensor_tensor(out, in0, s, in1, op0, op1), *w)

        def red(out, in_, op, *w):
            return Q.op("vector", lambda g: g.tensor_reduce(out, in_, AX.X, op), *w)

        def rec(out, in_, *w):
            return Q.op("vector", lambda g: g.reciprocal(out, in_), *w)

        def cp(e, out, in_, *w):
            if e == "scalar":
                return act(out, in_, ACT.Copy, *w)
            return Q.op(e, lambda g: g.tensor_copy(out, in_), *w)

        def memset(e, out, v, *w):
            return Q.op(e, lambda g: g.memset(out, v), *w)

        def load(dst, name, *w, e="sync"):
            return Q.dma(e, "in_" + name, dst, a[name], *w)

        def bc(ap, shape):
            return ap.to_broadcast(shape)

        def rsqrt(y, v, tmp, *w):
            t = act(tmp, v, ACT.Sqrt, *w)
            t = rec(y, tmp, t)
            t = tt("vector", tmp, y, y, ALU.mult, t)
            t = tt("vector", tmp, tmp, v, ALU.mult, t)
            t = ts("vector", tmp, tmp, -0.5, 1.5, ALU.mult, ALU.add, t)
            return tt("vector", y, y, tmp, ALU.mult, t)

        def stats(src, n, eps, mv, st, y, v, tmp, *w):
            ts_ = [Q.op("vector", lambda g, i=i: g.bn_stats(st[:, i, :], src[:, i, :]), *w) for i in range(n)]
            for i in range(n):
                t = Q.op("vector", lambda g, i=i: g.bn_aggr(mv[:, i, :], st[:, i, :]), ts_[i])
            t = ts("vector", v, mv[:, 0:n, 1], eps, None, ALU.add, None, t)
            return rsqrt(y, v, tmp, t)

        t_id = load(ident[:, :], "ident")
        t_z = [memset("vector", PS[:, k, :], 0.0) for k in range(8)]
        t_x = Q.dma("scalar", "x", X[:, :, :], a["x"])

        def norm_top(*w):
            o = top[0]
            st, mv = take(NT, 6), take(NT, 2)
            y, v, tmp = take(NT), take(NT), take(NT)
            R = Ring([PS[:, k, :] for k in range(8)], [*w])
            t = stats(X, NT, 1e-5, mv, st, y, v, tmp, *w)
            tn = []
            for i in range(NT):
                e = "vector" if i % 2 else "gpsimd"
                tn.append(Q.op(e, lambda g, i=i: g.tensor_scalar(XN[:, i, :], X[:, i, :], mv[:, i, 0:1], y[:, i:i + 1],
                                                                 ALU.subtract, ALU.mult), t, *w))
            done = []
            for k in range(NT // 4):
                r, ps, free = R.take()
                for j in range(4):
                    t = TR(ps[:, j * 128:j * 128 + 128], XN[:, 4 * k + j, :], tn[4 * k + j], free, t_id)
                t = cp("scalar", XT[:, k * 512:k * 512 + 512], ps, t)
                R.done(r, t)
                done.append(t)
            return tn + done
        ptb = take(5, 4, 512)
        wq, wk, wv, wo, sw = take(128), take(128), take(128), take(128), take(128)
        tri = take(2, 128)
        lnsc, lnb, bvt, bot = take(128), take(128), take(128), take(128)
        colb, pat, mask16 = take(2), take(3), take(16)
        relT, oh, bkt = ptb[:, 0, 0, 0:64], ptb[0:64, 0, 1, 0:258], ptb[0:64, 0, 2, 0:128]
        t_w = [load(wq, "l0_wq"), load(wk, "l0_wk", e="scalar"), load(wv, "l0_wv"), load(wo, "l0_wo", e="scalar"),
               load(sw, "l0_sw"), load(relT, "relT"), load(bkt, "l0_bkt", e="scalar"), load(colb, "l0_cols"),
               load(oh, "oh"), load(lnsc, "l0_lnsc"), load(lnb, "l0_lnb"), load(bvt, "l0_bvt"), load(bot, "l0_bot"),
               load(tri, "tri"), load(pat, "pat"), load(mask16, "mask16")]
        t_sw = act(sw, sw, ACT.Sign, t_w)
        posk, PGF, PGR = ptb[0:64, 1, 0, 0:128], ptb[:, 1, 1, 0:256], ptb[:, 1, 2, 0:256]
        PGS = ptb[:, 1, 3, 0:384].bitcast(BF).rearrange("p (a s) -> p a s", a=3)

        def take16(*dims):
            n = int(np.prod(dims))
            ap = take(n // 2).bitcast(BF)
            names = "abcd"[:len(dims)]
            return ap.rearrange(f"p ({' '.join(names)}) -> p {' '.join(names)}",
                                **{names[i]: dims[i] for i in range(1, len(dims))})

        PGO = take16(2, 16, 128)
        OP = [[take16(4, 512) for _ in range(3)] for _ in range(2)]
        SEL = take(2, 16, 4)
        xf_at = top[0]
        XF = take(3, 512)
        XR_ = take(512)
        PARTS = [take16(3, 512) for _ in range(3)]
        VA = [take(4, 16, 9) for _ in range(2)]
        PTB = Ring([ptb[:, k, :, :] for k in range(5)])
        GG = [take(8, 129) for _ in range(3)]
        CD = [take(8, PITCH) for _ in range(3)] + [XN[:, 16 * x:16 * x + 16, :].rearrange("p a b -> p (a b)").rearrange("p (a b) -> p a b", b=PITCH) for x in range(NCD - 3)]
        CB, DB = [c[:, 0:4, :] for c in CD], [c[:, 4:8, :] for c in CD]
        PB = Ring([take(512) for _ in range(PBN)])
        TMP = take(8, 128)
        OS = take(512)
        CT = take(4, 4, 4, 8)
        RD = take(4, 4)
        MX = take(8, 2)
        T1 = take(4, 128)
        CTT = T1.rearrange("p a b -> p (a b)")
        lst, lmv, ly, lv, ltmp = take(4, 6), take(4, 2), take(4), take(4), take(4)
        save = top[0]

        zt = memset("vector", ptb[:, 2, :, :], 0.0)
        SZ = 2 * SLOT
        t_scr = [Q.dma("sync", f"z{k}", bass.AP(scr.tensor, k * SLOT, [[SLOT // 128, 128], [1, SLOT // 128]]),
                       ptb[:, 2, :, :].rearrange("p a b -> p (a b)")[:, 0:SLOT // 128], zt) for k in range(2 * SLOTS)]
        t_cb = [memset("gpsimd", CD[k], 0.0) for k in range(3)]
        t_cb += [memset("vector", g, 0.0) for g in GG]
        t_va = [memset("gpsimd", VA[k], 1.0) for k in range(2)]
        t_pg0 = memset("gpsimd", PGO, 0.0)
        t_op = [ts("vector", OP[s_][x].rearrange("p a b -> p (a b)"), ptb[:, 2, :, :].rearrange("p a b -> p (a b)"),
                   pat[:, x:x + 1], None, ALU.add, None, zt, t_w) for s_ in range(2) for x in range(3)]
        top[0] = xf_at
        t_n = norm_top(t_x, t_z)
        top[0] = save
        t_cb += [memset("gpsimd", CD[k], 0.0, t_n) for k in range(3, NCD)]
        RS = Ring([PS[:, k, :] for k in range(NRS)], t_n)
        R = Ring([PS[:, k, :] for k in range(NRS, 8)], t_n)

        def split(parts, x, tmp, e, t, before=None):
            t = cp("scalar", parts[:, 0], x, t)
            t = tt(e, tmp, x, parts[:, 0], ALU.subtract, t, before)
            t = cp("scalar", parts[:, 1], tmp, t)
            return tt(e, parts[:, 2], tmp, parts[:, 1], ALU.subtract, t)

        SC = float(1.0 / np.sqrt(np.float32(24.0)))
        t_cs = ts("vector", colb[:, 0:1], colb[:, 0:1], SC, None, ALU.mult, None, t_w)
        r, ps, free = R.take()
        t = M(ps[0:64, 0:128], relT, wk, True, True, free, t_w)
        t = tt("vector", posk, ps[0:64, 0:128], bkt, ALU.add, t)
        R.done(r, t)
        r, ps, free = R.take()
        M(ps[:, 0:256], posk, oh[:, 0:256], True, True, free, t)
        t = M(ps[:, 256:258], posk, oh[:, 256:258], True, True)
        cp("vector", PGF[:, 0:128], ps[:, 0:128], t)
        tp = ts("vector", PGF[:, 128:256], ps[:, 128:256], SC, None, ALU.mult, None, t)
        far = take(2)
        t = cp("vector", far, ps[:, 256:258], t)
        R.done(r, t)
        tz = memset("vector", SEL, 0.0)
        t_sel = [ts("vector", SEL[:, x, :, 2 * x + y], mask16, far[:, y:y + 1], None, ALU.mult, None, t, tz, t_w)
                 for x in range(2) for y in range(2)]
        t_sel.append(ts("vector", SEL[:, 1], SEL[:, 1], SC, None, ALU.mult, None, t_sel))
        t = split(PGS, PGF, PGR, "vector", tp)
        t = Q.dma("sync", "pgw", pgd, PGS, t)
        t_pg = []
        for k, order in enumerate(((0, 1, 2, 0, 1, 0), (0, 0, 0, 1, 1, 2))):
            for x, part in enumerate(order):
                src = bass.AP(pgd.tensor, part * 256 + k * 128, [[768, 8], [8 * 768, 16], [1, 128]])
                t_pg.append(Q.dma("sync", f"pg{k}{x}", PGO[8 * x:8 * x + 8, k], src, t, t_pg0))
        t_pos = t_pg + t_sel + [t_cs]
        PTB.free = [Q.last() for _ in range(5)]

        st = {"opfree": [t_op, t_op], "op": {}, "g": {}, "c": {}, "d": {}, "rd": {}, "s": {}, "va": [[], []],
              "tv": {}, "cfree": [[] for _ in range(NCD)], "gfree": [[], [], []], "ofree": [t_n], "ctfree": [],
              "mx": [[] for _ in range(8)], "m": {}, "tmpfree": [], "qd": [[], []], "wrote": {}, "parts": [[], [], []],
              "xf": [], "xr": [], "t1free": []}

        def proj(b):
            xb = XT[:, b * SEQ:b * SEQ + SEQ]
            tx = []
            for k, w in enumerate((wq, wk)):
                r, ps, free = R.take()
                t = M(ps, w, xb, True, True, free, t_w, t_n)
                t = act(XF[:, k, :], ps, ACT.Identity, t, st["xf"], t_cs, bias=colb[:, k:k + 1], scale=1.0 if k else SC)
                R.done(r, t)
                tx.append(t)
            r, ps, free = R.take()
            M(ps[0:64, :], SEL[:, 0].rearrange("p a b -> p (a b)"), XF[:, 0, :], True, False, free, tx, t_pos)
            t = M(ps[0:64, :], SEL[:, 1].rearrange("p a b -> p (a b)"), XF[:, 1, :], False, True)
            t = cp("scalar", XF[0:64, 2, :], ps[0:64, :], t, st["xf"])
            R.done(r, t)
            tx.append(t)
            wrote = []
            s_ = b % 2
            for k in range(3):
                n = 64 if k == 2 else 128
                P = PARTS[k]
                t = split(P[0:n], XF[0:n, k, :], XR_[0:n], "vector", [tx[k], st["parts"][k]], st["xr"])
                st["xr"] = [t]
                base = s_ * QSZ + k * 16 * 48 * 512
                if k == 2:
                    w = [Q.dma("sync", f"qw2_{s_}", bass.AP(qsc.tensor, base, [[1536, 64], [1, 1536]]),
                               P[0:64].rearrange("p a b -> p (a b)"), t, st["qd"][s_])]
                else:
                    order = (0, 0, 0, 1, 1, 2) if k == 0 else (0, 1, 2, 0, 1, 0)
                    w = [Q.dma("sync", f"qw{k}{x}_{s_}",
                               bass.AP(qsc.tensor, base + x * 8 * 512, [[48 * 512, 16], [512, 8], [1, 512]]),
                               P[:, part, :], t, st["qd"][s_]) for x, part in enumerate(order)]
                st["parts"][k] = w
                wrote += w
            st["xf"] = [t]
            st["wrote"][b] = wrote
            st["qd"][s_] = []
            r, ps, free = R.take()
            for q in range(4):
                i = b * 4 + q
                t = M(ps[:, q * 128:q * 128 + 128], XT[:, i * 128:i * 128 + 128], wv, True, True, free)
            t = tt("vector", VA[b % 2][:, :, :, 0:8], ps.rearrange("p (q h d) -> p q h d", q=4, h=16),
                   bc(bvt.rearrange("p (h d) -> p h d", h=16).unsqueeze(1), [128, 4, 16, 8]), ALU.add, t, t_va,
                   st["va"][b % 2])
            R.done(r, t)
            st["tv"][b] = t

        def load_group(G):
            b, g = divmod(G, 4)
            s_, o = b % 2, OP[G % 2]
            fr = st["opfree"][G % 2]
            base = s_ * QSZ
            rows = lambda k: bass.AP(qsc.tensor, base + (k * 16 + 4 * g) * 48 * 512, [[512, 48], [48 * 512, 4], [1, 512]])
            far_ = base + 2 * 16 * 48 * 512 + 4 * g * 4 * 1536
            toks = [Q.dma("sync", f"o{G % 2}q", o[0][0:48], rows(0), st["wrote"][b], fr),
                    Q.dma("sync", f"o{G % 2}a", o[0][48:54], bass.AP(qsc.tensor, far_, [[512, 6], [6144, 4], [1, 512]]),
                          st["wrote"][b], fr)]
            for x in (1, 2):
                toks.append(Q.dma("sync", f"o{G % 2}k{x}", o[x][0:48], rows(1), st["wrote"][b], fr))
                src = bass.AP(qsc.tensor, far_ + (1 + x) * 1536, [[512, 3], [6144, 4], [1, 512]])
                toks.append(Q.dma("sync", f"o{G % 2}f{x}", o[x][54:57], src, st["wrote"][b], fr))
            st["op"][G] = toks
            st["qd"][s_] = st["qd"][s_] + toks

        def emit_g(n, x):
            G, hh = divmod(n, 4)
            r, ps, free = R.take()
            for q in range(4):
                t = M(ps[:, q * 128:q * 128 + 128], OP[G % 2][x][:, hh, q * 128:q * 128 + 128],
                      PGO[:, x, n % 16, :], True, True, free, st["op"][G], t_pos)
            later(1, lambda: g_out(n, x, r, ps, t))

        def g_out(n, x, r, ps, t):
            k = n % 3
            t = cp(G_OUT[x], GG[k][:, 4 * x:4 * x + 4, 0:128], ps.rearrange("p (a b) -> p a b", a=4), t, st["gfree"][k], t_cb)
            R.done(r, t)
            st["g"].setdefault(n, []).append(t)
            if x == 0:
                return
            s_ = n % SLOTS
            dst = bass.AP(scr.tensor, s_ * SZ + 129, [[PITCH, 128], [128 * PITCH, 8], [1, 128]])
            toks = st["g"][n]
            wr = Q.dma("sync", f"w{s_}", dst, GG[k][:, :, 1:129], toks, st["rd"].get(n - SLOTS, []), t_scr, t_cb)
            st["g"][n] = (toks, wr)

        def emit_r(n):
            s_, k = n % SLOTS, n % NCD
            toks, wr = st["g"][n]
            base = s_ * SZ + 128
            buf, G = CD[k], GG[n % 3]
            lo = bass.AP(scr.tensor, base, [[PITCH - 1, 64], [128 * PITCH, 8], [1, 192]])
            hi = bass.AP(scr.tensor, base + 64 * (PITCH - 1) + 64, [[PITCH - 1, 64], [128 * PITCH, 8], [1, 192]])
            r1 = Q.dma("sync", f"r{k}l", buf[0:64, :, 0:192], lo, wr, st["cfree"][k], t_cb)
            r2 = Q.dma("sync", f"r{k}h", buf[64:128, :, 64:256], hi, wr, st["cfree"][k], t_cb)
            t = tt("gpsimd", TMP.rearrange("p (x a) b -> p x a b", x=2), bc(tri.unsqueeze(2), [128, 2, 4, 128]),
                   bc(G[:, :, 0:1].rearrange("p (x a) b -> p x a b", x=2), [128, 2, 4, 128]), ALU.mult, toks, t_w, st["tmpfree"])
            st["gfree"][n % 3] = [t, wr]
            t = tt("gpsimd", buf[:, :, 64:192], buf[:, :, 64:192], TMP, ALU.add, t, r1, r2)
            st["tmpfree"] = [t]
            st["rd"][n] = [r1, r2]
            st["c"][n] = st["d"][n] = [t, r1, r2]

        def s_mm(v):
            n, ib = divmod(v, 4)
            G, hh = divmod(n, 4)
            k = n % NCD
            OQ, OL, OU = OP[G % 2]
            r, S, free = RS.take()
            q = OQ[:, hh, ib * 128:ib * 128 + 128]
            if ib:
                M(S[:, 0:128 * ib], q, OL[:, hh, 0:128 * ib], True, False, free)
            M(S[:, 128 * ib:512], q, OU[:, hh, 128 * ib:512], ib == 0, False, free)
            if ib:
                jb = ib - 1
                M(S[0:64, 128 * jb + 64:128 * jb + 128], DB[k][:, jb, 192:256], ident[:, 64:128],
                  False, False, st["d"][n])
            if ib < 3:
                jb = ib + 1
                M(S[64:128, 128 * jb:128 * jb + 64], DB[k][:, jb, 0:64], ident[:, 0:64], False, False,
                  st["d"][n])
            tS = M(S[:, 128 * ib:128 * ib + 128], DB[k][:, ib, 64:192], ident[:, :], False, True, st["d"][n])
            st["s"][v] = (r, S, tS)
            if ib == 3 and hh == 3:
                st["opfree"][G % 2] = [tS]

        def s_soft(v):
            n, ib = divmod(v, 4)
            k, m = n % NCD, v % 8
            r, S, tS = st["s"][v]
            lo, hi = max(0, 128 * ib - 64), min(512, 128 * ib + 192)
            o = 64 - 128 * ib
            t = tt("vector", S[:, lo:hi], S[:, lo:hi], CB[k][:, ib, lo + o:hi + o], ALU.add, tS, st["c"][n])
            if ib == 3:
                st["cfree"][k] = [t, tS]
            st["m"][v] = Q.op("vector", lambda g: g.tensor_reduce(MX[:, m, 0:1], S, AX.X, ALU.max, negate=True),
                              t, st["mx"][m])

        def s_exp(v):
            m = v % 8
            r, S, _ = st["s"][v]
            kp, P, fp = PB.take()
            te = act(P, S, ACT.Exp, st["m"][v], fp, bias=MX[:, m, 0:1])
            st["mx"][m] = [te]
            st["s"][v] = (te, kp, P)
            RS.done(r, te)

        def p_mm(v):
            te, kp, P = st["s"][v]
            r, ps, free = R.take()
            for jb in range(4):
                t = TR(ps[:, jb * 128:jb * 128 + 128], P[:, jb * 128:jb * 128 + 128], te, free)
            PB.done(kp, t)
            st["s"][v] = (r, ps, t)

        def p_out(v):
            n, ib = divmod(v, 4)
            if ib == 0:
                st["ptk", n] = PTB.take()
                st["pte", n] = []
            kb, PT, fpt = st["ptk", n]
            r, ps, t = st["s"].pop(v)
            t = cp("vector" if ib in VEC_PT else "scalar", PT[:, :, ib * 128:ib * 128 + 128],
                   ps.rearrange("p (a b) -> p a b", a=4), t, fpt)
            R.done(r, t)
            st["pte", n].append(t)
            if ib == 3 and n % 4 == 3:
                later(1, lambda: emit_pv(n // 16, n % 16 // 4))

        def emit_pv(b, g, jb=0, ro=None):
            ns = [b * 16 + g * 4 + hh for hh in range(4)]
            if jb == 0:
                ro = R.take()
            r, OB, fo = ro
            for hh in range(4):
                kb, PT, _ = st["ptk", ns[hh]]
                t = M(OB[32 * hh:32 * hh + 9, :], VA[b % 2][:, jb, g * 4 + hh, :], PT[:, jb, :], jb == 0, jb == 3,
                      st["pte", ns[hh]], st["tv"][b], fo)
            if jb < 3:
                later(1, lambda: emit_pv(b, g, jb + 1, ro))
                return
            for hh in range(4):
                PTB.done(st["ptk", ns[hh]][0], t)
            if g == 3:
                st["va"][b % 2] = [t]
            later(1, lambda: pv_out(b, g, r, OB, t))

        def pv_out(b, g, r, OB, t):
            t = cp("scalar", OS, OB, t, st["ofree"])
            R.done(r, t)
            later(1, lambda: heads(b, g, t))

        def heads(b, g, t):
            r, ps, free = R.take()
            for q in range(4):
                t2 = TR(ps[:, q * 128:q * 128 + 128], OS[:, q * 128:q * 128 + 128], t, free)
            st["ofree"] = [t2]
            later(1, lambda: heads_out(b, g, r, ps, t2))

        def heads_out(b, g, r, ps, t2):
            v = ps.rearrange("p (q h r) -> p q h r", q=4, h=4)
            t = rec(RD, v[:, :, :, 8], t2)
            t = tt("vector", CT[:, :, g, :, :], v[:, :, :, 0:8], bc(RD.unsqueeze(3), [128, 4, 4, 8]), ALU.mult, t,
                   st["ctfree"])
            R.done(r, t)
            if g == 3:
                later(1, lambda: tail(b, t))

        def later(k, fn):
            todo.setdefault(now[0] + k, []).append(fn)

        now, todo = [0], {}

        def tail(b, tc):
            r, ps, free = R.take()
            for q in range(4):
                t = TR(ps[:, q * 128:q * 128 + 128], CT[:, q, :, :, :].rearrange("p g h d -> p (g h d)"), tc, free)
            st["ctfree"] = [t]
            later(1, lambda: tail_ct(b, r, ps, t))

        def tail_ct(b, r, ps, t):
            t = cp("scalar", CTT, ps, t, st["t1free"])
            R.done(r, t)
            later(1, lambda: tail_mm(b, t))

        def tail_mm(b, t):
            r, ps, free = R.take()
            for q in range(4):
                o = ps[:, q * 128:q * 128 + 128]
                i = b * 4 + q
                M(o, CTT[:, q * 128:q * 128 + 128], wo, True, False, t, free)
                t1 = M(o, XT[:, i * 128:i * 128 + 128], ident[:, :], False, True)
            later(1, lambda: tail_out(b, r, ps, t1))

        def tail_out(b, r, ps, t1):
            t = tt("vector", T1, ps.rearrange("p (q c) -> p q c", q=4), bc(bot.unsqueeze(1), [128, 4, 128]), ALU.add, t1)
            R.done(r, t)
            r, ps, free = R.take()
            for q in range(4):
                i = b * 4 + q
                t2 = M(ps[:, q * 128:q * 128 + 128], XT[:, i * 128:i * 128 + 128], sw, True, True, free, t_sw)
            later(1, lambda: tail_sw(b, r, ps, t2, t))

        def tail_sw(b, r, ps, t2, t):
            xs = slice(b * 4, b * 4 + 4)
            tx = tt("vector", X[:, xs, :], ps.rearrange("p (q c) -> p q c", q=4), X[:, xs, :], ALU.add, t2)
            R.done(r, tx)
            later(1, lambda: tail_norm(b, t, tx))

        def tail_norm(b, t, tx):
            xs = slice(b * 4, b * 4 + 4)
            t = stats(T1, 4, 1e-7, lmv, lst, ly, lv, ltmp, t)
            later(1, lambda: tail_end(b, t, tx))

        def tail_end(b, t, tx):
            xs = slice(b * 4, b * 4 + 4)
            for q in range(4):
                t3 = ts("vector", T1[:, q, :], T1[:, q, :], lmv[:, q, 0:1], ly[:, q:q + 1], ALU.subtract, ALU.mult, t)
            t = tt("vector", T1, T1, bc(lnsc.unsqueeze(1), [128, 4, 128]), ALU.mult, t3)
            t = tt("vector", T1, T1, bc(lnb.unsqueeze(1), [128, 4, 128]), ALU.add, t)
            st["t1free"] = [tt("vector", X[:, xs, :], X[:, xs, :], T1, ALU.add, t, tx)]

        NBH = NB * NH
        G_OUT = ("scalar", "vector")
        R_AT = 1
        STAGES = ((s_exp, 2), (p_out, 5), (s_soft, 1), (s_mm, 0),  (p_mm, 4))

        def step(v):
            n, ib = divmod(v, 4)
            for stage, lag in STAGES:
                if 0 <= v - lag < 4 * NBH:
                    stage(v - lag)
            run_later()

        def run_later():
            for fn in todo.pop(now[0], []):
                fn()
            now[0] += 1

        proj(0)
        load_group(0)
        for n in range(3):
            for x in range(2):
                emit_g(n, x)
                run_later()
        run_later()
        emit_r(0)
        emit_r(1)
        for v in range(-1, 4 * NBH + 8):
            n, ib = divmod(v, 4)
            if ib == 0 and n % 16 == 6 and n // 16 + 1 < NB:
                proj(n // 16 + 1)
            if ib == 0 and v >= 0 and n % 4 == 0 and n // 4 + 1 < NBH // 4:
                load_group(n // 4 + 1)
            if ib == R_AT and 0 <= v and n + 2 < NBH:
                emit_r(n + 2)
            if ib in (0, 2) and v >= 0 and n + 3 < NBH:
                emit_g(n + 3, ib // 2)
            step(v)
        while todo:
            run_later()

        barrier()
        names = ["wz_f", "wh_f", "wz_b", "wh_b"]
        w1 = [take(128) for _ in names]
        c1 = take(4)
        wout, bout = take(2, 128), take(128)
        router = take(8)
        trile, iota, rev = take(128), take(64), take(8)
        wi, wo2 = take(8, 512), take(8, 4, 128)
        t_w = [load(w1[k], names[k]) for k in range(4)] + [load(c1, "l1_cols"), load(wout, "l1_wout"), load(bout, "l1_bout"),
               load(router, "router"), load(trile, "trile"), load(iota, "iota"), load(rev, "rev")]
        t_wi, t_wo2 = load(wi, "wi", e="scalar"), load(wo2, "wo2", e="scalar")
        ones128 = take(128)
        t_o = memset("gpsimd", ones128, 1.0)
        c1x = take(4)
        t_c = None
        for k in range(4):
            t_c = ts("vector", c1x[:, k:k + 1], c1[:, k:k + 1], 1.0 if k % 2 else -1.0, 0.5 if k % 2 else 0.0, ALU.mult,
                     ALU.add, t_w)
        PRI, PROB = take(NT, 8), take(NT, 8)
        big = top[0]
        t_n = norm_top()
        top[0] = big
        R = Ring([PS[:, k, :] for k in range(8)], t_n)

        t_x = tt("gpsimd", X[:, :, :], X[:, :, :], bc(bout.unsqueeze(1), [128, NT, 128]), ALU.add, t_w, t_n)

        L, L2, E1, E2, W_ = (take(NT, 8) for _ in range(5))
        m8, s8 = take(NT), take(NT)
        full = [128, NT, 8]
        col = lambda v: bc(v.unsqueeze(2), full)
        r, ps, free = R.take()
        for i in range(NT):
            t = M(ps[:, i * 8:i * 8 + 8], XT[:, i * 128:i * 128 + 128], router, True, True, free, t_w)
        t = cp("vector", L.rearrange("p a b -> p (a b)"), ps[:, 0:256], t)
        R.done(r, t)
        tL = t
        t = red(m8, L, ALU.max, tL)
        t = tt("vector", PROB, L, col(m8), ALU.subtract, t)
        t = act(PROB, PROB, ACT.Exp, t)
        t = red(s8, PROB, ALU.add, t)
        t = rec(s8, s8, t)
        tP = tt("vector", PROB, PROB, col(s8), ALU.mult, t)
        revb = bc(rev.unsqueeze(1), full)

        def first_max(dst, src, t):
            t = red(m8, src, ALU.max, t)
            t = tt("vector", W_, src, col(m8), ALU.is_equal, t)
            t = tt("vector", W_, W_, revb, ALU.mult, t)
            t = red(m8, W_, ALU.max, t)
            return tt("vector", dst, W_, col(m8), ALU.is_equal, t)
        t1 = first_max(E1, L, tP)
        t = stt(L2, E1, -3.0e38, L, ALU.mult, ALU.add, t1)
        t2 = first_max(E2, L2, t)
        v1, v2 = (E.rearrange("p (b q) e -> p b q e", q=4) for E in (E1, E2))
        r, ps, free = R.take()
        for k, (E, v) in enumerate(((E1, v1), (E2, v2))):
            o = ps[:, 256 * k:256 * k + 256]
            ov = o.rearrange("p (b q e) -> p b q e", q=4, e=8)
            for q in range(4):
                prev = [(v, j) for j in range(q)] + ([(v1, j) for j in range(4)] if k else [])
                t = M(ov[:, :, q, :], trile, v[:, :, q, :], True, not prev, free, t1, t2, t_w)
                for x, (pv, j) in enumerate(prev):
                    t = M(ov[:, :, q, :], ones128, pv[:, :, j, :], False, x == len(prev) - 1, t_o)
        ps_v = ps.rearrange("p (k n e) -> p k n e", k=2, e=8)
        ta = tt("vector", E1, E1, ps_v[:, 0], ALU.mult, t)
        tb = tt("vector", E2, E2, ps_v[:, 1], ALU.mult, t)
        R.done(r, tb)
        t = tt("vector", PRI, E1, E2, ALU.max, ta, tb)
        tPRI = ts("vector", PRI, PRI, -1.0, None, ALU.add, None, t)

        top[0] = big
        A_ = Ring([take(512) for _ in range(3)], [tPRI])
        Z_ = Ring([take(512) for _ in range(3)], [tPRI])
        G_ = Ring([take(512) for _ in range(3)], [tPRI])
        H_ = Ring([take(512) for _ in range(4)], [tPRI])

        def scan_unit(b, d):
            toks = []
            for k in range(2):
                r, ps, free = R.take()
                t = M(ps, w1[2 * d + k], XT[:, b * SEQ:b * SEQ + SEQ], True, True, free, t_w)
                toks.append((r, ps, t))
            (r0, p0, tz), (r1, p1, th) = toks
            ka, A, fa = A_.take()
            kz, Z, fz = Z_.take()
            kg, G, fg = G_.take()
            kh, H, fh = H_.take()
            t_a = act(A, p0, ACT.Sigmoid, tz, fa, t_c, bias=c1x[:, 2 * d:2 * d + 1], scale=-1.0)
            t_z = act(Z, p0, ACT.Sigmoid, fz, bias=c1[:, 2 * d:2 * d + 1])
            R.done(r0, t_z)
            t_g = act(G, p1, ACT.Sigmoid, th, fg, bias=c1[:, 2 * d + 1:2 * d + 2])
            t = stt(G, p1, c1x[:, 2 * d + 1:2 * d + 2], G, ALU.add, ALU.max, t_g)
            R.done(r1, t)
            t = tt("gpsimd", G, G, Z, ALU.mult, t, t_z)
            Z_.done(kz, t)
            rv = slice(None, None, -1) if d else slice(None)
            t = Q.op("vector", lambda g: g.tensor_tensor_scan(H, A[:, rv], G[:, rv], 0.0, ALU.mult, ALU.add), t, t_a, fh)
            A_.done(ka, t)
            G_.done(kg, t)
            return kh, H, t

        def scan_out(b, hs):
            r, ps, free = R.take()
            for q in range(4):
                o = ps[:, q * 128:q * 128 + 128]
                sl = slice(q * 128, q * 128 + 128)
                M(o, hs[0][1][:, sl], wout[:, 0, :], True, False, hs[0][2], free)
                t = M(o, hs[1][1][:, sl], wout[:, 1, :], False, True, hs[1][2])
            for kh, _, _ in hs:
                H_.done(kh, t)
            xs = slice(b * 4, b * 4 + 4)
            t = tt("vector", X[:, xs, :], X[:, xs, :], ps.rearrange("p (q c) -> p q c", q=4), ALU.add, t, t_x)
            R.done(r, t)
            return t
        hs = None
        tX = []
        for b in range(NB):
            cur = [scan_unit(b, d) for d in range(2)]
            if b:
                tX.append(scan_out(b - 1, hs))
            hs = cur
        tX.append(scan_out(NB - 1, hs))

        for e in ("vector", "gpsimd", "scalar"):
            Q._waits(e, Q.last())
        top[0] = big
        XIN = take(8, 8, 64)
        EO = take(4, 8, 128)
        HT = Ring([take(4, 512) for _ in range(2)])
        DD = Ring([take(8, 64) for _ in range(5)])
        iob = bc(iota.unsqueeze(1), [128, 8, 64])
        t_in = []
        for g in range(8):
            r, ps, free = R.take()
            for q in range(4):
                i = g * 4 + q
                kd, D, fd = DD.take()
                t = tt("vector", D, iob, bc(PRI[:, i, :].unsqueeze(2), [128, 8, 64]), ALU.is_equal, fd)
                t = M(ps, XN[:, i, :], D.rearrange("p a b -> p (a b)"), q == 0, q == 3, t, free)
                DD.done(kd, t)
            t = cp("scalar", XIN[:, :, g, :], ps.rearrange("p (e c) -> p e c", e=8), t)
            R.done(r, t)
            t_in.append(t)
        t_eo = []
        R1 = Ring([PS[:, k, :] for k in range(4)], Q.last())
        R2 = Ring([PS[:, 4:6, :], PS[:, 6:8, :]], Q.last())

        def down(e, kh, H, toks):
            r, ps, free = R2.take()
            rows = slice(64 * (e % 2), 64 * (e % 2) + 64)
            pv = ps.rearrange("p k (g c) -> p (k g) c", c=128)
            for g in range(8):
                for f in range(4):
                    t = M(pv[rows, g, :], H[:, f, g * 64:g * 64 + 64], wo2[:, e, f, :], f == 0, f == 3, toks, free, t_wo2)
            HT.done(kh, t)
            t = cp("vector", EO[rows, e // 2, :, :], pv[rows, :, :], t)
            R2.done(r, t)
            t_eo.append(t)
        prev = None
        for e in range(8):
            kh, H, fh = HT.take()
            toks = []
            for f in range(4):
                r, ps, free = R1.take()
                t = M(ps, wi[:, e, f * 128:f * 128 + 128], XIN[:, e, :, :].rearrange("p g c -> p (g c)"), True, True,
                      t_in, free, t_wi)
                t = act(H[:, f, :], ps, ACT.Gelu_apprx_tanh, t, fh)
                R1.done(r, t)
                toks.append(t)
            if prev:
                down(*prev)
            prev = (e, kh, H, toks)
        down(*prev)
        R = Ring([PS[:, k, :] for k in range(8)], Q.last())
        CTB = Ring([take(4, 128) for _ in range(2)])

        def comb_a(i):
            kd, D, fd = DD.take()
            for e in range(8):
                t = ts("vector", D[:, e, :], iota, PRI[:, i, e:e + 1], PROB[:, i, e:e + 1], ALU.is_equal, ALU.mult, fd)
            r, ps, free = R.take()
            Df = D.rearrange("p a b -> p (a b)")
            for c in range(4):
                t2 = TR(ps[:, c * 128:c * 128 + 128], Df[:, c * 128:c * 128 + 128], t, free)
            DD.done(kd, t2)
            kc, CB_, fc = CTB.take()
            t = cp("scalar", CB_, ps.rearrange("p (a b) -> p a b", a=4), t2, fc)
            R.done(r, t)
            return i, kc, CB_, t

        def comb_b(i, kc, CB_, t):
            r, ps, free = R.take()
            for c in range(4):
                t = M(ps[:, 0:128], CB_[:, c, :], EO[:, c, i // 4, :], c == 0, c == 3, t, t_eo, free)
            CTB.done(kc, t)
            t = tt("vector", X[:, i, :], X[:, i, :], ps[:, 0:128], ALU.add, t)
            R.done(r, t)
        prev = None
        for i in range(NT):
            cur = comb_a(i)
            if prev:
                comb_b(*prev)
            prev = cur
        comb_b(*prev)

        barrier()
        ctxT, wk_, wv_ = take(512, rows=96), take(1024, rows=96), take(1024, rows=96)
        wqT, wout2 = take(8, 128), take(8, 128)
        w3, mu, mu1 = take(3, 128), take(2), take(2)
        BO = take(128)
        t_w = [load(ctxT, "ctxT"), load(wk_, "l2_wk"), load(wv_, "l2_wv", e="scalar"), load(wqT, "l2_wqT"),
               load(wout2, "l2_wout", e="scalar"), load(BO, "l2_bout"), load(w3, "l2_w"), load(mu, "l2_mu")]
        MH, VW = take(8, 512), take(8, 4, 128)
        XR, XK = take(NB, SEQ), take(NB, SEQ)
        KA = Ring([take(512) for _ in range(2)])
        RG = Ring([take(512) for _ in range(2)])
        SVK = Ring([take(512) for _ in range(2)])
        base = top[0]
        R = Ring([PS[:, k, :] for k in range(4)])
        t_v = []
        for h in range(8):
            hs_ = slice(h * 128, h * 128 + 128)
            for w, kind in ((wk_, 0), (wv_, 1)):
                r, ps, free = R.take()
                t = M(ps, w[:, hs_], ctxT, True, True, free, t_w)
                k, S_, fs = SVK.take()
                t = cp("scalar" if kind else "vector", S_, ps, t, fs)
                R.done(r, t)
                r, ps, free = R.take()
                if kind == 0:
                    t = M(ps, wqT[:, h, :], S_, True, True, t, free)
                    SVK.done(k, t)
                    t = cp("scalar", MH[:, h, :], ps, t)
                else:
                    for j in range(4):
                        t = M(ps[:, j * 128:j * 128 + 128], S_[:, j * 128:j * 128 + 128], wout2[:, h, :], True, True, t, free)
                    SVK.done(k, t)
                    t = cp("vector", VW[:, h, :, :], ps.rearrange("p (j c) -> p j c", j=4), t)
                R.done(r, t)
                t_v.append(t)
        Q._waits("tensor", Q.last())
        Q._waits("scalar", Q.last())
        t_n = norm_top(Q.last())
        top[0] = base
        R = Ring([PS[:, k, :] for k in range(8)], t_n)
        t_mu = ts("vector", mu1, mu, -1.0, 1.0, ALU.mult, ALU.add, t_w)
        XTb = XT[:, :].rearrange("p (b t) -> p b t", b=NB)
        t_x = tt("gpsimd", X[:, :, :], X[:, :, :], bc(BO.unsqueeze(1), [128, NT, 128]), ALU.add, t_w, t_n)
        t_f = []
        for b in range(NB):
            toks = []
            for k, dst in enumerate((XR, XK)):
                t0 = memset("gpsimd", dst[:, b, 0:1], 0.0)
                t = act(dst[:, b, 1:], XTb[:, b, 0:SEQ - 1], ACT.Copy, t_n, t_mu, scale=mu1[:, k:k + 1])
                toks.append(stt(dst[:, b, :], XTb[:, b, :], mu[:, k:k + 1], dst[:, b, :], ALU.mult, ALU.add, t, t0))
            r, ps, free = R.take()
            t = M(ps, w3[:, 1, :], XK[:, b, :], True, True, toks[1], free)
            k, K_, fk = KA.take()
            t = act(K_, ps, ACT.Relu, t, fk)
            R.done(r, t)
            t = act(K_, K_, ACT.Square, t)
            r, ps, free = R.take()
            r2, ps2, free2 = R.take()
            for q in range(4):
                sl = slice(q * 128, q * 128 + 128)
                tr = M(ps[:, sl], XR[:, b, sl], w3[:, 0, :], True, True, toks[0], free)
            for q in range(4):
                sl = slice(q * 128, q * 128 + 128)
                tv = M(ps2[:, sl], K_[:, sl], w3[:, 2, :], True, True, t, free2)
            KA.done(k, tv)
            k, G, fg = RG.take()
            t = act(G, ps, ACT.Sigmoid, tr, fg)
            R.done(r, t)
            t = tt("vector", G, G, ps2, ALU.mult, t, tv)
            R.done(r2, t)
            xs = slice(b * 4, b * 4 + 4)
            t = tt("gpsimd", X[:, xs, :], X[:, xs, :], G.rearrange("p (q c) -> p q c", q=4), ALU.add, t, t_x)
            RG.done(k, t)
            t_f.append(t)
        for e in ("vector", "scalar", "gpsimd"):
            Q._waits(e, Q.last())
        top[0] = base
        now = Q.last()
        RS = Ring([PS[:, 0:2, :], PS[:, 2:4, :]], now)
        R = Ring([PS[:, 4, :], PS[:, 5, :]], now)
        RO = Ring([PS[:, 6, :], PS[:, 7, :]], now)
        PB = Ring([take(512) for _ in range(6)])
        PT = Ring([take(512) for _ in range(4)])
        MXR = Ring([take(2) for _ in range(4)])
        NBR = Ring([take(2) for _ in range(4)])
        DNR = Ring([take(8) for _ in range(3)])
        C = 1.5 * 128 ** -0.5
        pend = {}

        def att_s(i, p):
            r, S, free = RS.take()
            for x in range(2):
                t = M(S[:, x, :], XT[:, i * 128:i * 128 + 128], MH[:, 2 * p + x, :], True, True, free, t_v)
            km, MX_, fm = MXR.take()
            kn, NB_, fn = NBR.take()
            t = red(MX_, S, ALU.max, t, fm)
            t = ts("vector", NB_, MX_, -C, None, ALU.mult, None, t, fn)
            MXR.done(km, t)
            if p == 0:
                pend["d", i] = DNR.take()
            kd, DN, fd = pend["d", i]
            es = []
            for x in range(2):
                kp, P, fp = PB.take()
                te = act(P, S[:, x, :], ACT.Exp, t, fp, fd, bias=NB_[:, x:x + 1], scale=C,
                         accum=DN[:, 2 * p + x:2 * p + x + 1])
                es.append((te, kp, P))
            NBR.done(kn, te)
            RS.done(r, te)
            pend[i, p] = es

        def att_t(i, p):
            res = []
            for x, (te, kp, P) in enumerate(pend[i, p]):
                r, ps, free = R.take()
                for j in range(4):
                    t = TR(ps[:, j * 128:j * 128 + 128], P[:, j * 128:j * 128 + 128], te, free)
                PB.done(kp, t)
                kt, T_, ft = PT.take()
                t = cp("vector" if x else "scalar", T_, ps, t, ft)
                R.done(r, t)
                res.append((kt, T_, t))
            pend["t", i, p] = res

        def att_v(i, p):
            if p % 2 == 0:
                pend["o", i, p // 2] = RO.take()
            ro, O, fo = pend["o", i, p // 2]
            for x, (kt, T_, t) in enumerate(pend["t", i, p]):
                h = 2 * p + x
                for j in range(4):
                    tv = M(O[:, (h % 4) * 128:(h % 4) * 128 + 128], T_[:, j * 128:j * 128 + 128], VW[:, h, j, :], j == 0,
                           j == 3, t, fo)
                PT.done(kt, tv)
            if p % 2:
                kd, DN, _ = pend["d", i]
                half = slice(2 * p - 2, 2 * p + 2)
                t = rec(DN[:, half], DN[:, half], tv)
                for h in range(2 * p - 2, 2 * p + 2):
                    t = stt(X[:, i, :], O[:, (h % 4) * 128:(h % 4) * 128 + 128], DN[:, h:h + 1], X[:, i, :], ALU.mult,
                            ALU.add, t)
                RO.done(ro, t)
                if p == 3:
                    DNR.done(kd, t)
        seq = [(i, p) for i in range(NT) for p in range(4)]
        for n in range(len(seq) + 2):
            if n < len(seq):
                att_s(*seq[n])
            if 1 <= n < len(seq) + 1:
                att_t(*seq[n - 1])
            if n >= 2:
                att_v(*seq[n - 2])

        barrier()
        wqkv, rows3, cols3 = take(384), take(384), take(3)
        gb, ab, pw, bdm = take(2, 256), take(128), take(2, 128), take(128)
        ng, nb_, sg, sbb, scl = take(128), take(128), take(128), take(128), take(1)
        fb, bd = take(16, 2, 2), take(8, 128)
        SE = take(8, 128)
        t_w = [load(wqkv, "l3_qkv"), load(rows3, "l3_rows"), load(cols3, "l3_cols"), load(gb, "l3_gb", e="scalar"),
               load(ab, "l3_ab"), load(pw, "l3_p"), load(bdm, "bdmask", e="scalar"), load(ng, "l3_ng"), load(nb_, "l3_nb"),
               load(sg, "l3_sg"), load(sbb, "l3_sb"), load(scl, "l3_scale"), load(fb, "l3_fb", e="scalar"),
               load(bd, "l3_bd"), load(SE, "slots", e="scalar")]
        SET = take(1024)
        SLT = take(16, NB, 64)
        base = top[0]
        t_n = norm_top()
        top[0] = base
        R = Ring([PS[:, k, :] for k in range(8)], t_n)
        t_x = tt("gpsimd", X[:, :, :], X[:, :, :], bc(rows3[:, 256:384].unsqueeze(1), [128, NT, 128]), ALU.add, t_w, t_n)
        QT = Ring([take(512) for _ in range(2)])
        KV = Ring([take(4, 256) for _ in range(2)])
        SQ = Ring([take(4, 256) for _ in range(2)])
        S1, V1, T2, Y1 = (Ring([take(128) for _ in range(2)]) for _ in range(4))
        KVM = Ring([take(128) for _ in range(2)])
        AT = Ring([take(512) for _ in range(2)])
        HB = Ring([take(512) for _ in range(2)])
        t_tc = ts("vector", cols3[:, 2:3], cols3[:, 2:3], 1.0 / 512, None, ALU.mult, None, t_w)

        def heads_ln(b):
            rq, pq, fq = R.take()
            t = M(pq, wqkv[:, 0:128], XT[:, b * SEQ:b * SEQ + SEQ], True, True, fq, t_w)
            kq, QT_, f = QT.take()
            tq = act(QT_, pq, ACT.Identity, t, f, bias=cols3[:, 0:1])
            R.done(rq, tq)
            kk, KV_, f = KV.take()
            for x in range(2):
                r, ps, free = R.take()
                for y in range(2):
                    q = 2 * x + y
                    o = ps[:, y * 256:y * 256 + 256]
                    i = b * 4 + q
                    t = M(o, XT[:, i * 128:i * 128 + 128], wqkv[:, 128:384], True, True, free)
                t = tt("vector", KV_[:, 2 * x:2 * x + 2, :], ps.rearrange("p (y c) -> p y c", y=2),
                       bc(rows3[:, 0:256].unsqueeze(1), [128, 2, 256]), ALU.add, t, f)
                R.done(r, t)
            v = KV_.rearrange("p q (h d) -> p (q h) d", d=8)
            ks, SQ_, fs = SQ.take()
            sv = SQ_.rearrange("p q (h d) -> p (q h) d", d=8)
            k1, s1, f1 = S1.take()
            k2, v1, f2 = V1.take()
            k3, tm, f3 = T2.take()
            k4, y1, f4 = Y1.take()
            wide = lambda z: bc(z.unsqueeze(2), [128, 128, 8])
            t = red(s1, v, ALU.add, t, f1)
            t = ts("vector", s1, s1, 0.125, None, ALU.mult, None, t)
            t = tt("gpsimd", v, v, wide(s1), ALU.subtract, t)
            S1.done(k1, t)
            tc_ = t
            t = act(SQ_, KV_, ACT.Square, t, fs)
            t = red(v1, sv, ALU.add, t, f2)
            SQ.done(ks, t)
            t = ts("vector", v1, v1, 0.125, 1e-5, ALU.mult, ALU.add, t)
            t = rsqrt(y1, v1, tm, t, f3, f4)
            V1.done(k2, t)
            T2.done(k3, t)
            t = tt("vector", v, v, wide(y1), ALU.mult, t, tc_)
            Y1.done(k4, t)
            t = tt("gpsimd", KV_, KV_, bc(gb[:, 0, :].unsqueeze(1), [128, 4, 256]), ALU.mult, t, t_w)
            t = tt("gpsimd", KV_, KV_, bc(gb[:, 1, :].unsqueeze(1), [128, 4, 256]), ALU.add, t)
            return b, kq, QT_, tq, kk, KV_, t

        def linear(b, kq, QT_, tq, kk, KV_, tkv):
            r, ps, free = R.take()
            for q in range(4):
                t = M(ps[:, 0:128], KV_[:, q, 0:128], KV_[:, q, 128:256], q == 0, q == 3, tkv, free)
            KV.done(kk, t)
            km, KM, f = KVM.take()
            t = stt(KM, ps[:, 0:128], cols3[:, 2:3], bdm, ALU.mult, ALU.mult, t, t_tc, f)
            R.done(r, t)
            t = tt("vector", KM, KM, ab, ALU.add, t)
            r, ps, free = R.take()
            t = M(ps, KM, QT_, True, True, t, tq, free)
            KVM.done(km, t)
            QT.done(kq, t)
            ka, A, f = AT.take()
            t = tt("vector", A, ps, XT[:, b * SEQ:b * SEQ + SEQ], ALU.add, t, f)
            R.done(r, t)
            r, ps, free = R.take()
            t = M(ps, pw[:, 0, :], A, True, True, t, free)
            AT.done(ka, t)
            kh, H, f = HB.take()
            t = act(H, ps, ACT.Gelu, t, f, bias=cols3[:, 1:2])
            R.done(r, t)
            r, ps, free = R.take()
            for q in range(4):
                o = ps[:, q * 128:q * 128 + 128]
                t2 = M(o, H[:, q * 128:q * 128 + 128], pw[:, 1, :], True, True, t, free)
            HB.done(kh, t2)
            xs = slice(b * 4, b * 4 + 4)
            t = tt("vector", X[:, xs, :], X[:, xs, :], ps.rearrange("p (q c) -> p q c", q=4), ALU.add, t2, t_x)
            R.done(r, t)
            return tt("gpsimd", X[:, xs, :], X[:, xs, :], XN[:, xs, :], ALU.add, t)
        prev = None
        for b in range(NB):
            cur = heads_ln(b)
            if prev:
                linear(*prev)
            prev = cur
        linear(*prev)

        for e in ("vector", "scalar", "gpsimd", "tensor"):
            Q._waits(e, Q.last())
        top[0] = base
        st3, mv3 = take(NT, 6), take(NT, 2)
        y3, v3, tm3 = take(NT), take(NT), take(NT)
        R = Ring([PS[:, k, :] for k in range(8)], Q.last())

        def norm_affine(src, n, g_, b_, dstT, extra):
            t = stats(src, n, 1e-5, mv3, st3, y3[:, 0:n], v3[:, 0:n], tm3[:, 0:n], Q.last())
            for i in range(n):
                tl = ts("vector", src[:, i, :], src[:, i, :], mv3[:, i, 0:1], y3[:, i:i + 1], ALU.subtract, ALU.mult, t)
            t = tt("gpsimd", src, src, bc(g_.unsqueeze(1), [128, n, 128]), ALU.mult, tl, t_w)
            t = tt("gpsimd", src, src, bc(b_.unsqueeze(1), [128, n, 128]), ALU.add, t)
            if extra is not None:
                t = ts("vector", src, src, extra, None, ALU.mult, None, t)
            res = []
            for k in range(n // 4):
                r, ps, free = R.take()
                for j in range(4):
                    tr = TR(ps[:, j * 128:j * 128 + 128], src[:, 4 * k + j, :], t, free)
                tr = cp("scalar", dstT[:, k * 512:k * 512 + 512], ps, tr)
                R.done(r, tr)
                res.append(tr)
            return res + [t]
        t_se = norm_affine(SE, 8, sg, sbb, SET, scl)
        t_x2 = norm_affine(XN[:, :, :], NT, ng, nb_, XT, None)
        top[0] = base
        for e in ("vector", "scalar", "gpsimd"):
            Q._waits(e, Q.last())
        now = Q.last()
        RS = Ring([PS[:, 0:2, :], PS[:, 2:4, :]], now)
        R = Ring([PS[:, 4, :], PS[:, 5, :]], now)
        RO = Ring([PS[:, 6, :], PS[:, 7, :]], now)
        PB = Ring([take(512) for _ in range(6)])
        PT = Ring([take(512) for _ in range(6)])
        MXR = Ring([take(2) for _ in range(4)])
        DNR = Ring([take(2) for _ in range(6)])
        SLK = Ring([take(2, 128) for _ in range(2)])
        pend = {}

        def pair_s(key, lhs, rhs, joint):
            r, S, free = RS.take()
            for x in range(2):
                t = M(S[:, x, :], lhs[x], rhs[x], True, True, free)
            km, MX_, fm = MXR.take()
            if joint:
                t = red(MX_[:, 0:1], S.rearrange("p a b -> p (a b)"), ALU.max, t, fm)
                t = ts("vector", MX_[:, 1:2], MX_[:, 0:1], -1.0, None, ALU.mult, None, t)
                nb2 = [MX_[:, 1:2], MX_[:, 1:2]]
            else:
                t = red(MX_, S, ALU.max, t, fm)
                t = ts("vector", MX_, MX_, -1.0, None, ALU.mult, None, t)
                nb2 = [MX_[:, 0:1], MX_[:, 1:2]]
            kd, DN, fd = DNR.take()
            es = []
            for x in range(2):
                kp, P, fp = PB.take()
                te = act(P, S[:, x, :], ACT.Exp, t, fp, fd, bias=nb2[x], accum=DN[:, x:x + 1])
                es.append((te, kp, P))
            MXR.done(km, te)
            RS.done(r, te)
            pend["e", key] = es, kd, DN

        def pair_t(key):
            es, kd, DN = pend["e", key]
            res = []
            for x, (te, kp, P) in enumerate(es):
                r, ps, free = R.take()
                for j in range(4):
                    t = TR(ps[:, j * 128:j * 128 + 128], P[:, j * 128:j * 128 + 128], te, free)
                PB.done(kp, t)
                kt, T_, ft = PT.take()
                t = cp("vector" if x else "scalar", T_, ps, t, ft)
                R.done(r, t)
                res.append((kt, T_, t))
            pend["t", key] = res

        def slot_v(key):
            b, p = key
            _, kd, DN = pend["e", key]
            ro, O, fo = RO.take()
            for x, (kt, T_, t) in enumerate(pend["t", key]):
                for j in range(4):
                    tv = M(O[:, x * 128:x * 128 + 128], T_[:, j * 128:j * 128 + 128], XN[:, b * 4 + j, :], j == 0, j == 3,
                           t, fo)
                PT.done(kt, tv)
            t = rec(DN, DN, tv)
            ks, S_, fs = SLK.take()
            t = tt("vector", S_, O[:, 0:256].rearrange("p (x c) -> p x c", x=2), bc(DN.unsqueeze(2), [128, 2, 128]),
                   ALU.mult, t, fs)
            DNR.done(kd, t)
            for x in range(2):
                tr = TR(O[:, 256 + x * 128:384 + x * 128], S_[:, x, :], t)
            SLK.done(ks, tr)
            t = cp("scalar", SLT[:, 4 * p:4 * p + 4, b, :], O[:, 256:512].rearrange("p (e s) -> p e s", e=4), tr)
            RO.done(ro, t)
            return t
        seq = [(b, p) for b in range(NB) for p in range(4)]
        for n in range(len(seq) + 2):
            if n < len(seq):
                b, p = seq[n]
                xb = XT[:, b * SEQ:b * SEQ + SEQ]
                pair_s((b, p), [SET[:, (2 * p + x) * 128:(2 * p + x) * 128 + 128] for x in range(2)], [xb, xb], False)
            if 1 <= n < len(seq) + 1:
                pair_t(seq[n - 1])
            if n >= 2:
                t_sl = slot_v(seq[n - 2])

        for e in ("vector", "scalar", "gpsimd", "tensor"):
            Q._waits(e, Q.last())
        top[0] = base
        EO = take(8, NB, 128)
        WG = Ring([take(2, 256) for _ in range(3)])
        WD = Ring([take(2, 128) for _ in range(3)])
        GB = Ring([take(2, 512) for _ in range(2)])
        now = Q.last()
        R1 = Ring([PS[:, k, :] for k in range(4)], now)
        R2 = Ring([PS[:, 4:6, :], PS[:, 6:8, :]], now)

        def up(e):
            kw, W, fw = WG.take()
            kd, D, fd = WD.take()
            tw = Q.dma("sync", f"wg{kw}", W, a["wgu"][:, e, :, :], fw, now)
            td = Q.dma("sync", f"wd{kd}", D, a["wd"][:, e, :, :], fd, now)
            kg, G, fg = GB.take()
            toks = []
            rhs = SLT[:, e, :, :].rearrange("p b s -> p (b s)")
            for f in range(2):
                r, ps, free = R1.take()
                t = M(ps, W[:, 0, f * 128:f * 128 + 128], rhs, True, True, tw, free)
                r2, ps2, free2 = R1.take()
                t2 = M(ps2, W[:, 1, f * 128:f * 128 + 128], rhs, True, True, free2)
                t = act(G[:, f, :], ps, ACT.Gelu, t, fg, bias=fb[:, e, 0, f:f + 1])
                R1.done(r, t)
                t = stt(G[:, f, :], ps2, fb[:, e, 1, f:f + 1], G[:, f, :], ALU.add, ALU.mult, t, t2)
                R1.done(r2, t)
                toks.append(t)
            WG.done(kw, t2)
            return e, kd, D, td, kg, G, toks

        def dn(e, kd, D, td, kg, G, toks):
            r, ps, free = R2.take()
            rows = slice(64 * (e % 2), 64 * (e % 2) + 64)
            pv = ps.rearrange("p k (g c) -> p (k g) c", c=128)
            for g in range(8):
                for f in range(2):
                    t = M(pv[rows, g, :], G[:, f, g * 64:g * 64 + 64], D[:, f, :], f == 0, f == 1, toks, td, free)
            WD.done(kd, t)
            GB.done(kg, t)
            t = tt("vector", EO[rows, e // 2, :, :], pv[rows, :, :], bc(bd[rows, e // 2, :].unsqueeze(1), [64, 8, 128]),
                   ALU.add, t, t_w)
            R2.done(r, t)
            return t
        prev = None
        t_eo = []
        for e in range(16):
            cur = up(e)
            if prev:
                t_eo.append(dn(*prev))
            prev = cur
        t_eo.append(dn(*prev))

        for e in ("vector", "scalar", "gpsimd", "tensor"):
            Q._waits(e, Q.last())
        now = Q.last()
        RS = Ring([PS[:, 0:2, :], PS[:, 2:4, :]], now)
        R = Ring([PS[:, 4, :], PS[:, 5, :]], now)
        RO = Ring([PS[:, 6, :], PS[:, 7, :]], now)
        PB = Ring([take(512) for _ in range(6)])
        PT = Ring([take(512) for _ in range(6)])
        MXR = Ring([take(2) for _ in range(4)])
        DNR = Ring([take(2) for _ in range(6)])
        pend.clear()

        def comb_v(i):
            _, kd, DN = pend["e", i]
            ro, O, fo = RO.take()
            for x, (kt, T_, t) in enumerate(pend["t", i]):
                for j in range(4):
                    tv = M(O[:, 0:128], T_[:, j * 128:j * 128 + 128], EO[:, 4 * x + j, i // 4, :], x + j == 0,
                           x + j == 4, t, fo)
                PT.done(kt, tv)
            t = tt("vector", DN[:, 0:1], DN[:, 0:1], DN[:, 1:2], ALU.add, tv)
            t = rec(DN[:, 0:1], DN[:, 0:1], t)
            t = stt(X[:, i, :], O[:, 0:128], DN[:, 0:1], X[:, i, :], ALU.mult, ALU.add, t)
            DNR.done(kd, t)
            RO.done(ro, t)
        for n in range(NT + 2):
            if n < NT:
                xt = XT[:, n * 128:n * 128 + 128]
                pair_s(n, [xt, xt], [SET[:, 0:512], SET[:, 512:1024]], True)
            if 1 <= n < NT + 1:
                pair_t(n - 1)
            if n >= 2:
                comb_v(n - 2)

        Q.dma("sync", "out", out, X[:, :, :], Q.last())
        Q._waits("sync", Q.alldma())
        block = ctx.enter_context(nc.Block())
        Q.emit(block)


def layout(inp):
    f = {k: np.asarray(v) for k, v in inp.items()}
    d = constants()

    d["x"] = f["L0_attn_hidden_states"].reshape(NT, 128, 128).transpose(1, 0, 2)
    d["l0_wq"], d["l0_wk"] = f["L0_attn_Wq"], f["L0_attn_Wk"]
    d["l0_wv"], d["l0_wo"] = f["L0_attn_Wv"], f["L0_attn_Wo"]
    d["l0_sw"] = f["L0_ffn_weight"].T
    d["relT"] = f["L0_attn_rel_embeddings"].T
    d["l0_cols"] = np.stack([f["L0_attn_bq"], f["L0_attn_bk"]], 1)
    rep = lambda v: np.tile(np.asarray(v)[None, :], (128, 1))
    d["l0_lnsc"], d["l0_lnb"] = rep(f["L0_attn_ln_scale"]), rep(f["L0_attn_ln_bias"])
    d["l0_bvt"], d["l0_bot"], d["l0_bkt"] = rep(f["L0_attn_bv"]), rep(f["L0_attn_bo"]), rep(f["L0_attn_bk"])[:64]
    for s in "fb":
        d["wz_" + s], d["wh_" + s] = f["L1_attn_Wz_" + s], f["L1_attn_Wh_" + s]
    d["l1_cols"] = np.stack([f["L1_attn_bz_f"], f["L1_attn_bh_f"], f["L1_attn_bz_b"], f["L1_attn_bh_b"]], 1)
    d["l1_wout"] = f["L1_attn_W_out"].reshape(2, 128, 128).transpose(1, 0, 2)
    d["l1_bout"] = rep(f["L1_attn_b_out"])
    d["router"] = f["L1_ffn_w_router"]
    d["wi"] = f["L1_ffn_wi"].transpose(1, 0, 2)
    d["wo2"] = f["L1_ffn_wo"].reshape(8, 4, 128, 128).transpose(2, 0, 1, 3)
    d["ctxT"] = f["L2_attn_context"].reshape(512, 96).T
    d["l2_wqT"] = f["L2_attn_Wq"].reshape(128, 8, 128).transpose(2, 1, 0)
    d["l2_wk"], d["l2_wv"] = f["L2_attn_Wk"], f["L2_attn_Wv"]
    d["l2_wout"] = f["L2_attn_Wout"].reshape(8, 128, 128).transpose(1, 0, 2)
    d["l2_bout"] = rep(f["L2_attn_bout"])
    d["l2_w"] = np.stack([f["L2_ffn_W_r"].T, f["L2_ffn_W_k"].T, f["L2_ffn_W_v"].T], 1)
    d["l2_mu"] = np.stack([f["L2_ffn_mu_r"], f["L2_ffn_mu_k"]], 1)
    qkv = f["L3_attn_qkv_w"].T
    d["l3_qkv"] = qkv
    qb = f["L3_attn_qkv_b"]
    d["l3_rows"] = rep(np.concatenate([qb[128:], f["L3_attn_p2_b"]]))
    d["l3_cols"] = np.stack([qb[:128], f["L3_attn_p1_b"], np.repeat(f["L3_attn_temperature"].reshape(16), 8)], 1)
    g = np.stack([np.tile(f["L3_attn_kn_g"], 16), np.tile(f["L3_attn_vn_g"], 16)])
    b = np.stack([np.tile(f["L3_attn_kn_b"], 16), np.tile(f["L3_attn_vn_b"], 16)])
    d["l3_gb"] = np.tile(np.stack([g, b])[None].reshape(1, 2, 256), (128, 1, 1))
    ab = np.zeros((16, 8, 16, 8), np.float32)
    for h in range(16):
        ab[h, :, h, :] = f["L3_attn_attn_bias"][h]
    d["l3_ab"] = ab.reshape(128, 128)
    d["l3_p"] = np.stack([f["L3_attn_p1_w"].T, f["L3_attn_p2_w"].T], 1)
    d["l3_ng"], d["l3_nb"] = rep(f["L3_ffn_norm_g"]), rep(f["L3_ffn_norm_b"])
    d["l3_sg"], d["l3_sb"] = rep(f["L3_ffn_slot_g"]), rep(f["L3_ffn_slot_b"])
    d["l3_scale"] = np.tile(f["L3_ffn_scale"][None], (128, 1))
    d["slots"] = f["L3_ffn_slot_embeds"].reshape(8, 128, 128).transpose(1, 0, 2)
    d["wgu"] = np.stack([f["L3_ffn_Wg"], f["L3_ffn_Wu"]], 1).transpose(2, 0, 1, 3)
    d["wd"] = f["L3_ffn_Wd"].reshape(16, 2, 128, 128).transpose(2, 0, 1, 3)
    d["l3_fb"] = np.stack([f["L3_ffn_bg"].reshape(16, 2, 128), f["L3_ffn_bu"].reshape(16, 2, 128)], 1).transpose(3, 0, 1, 2)
    d["l3_bd"] = np.repeat(f["L3_ffn_bd"].reshape(8, 2, 128).transpose(1, 0, 2), 64, axis=0)
    return {k: np.ascontiguousarray(v) for k, v in d.items()}


def kernel(**inputs):
    import concourse.bacc as bacc
    from concourse.bass_utils import run_bass_kernel_spmd

    nc = bacc.Bacc("TRN2", target_bir_lowering=False, num_devices=1)
    arrays = layout(inputs)
    a = {k: nc.dram_tensor("in_" + k, v.shape, mybir.dt.from_np(v.dtype), kind="ExternalInput").ap()
         for k, v in arrays.items()}
    out = nc.dram_tensor("out", (128, NT, 128), F32, kind="ExternalOutput").ap()
    program(nc, a, out)
    r = run_bass_kernel_spmd(nc, [{"in_" + k: v for k, v in arrays.items()}], core_ids=[0])
    y = r.results[0]["out"]
    return np.ascontiguousarray(y.transpose(1, 0, 2)).reshape(8, 512, 128)
```

```python
import numpy as np
from contextlib import ExitStack
import concourse.bass as bass
from concourse import mybir

F32 = mybir.dt.float32
F32R = mybir.dt.float32r
BF = mybir.dt.bfloat16
ACT = mybir.ActivationFunctionType
ALU = mybir.AluOpType
AX = mybir.AxisListType


class Queues:
    ENG = ("tensor", "vector", "scalar", "gpsimd", "sync")

    def __init__(self, nc, ctx):
        self.nc, self.ctx = nc, ctx
        self.q = {e: [] for e in self.ENG}
        self.sem = {e: ctx.enter_context(nc.semaphore("s_" + e)) for e in self.ENG}
        self.n = {e: 0 for e in self.ENG}
        self.seen = {e: {} for e in self.ENG}
        self.dsem, self.dn = {}, {}

    def _waits(self, e, waits):
        flat = []

        def walk(w):
            if w is None:
                return
            if isinstance(w, tuple) and w and isinstance(w[0], str):
                flat.append(w)
            else:
                for x in w:
                    walk(x)
        walk(waits)
        most = {}
        for name, sem, v in flat:
            if v > most.get(name, (None, 0))[1]:
                most[name] = (sem, v)
        for name, (sem, v) in most.items():
            if self.seen[e].get(name, 0) < v:
                self.seen[e][name] = v
                self.q[e].append(("w", sem, v))

    def op(self, e, fn, *waits):
        self._waits(e, waits)
        self.n[e] += 1
        self.q[e].append(("i", fn, self.sem[e], 1))
        return (e, self.sem[e], self.n[e])

    def dma(self, e, name, out, in_, *waits):
        self._waits(e, waits)
        if name not in self.dsem:
            self.dsem[name] = self.ctx.enter_context(self.nc.semaphore("d_" + name))
            self.dn[name] = 0
        self.dn[name] += 16
        self.q[e].append(("i", lambda g: g.dma_start(out, in_), self.dsem[name], 16))
        return (name, self.dsem[name], self.dn[name])

    def last(self):
        return [(e, self.sem[e], self.n[e]) for e in self.ENG if self.n[e]]

    def alldma(self):
        return [(n, self.dsem[n], self.dn[n]) for n in self.dsem]

    def emit(self, block):
        def run(e):
            def body(g):
                for item in self.q[e]:
                    if item[0] == "w":
                        g.wait_ge(item[1], item[2])
                    else:
                        item[1](g).then_inc(item[2], item[3])
            return body
        block.tensor(run("tensor"))
        block.vector(run("vector"))
        block.scalar(run("scalar"))
        block.gpsimd(run("gpsimd"))
        block.sync(run("sync"))


class Ring:

    def __init__(self, bufs, free=()):
        self.bufs, self.free = bufs, [list(free) for _ in bufs]
        self.queue = list(range(len(bufs)))

    def take(self):
        assert self.queue, "all buffers are in use"
        k = self.queue.pop(0)
        return k, self.bufs[k], self.free[k]

    def done(self, k, *tokens):
        self.free[k] = list(tokens)
        self.queue.append(k)


NB, NT, NH = 8, 32, 16
SEQ = 512
SLOTS = 6
PITCH = 256
SLOT = 4 * 128 * PITCH + 128
QSZ = 2 * 16 * 48 * 512 + 16 * 12 * 512
PBN = 6
NRS = 4
NCD = 4
VEC_PT = (1,)

_FAR = [0] + [1] * 6 + [2] * 5 + [3] * 5 + [4] * 4 + [5] * 4 + [6] * 3 + [7] * 3 + [8] * 3 + [9] * 3
_FAR += [10] * 2 + [11] * 2 + [12] * 2 + [13] * 2 + [14] * 2 + [15]


def buckets(near, edge):
    out = {}
    for n, f in enumerate(_FAR):
        r = -64 + n
        out[r] = f
        out[-r] = min(64 - f, 63)
    for r in range(-15, 16):
        out[r] = near
    out[16] = out[-16] = edge
    return out


def constants():
    c = {}
    c["ident"] = np.eye(128, dtype=np.float32)
    i = np.arange(128)
    c["tri"] = np.stack([i[None, :] < i[:, None], i[None, :] > i[:, None]], 1).astype(np.float32)
    c["trile"] = (i[:, None] <= i[None, :]).astype(np.float32)
    oc, od = np.zeros((64, 128), np.float32), np.zeros((64, 128), np.float32)
    bc, bd = buckets(47, 48), buckets(17, 16)
    oc[63, 0] = od[63, 0] = 1
    oc[0, 0] = od[0, 0] = -1
    for s in range(1, 128):
        r = 64 - s
        oc[bc[r], s] += 1
        oc[63 if r > 0 else 0, s] -= 1
        r = s - 64
        od[bd[r], s] += 1
        od[63 if r > 0 else 0, s] -= 1
    ends = np.zeros((64, 2), np.float32)
    ends[63, 0] = 1
    ends[0, 1] = 1
    c["oh"] = np.concatenate([oc, od, ends], axis=1)
    c["iota"] = np.tile(np.arange(64, dtype=np.float32)[None, :], (128, 1))
    c["rev"] = np.tile(np.arange(8, 0, -1).astype(np.float32)[None, :], (128, 1))
    head = i // 8
    pat = np.zeros((128, 3), np.float32)
    pat[54:57, 0] = 1
    pat[48:51, 1] = 1
    pat[51:54, 2] = 1
    c["pat"] = pat
    c["mask16"] = (head[:, None] == i[None, :16]).astype(np.float32)
    c["bdmask"] = (head[:, None] == head[None, :]).astype(np.float32)
    return c


def program(nc, a, out):
    ctx = ExitStack()
    with ctx:
        at, rounded = {"n": 0}, []

        def sb(name, shape):
            at[name] = -(-nc.sbuf_base // 32) * 32
            return ctx.enter_context(nc.sbuf_tensor(name, shape, F32))

        X = sb("X", [128, NT, 128])
        XN = sb("XN", [128, NT, 128])
        XT = sb("XT", [128, NT * 128])
        ident = sb("ident", [128, 128])
        NMV = sb("NMV", [128, NT, 2])
        ARENA = 40700
        AR = sb("AR", [128, ARENA])
        PS = ctx.enter_context(nc.psum_tensor("PS", [128, 8, 512], F32))
        scr = nc.dram_tensor("scr", [2 * SLOTS, SLOT], F32, kind="Internal").ap()
        qsc = nc.dram_tensor("qsc", [2 * QSZ], BF, kind="Internal").ap()
        pgd = nc.dram_tensor("pgd", [128, 3, 256], BF, kind="Internal").ap()
        Q = Queues(nc, ctx)
        top = [0]

        def take(*dims, rows=128):
            n = int(np.prod(dims))
            ap = AR[0:rows, top[0]:top[0] + n]
            top[0] += -(-n // 8) * 8
            assert top[0] <= ARENA, top[0]
            if len(dims) == 1:
                return ap
            names = "abcd"[:len(dims)]
            spec = {names[i]: dims[i] for i in range(1, len(dims))}
            return ap.rearrange(f"p ({' '.join(names)}) -> p {' '.join(names)}", **spec)

        def barrier():
            now = Q.last() + Q.alldma()
            for e in Q.ENG:
                Q._waits(e, now)
            top[0] = 0
            rounded.clear()

        def M(out, lhsT, rhs, start, stop, *w):
            return Q.op("tensor", lambda e: e.matmul(out, lhsT, rhs, start=start, stop=stop), *w)

        def TR(out, in_, *w):
            k = in_.shape[0]
            return Q.op("tensor", lambda e: e.transpose(out, in_, ident[0:k, 0:k]), *w)

        def act(out, in_, func, *w, bias=0.0, scale=1.0, accum=None):
            return Q.op("scalar", lambda e: e.activation(out, in_, func, bias=bias, scale=scale, accum_out=accum), *w)

        def tt(e, out, in0, in1, op, *w):
            return Q.op(e, lambda g: g.tensor_tensor(out, in0, in1, op), *w)

        def ts(e, out, in0, s1, s2, op0, op1, *w):
            if op1 is None:
                return Q.op(e, lambda g: g.tensor_scalar(out, in0, s1, None, op0), *w)
            return Q.op(e, lambda g: g.tensor_scalar(out, in0, s1, s2, op0, op1), *w)

        def stt(out, in0, s, in1, op0, op1, *w):
            return Q.op("vector", lambda g: g.scalar_tensor_tensor(out, in0, s, in1, op0, op1), *w)

        def red(out, in_, op, *w):
            return Q.op("vector", lambda g: g.tensor_reduce(out, in_, AX.X, op), *w)

        def minus_max(out, in_, *w):
            return Q.op("vector", lambda g: g.tensor_reduce(out, in_, AX.X, ALU.max, negate=True), *w)

        def rec(out, in_, *w):
            return Q.op("vector", lambda g: g.reciprocal(out, in_), *w)

        def cp(e, out, in_, *w):
            if e == "scalar":
                return act(out, in_, ACT.Copy, *w)
            return Q.op(e, lambda g: g.tensor_copy(out, in_), *w)

        def memset(e, out, v, *w):
            return Q.op(e, lambda g: g.memset(out, v), *w)

        def load(dst, name, *w, e="sync"):
            return Q.dma(e, "in_" + name, dst, a[name], *w)

        def bc(ap, shape):
            return ap.to_broadcast(shape)

        def rsqrt(y, v, tmp, *w):
            return newton(y, v, tmp, act(tmp, v, ACT.Sqrt, *w))

        def newton(y, v, tmp, t):
            t = rec(y, tmp, t)
            t = tt("vector", tmp, y, y, ALU.mult, t)
            t = tt("vector", tmp, tmp, v, ALU.mult, t)
            t = ts("vector", tmp, tmp, -0.5, 1.5, ALU.mult, ALU.add, t)
            return tt("vector", y, y, tmp, ALU.mult, t)

        def stats(src, n, eps, mv, st, y, v, tmp, *w):
            ts_ = [Q.op("vector", lambda g, i=i: g.bn_stats(st[:, i, :], src[:, i, :]), *w) for i in range(n)]
            for i in range(n):
                t = Q.op("vector", lambda g, i=i: g.bn_aggr(mv[:, i, :], st[:, i, :]), ts_[i])
            t = ts("vector", v, mv[:, 0:n, 1], eps, None, ALU.add, None, t)
            return rsqrt(y, v, tmp, t)

        t_id = load(ident[:, :], "ident")
        t_z = [memset("vector", PS[:, k, :], 0.0) for k in range(8)]
        t_x = Q.dma("scalar", "x", X[:, :, :], a["x"])

        known = {}

        def next_stats(b, st4, *w):
            w = [w, known.get("last")]
            ts_ = [Q.op("vector", lambda g, i=i: g.bn_stats(st4[:, i, :], X[:, 4 * b + i, :]), *w) for i in range(4)]
            for i in range(4):
                t = Q.op("vector", lambda g, i=i: g.bn_aggr(NMV[:, 4 * b + i, :], st4[:, i, :]), ts_[i])
            known[b] = known["last"] = t

        def norm_known(pool):
            y, v, tmp = take(NT), take(NT), take(NT)
            t = ts("vector", v, NMV[:, :, 1], 1e-5, None, ALU.add, None, [known[b] for b in range(NB)])
            known.clear()
            t = newton(y, v, tmp, act(tmp, v, ACT.Sqrt, t))
            return [ts("gpsimd" if i % 8 in pool else "vector", XN[:, i, :], X[:, i, :], NMV[:, i, 0:1], y[:, i:i + 1],
                       ALU.subtract, ALU.mult, t) for i in range(NT)]

        def norm_a(*w, pool=(7,)):
            if known:
                return norm_known(pool)
            st_, mv = take(NT, 6), take(NT, 2)
            y, v, tmp = take(NT), take(NT), take(NT)
            tn, roots = [], []
            for c in range(5):
                if c < 4:
                    own = range(8 * c, 8 * c + 8)
                    sl = slice(8 * c, 8 * c + 8)
                    ts_ = [Q.op("vector", lambda g, i=i: g.bn_stats(st_[:, i, :], X[:, i, :]), *w) for i in own]
                    for i, t in zip(own, ts_):
                        t = Q.op("vector", lambda g, i=i: g.bn_aggr(mv[:, i, :], st_[:, i, :]), t)
                    t = ts("vector", v[:, sl], mv[:, sl, 1], 1e-5, None, ALU.add, None, t)
                    roots.append(act(tmp[:, sl], v[:, sl], ACT.Sqrt, t, *w))
                if c:
                    sl = slice(8 * c - 8, 8 * c)
                    t = newton(y[:, sl], v[:, sl], tmp[:, sl], roots[c - 1])
                    for i in range(8 * c - 8, 8 * c):
                        tn.append(ts("gpsimd" if i % 8 in pool else "vector", XN[:, i, :], X[:, i, :], mv[:, i, 0:1], y[:, i:i + 1],
                                     ALU.subtract, ALU.mult, t, *w))
            return tn

        def norm_b(tn, *w):
            R = Ring([PS[:, k, :] for k in range(8)], [*w])
            done = []
            for k in range(NT // 4):
                r, ps, free = R.take()
                for j in range(4):
                    t = TR(ps[:, j * 128:j * 128 + 128], XN[:, 4 * k + j, :], tn[4 * k + j], free, t_id)
                t = cp("scalar", XT[:, k * 512:k * 512 + 512], ps, t, *w)
                R.done(r, t)
                done.append(t)
            return done

        def norm_top(*w):
            tn = norm_a(*w)
            return tn + norm_b(tn, *w)

        def for_halves(*bufs):
            for ap in bufs:
                n = int(np.prod([d[1] for d in list(ap.ap)[1:]]))
                t = nc.alloc_sbuf_tensor_at(f"r{at['n']}", [128, n], F32R, offset=at[ap.tensor.name] + 4 * ap.offset)
                at["n"] += 1
                rounded.append((ap.tensor.name, ap.offset, n, t))

        def f32r(ap):
            name, o, n, t = [x for x in rounded if x[0] == ap.tensor.name and x[1] <= ap.offset < x[1] + x[2]][-1]
            return bass.AP(t, ap.offset - o, [[n, 128]] + list(ap.ap)[1:])

        def f32v(ap):
            return f32r(ap).bitcast(F32)

        def halves(hi, lo, x, t, *w):
            t1 = act(f32r(hi), x, ACT.Copy, t, *w)
            return [t1, tt("vector", f32r(lo), x, f32v(hi), ALU.subtract, t, t1, *w)]

        def M3(out, l, r, start, stop, *w):
            M(out, f32r(l[0]), f32r(r[0]), start, False, *w)
            M(out, f32r(l[1]), f32r(r[0]), False, False)
            return M(out, f32r(l[0]), f32r(r[1]), False, stop)

        def later(k, fn):
            todo.setdefault(now[0] + k, []).append(fn)

        def run_later():
            for fn in todo.pop(now[0], []):
                fn()
            now[0] += 1

        now, todo = [0], {}

        def spread(g, bank=True):
            if bank and len(R.queue) < 2:
                later(1, lambda: spread(g, bank))
                return
            for bank in g:
                later(1, lambda: spread(g, bank))
                return
        ptb = take(5, 4, 512)
        wq, wk, wv, wo, sw = take(128), take(128), take(128), take(128), take(128)
        tri = take(2, 128)
        lnsc, lnb, bvt, bot = take(128), take(128), take(128), take(128)
        colb, pat, mask16 = take(2), take(3), take(16)
        relT, oh, bkt = ptb[:, 0, 0, 0:64], ptb[0:64, 0, 1, 0:258], ptb[0:64, 0, 2, 0:128]
        t_w = [load(wq, "l0_wq"), load(wk, "l0_wk", e="scalar"), load(wv, "l0_wv"), load(wo, "l0_wo", e="scalar"),
               load(sw, "l0_sw"), load(relT, "relT"), load(bkt, "l0_bkt", e="scalar"), load(colb, "l0_cols"),
               load(oh, "oh"), load(lnsc, "l0_lnsc"), load(lnb, "l0_lnb"), load(bvt, "l0_bvt"), load(bot, "l0_bot"),
               load(tri, "tri"), load(pat, "pat"), load(mask16, "mask16")]
        t_sw = act(sw, sw, ACT.Sign, t_w)
        posk, PGF, PGR = ptb[0:64, 1, 0, 0:128], ptb[:, 1, 1, 0:256], ptb[:, 1, 2, 0:256]
        PGS = ptb[:, 1, 3, 0:384].bitcast(BF).rearrange("p (a s) -> p a s", a=3)

        def take16(*dims):
            n = int(np.prod(dims))
            ap = take(n // 2).bitcast(BF)
            names = "abcd"[:len(dims)]
            return ap.rearrange(f"p ({' '.join(names)}) -> p {' '.join(names)}",
                                **{names[i]: dims[i] for i in range(1, len(dims))})

        PGO = take16(2, 16, 128)
        OP = [[take16(4, 512) for _ in range(3)] for _ in range(2)]
        SEL = take(2, 16, 4)
        xf_at = top[0]
        XF = take(3, 512)
        XR_ = take(512)
        PARTS = [take16(3, 512) for _ in range(3)]
        VA = [take(4, 16, 9) for _ in range(2)]
        PTB = Ring([ptb[:, k, :, :] for k in range(5)])
        GG = [take(8, 129) for _ in range(3)]
        CD = [take(8, PITCH) for _ in range(3)] + [XN[:, 16 * x:16 * x + 16, :].rearrange("p a b -> p (a b)").rearrange("p (a b) -> p a b", b=PITCH) for x in range(NCD - 3)]
        CB, DB = [c[:, 0:4, :] for c in CD], [c[:, 4:8, :] for c in CD]
        PB = Ring([take(512) for _ in range(PBN)])
        TMP = take(8, 128)
        OS = take(512)
        CT = take(4, 4, 4, 8)
        RD = take(4, 4)
        MX = take(8, 2)
        T1 = take(4, 128)
        CTT = T1.rearrange("p a b -> p (a b)")
        nst4 = take(4, 6)
        lst, lmv, ly, lv, ltmp = take(4, 6), take(4, 2), take(4), take(4), take(4)
        save = top[0]

        zt = memset("vector", ptb[:, 2, :, :], 0.0)
        SZ = 2 * SLOT
        t_scr = [Q.dma("sync", f"z{k}", bass.AP(scr.tensor, k * SLOT, [[SLOT // 128, 128], [1, SLOT // 128]]),
                       ptb[:, 2, :, :].rearrange("p a b -> p (a b)")[:, 0:SLOT // 128], zt) for k in range(2 * SLOTS)]
        t_cb = [memset("gpsimd", CD[k], 0.0) for k in range(3)]
        t_cb += [memset("vector", g, 0.0) for g in GG]
        t_va = [memset("gpsimd", VA[k], 1.0) for k in range(2)]
        t_pg0 = memset("gpsimd", PGO, 0.0)
        t_op = [ts("vector", OP[s_][x].rearrange("p a b -> p (a b)"), ptb[:, 2, :, :].rearrange("p a b -> p (a b)"),
                   pat[:, x:x + 1], None, ALU.add, None, zt, t_w) for s_ in range(2) for x in range(3)]
        RS = Ring([PS[:, k, :] for k in range(NRS)], t_z)
        R = Ring([PS[:, k, :] for k in range(NRS, 8)], t_z)

        def split(parts, x, tmp, e, t, before=None):
            t = cp("scalar", parts[:, 0], x, t)
            t = tt(e, tmp, x, parts[:, 0], ALU.subtract, t, before)
            t = cp("scalar", parts[:, 1], tmp, t)
            return tt(e, parts[:, 2], tmp, parts[:, 1], ALU.subtract, t)

        SC = float(1.0 / np.sqrt(np.float32(24.0)))
        t_cs = ts("vector", colb[:, 0:1], colb[:, 0:1], SC, None, ALU.mult, None, t_w)
        r, ps, free = R.take()
        t = M(ps[0:64, 0:128], relT, wk, True, True, free, t_w)
        t = tt("vector", posk, ps[0:64, 0:128], bkt, ALU.add, t)
        R.done(r, t)
        r, ps, free = R.take()
        M(ps[:, 0:256], posk, oh[:, 0:256], True, True, free, t)
        t = M(ps[:, 256:258], posk, oh[:, 256:258], True, True)
        cp("vector", PGF[:, 0:128], ps[:, 0:128], t)
        tp = ts("vector", PGF[:, 128:256], ps[:, 128:256], SC, None, ALU.mult, None, t)
        far = take(2)
        t = cp("vector", far, ps[:, 256:258], t)
        R.done(r, t)
        tz = memset("vector", SEL, 0.0)
        t_sel = [ts("vector", SEL[:, x, :, 2 * x + y], mask16, far[:, y:y + 1], None, ALU.mult, None, t, tz, t_w)
                 for x in range(2) for y in range(2)]
        t_sel.append(ts("vector", SEL[:, 1], SEL[:, 1], SC, None, ALU.mult, None, t_sel))
        t = split(PGS, PGF, PGR, "vector", tp)
        t = Q.dma("sync", "pgw", pgd, PGS, t)
        t_pg = []
        for k, order in enumerate(((0, 1, 2, 0, 1, 0), (0, 0, 0, 1, 1, 2))):
            for x, part in enumerate(order):
                src = bass.AP(pgd.tensor, part * 256 + k * 128, [[768, 8], [8 * 768, 16], [1, 128]])
                t_pg.append(Q.dma("sync", f"pg{k}{x}", PGO[8 * x:8 * x + 8, k], src, t, t_pg0))
        t_pos = t_pg + t_sel + [t_cs]
        top[0] = xf_at
        tn = norm_a(t_x)
        t_n = norm_b(tn, t_z, Q.last())
        top[0] = save
        t_cb += [memset("gpsimd", CD[k], 0.0, t_n) for k in range(3, NCD)]
        RS = Ring([PS[:, k, :] for k in range(NRS)], t_n)
        R = Ring([PS[:, k, :] for k in range(NRS, 8)], t_n)

        PTB.free = [Q.last() for _ in range(5)]

        st = {"opfree": [t_op, t_op], "op": {}, "g": {}, "c": {}, "d": {}, "rd": {}, "s": {}, "va": [[], []],
              "tv": {}, "cfree": [[] for _ in range(NCD)], "gfree": [[], [], []], "ofree": [t_n], "ctfree": [],
              "mx": [[] for _ in range(8)], "m": {}, "tmpfree": [], "qd": [[], []], "wrote": {}, "parts": [[], [], []],
              "xf": [], "xr": [], "t1free": []}

        def proj(b):
            xb = XT[:, b * SEQ:b * SEQ + SEQ]
            tx = []
            for k, w in enumerate((wq, wk)):
                r, ps, free = R.take()
                t = M(ps, w, xb, True, True, free, t_w, t_n)
                yield False
                t = act(XF[:, k, :], ps, ACT.Identity, t, st["xf"], t_cs, bias=colb[:, k:k + 1], scale=1.0 if k else SC)
                R.done(r, t)
                tx.append(t)
                yield True
            r, ps, free = R.take()
            M(ps[0:64, :], SEL[:, 0].rearrange("p a b -> p (a b)"), XF[:, 0, :], True, False, free, tx, t_pos)
            t = M(ps[0:64, :], SEL[:, 1].rearrange("p a b -> p (a b)"), XF[:, 1, :], False, True)
            yield False
            t = cp("scalar", XF[0:64, 2, :], ps[0:64, :], t, st["xf"])
            R.done(r, t)
            tx.append(t)
            yield False
            wrote = []
            s_ = b % 2
            for k in range(3):
                n = 64 if k == 2 else 128
                P, x, tmp = PARTS[k][0:n], XF[0:n, k, :], XR_[0:n]
                t = cp("scalar", P[:, 0], x, tx[k], st["parts"][k])
                yield False
                t = tt("vector", tmp, x, P[:, 0], ALU.subtract, t, st["xr"])
                yield False
                t = cp("scalar", P[:, 1], tmp, t)
                yield False
                t = tt("vector", P[:, 2], tmp, P[:, 1], ALU.subtract, t)
                st["xr"] = [t]
                base = s_ * QSZ + k * 16 * 48 * 512
                if k == 2:
                    w = [Q.dma("sync", f"qw2_{s_}", bass.AP(qsc.tensor, base, [[1536, 64], [1, 1536]]),
                               P.rearrange("p a b -> p (a b)"), t, st["qd"][s_])]
                else:
                    order = (0, 0, 0, 1, 1, 2) if k == 0 else (0, 1, 2, 0, 1, 0)
                    w = [Q.dma("sync", f"qw{k}{x}_{s_}",
                               bass.AP(qsc.tensor, base + x * 8 * 512, [[48 * 512, 16], [512, 8], [1, 512]]),
                               P[:, part, :], t, st["qd"][s_]) for x, part in enumerate(order)]
                st["parts"][k] = w
                wrote += w
            st["xf"] = [t]
            st["wrote"][b] = wrote
            st["qd"][s_] = []
            yield True
            r, ps, free = R.take()
            for q in range(4):
                i = b * 4 + q
                t = M(ps[:, q * 128:q * 128 + 128], XT[:, i * 128:i * 128 + 128], wv, True, True, free)
            yield False
            t = tt("vector", VA[b % 2][:, :, :, 0:8], ps.rearrange("p (q h d) -> p q h d", q=4, h=16),
                   bc(bvt.rearrange("p (h d) -> p h d", h=16).unsqueeze(1), [128, 4, 16, 8]), ALU.add, t, t_va,
                   st["va"][b % 2])
            R.done(r, t)
            st["tv"][b] = t

        def load_group(G):
            b, g = divmod(G, 4)
            s_, o = b % 2, OP[G % 2]
            fr = st["opfree"][G % 2]
            base = s_ * QSZ
            rows = lambda k: bass.AP(qsc.tensor, base + (k * 16 + 4 * g) * 48 * 512, [[512, 48], [48 * 512, 4], [1, 512]])
            far_ = base + 2 * 16 * 48 * 512 + 4 * g * 4 * 1536
            toks = [Q.dma("sync", f"o{G % 2}q", o[0][0:48], rows(0), st["wrote"][b], fr),
                    Q.dma("sync", f"o{G % 2}a", o[0][48:54], bass.AP(qsc.tensor, far_, [[512, 6], [6144, 4], [1, 512]]),
                          st["wrote"][b], fr)]
            for x in (1, 2):
                toks.append(Q.dma("sync", f"o{G % 2}k{x}", o[x][0:48], rows(1), st["wrote"][b], fr))
                src = bass.AP(qsc.tensor, far_ + (1 + x) * 1536, [[512, 3], [6144, 4], [1, 512]])
                toks.append(Q.dma("sync", f"o{G % 2}f{x}", o[x][54:57], src, st["wrote"][b], fr))
            st["op"][G] = toks
            st["qd"][s_] = st["qd"][s_] + toks

        def emit_g(n, x):
            G, hh = divmod(n, 4)
            r, ps, free = R.take()
            for q in range(4):
                t = M(ps[:, q * 128:q * 128 + 128], OP[G % 2][x][:, hh, q * 128:q * 128 + 128],
                      PGO[:, x, n % 16, :], True, True, free, st["op"][G], t_pos)
            later(1, lambda: g_out(n, x, r, ps, t))

        def g_out(n, x, r, ps, t):
            k = n % 3
            t = cp(G_OUT[x], GG[k][:, 4 * x:4 * x + 4, 0:128], ps.rearrange("p (a b) -> p a b", a=4), t, st["gfree"][k], t_cb)
            R.done(r, t)
            st["g"].setdefault(n, []).append(t)
            if x == 0:
                return
            s_ = n % SLOTS
            dst = bass.AP(scr.tensor, s_ * SZ + 129, [[PITCH, 128], [128 * PITCH, 8], [1, 128]])
            toks = st["g"][n]
            wr = Q.dma("sync", f"w{s_}", dst, GG[k][:, :, 1:129], toks, st["rd"].get(n - SLOTS, []), t_scr[2 * s_:2 * s_ + 2], t_cb)
            st["g"][n] = (toks, wr)

        def emit_r(n):
            s_, k = n % SLOTS, n % NCD
            toks, wr = st["g"][n]
            base = s_ * SZ + 128
            buf, G = CD[k], GG[n % 3]
            lo = bass.AP(scr.tensor, base, [[PITCH - 1, 64], [128 * PITCH, 8], [1, 192]])
            hi = bass.AP(scr.tensor, base + 64 * (PITCH - 1) + 64, [[PITCH - 1, 64], [128 * PITCH, 8], [1, 192]])
            r1 = Q.dma("sync", f"r{k}l", buf[0:64, :, 0:192], lo, wr, st["cfree"][k], t_cb)
            r2 = Q.dma("sync", f"r{k}h", buf[64:128, :, 64:256], hi, wr, st["cfree"][k], t_cb)
            t = tt("gpsimd", TMP.rearrange("p (x a) b -> p x a b", x=2), bc(tri.unsqueeze(2), [128, 2, 4, 128]),
                   bc(G[:, :, 0:1].rearrange("p (x a) b -> p x a b", x=2), [128, 2, 4, 128]), ALU.mult, toks, t_w, st["tmpfree"])
            st["gfree"][n % 3] = [t, wr]
            t = tt("gpsimd", buf[:, :, 64:192], buf[:, :, 64:192], TMP, ALU.add, t, r1, r2)
            st["tmpfree"] = [t]
            st["rd"][n] = [r1, r2]
            st["c"][n] = st["d"][n] = [t, r1, r2]

        def s_mm(v):
            n, ib = divmod(v, 4)
            G, hh = divmod(n, 4)
            k = n % NCD
            OQ, OL, OU = OP[G % 2]
            r, S, free = RS.take()
            q = OQ[:, hh, ib * 128:ib * 128 + 128]
            if ib:
                M(S[:, 0:128 * ib], q, OL[:, hh, 0:128 * ib], True, False, free)
            M(S[:, 128 * ib:512], q, OU[:, hh, 128 * ib:512], ib == 0, False, free)
            if ib:
                jb = ib - 1
                M(S[0:64, 128 * jb + 64:128 * jb + 128], DB[k][:, jb, 192:256], ident[:, 64:128],
                  False, False, st["d"][n])
            if ib < 3:
                jb = ib + 1
                M(S[64:128, 128 * jb:128 * jb + 64], DB[k][:, jb, 0:64], ident[:, 0:64], False, False,
                  st["d"][n])
            tS = M(S[:, 128 * ib:128 * ib + 128], DB[k][:, ib, 64:192], ident[:, :], False, True, st["d"][n])
            st["s"][v] = (r, S, tS)
            if ib == 3 and hh == 3:
                st["opfree"][G % 2] = [tS]

        def s_soft(v):
            n, ib = divmod(v, 4)
            k, m = n % NCD, v % 8
            r, S, tS = st["s"][v]
            lo, hi = max(0, 128 * ib - 64), min(512, 128 * ib + 192)
            o = 64 - 128 * ib
            t = tt("vector", S[:, lo:hi], S[:, lo:hi], CB[k][:, ib, lo + o:hi + o], ALU.add, tS, st["c"][n])
            if ib == 3:
                st["cfree"][k] = [t, tS]
            st["b", v] = t

        def s_max(v):
            r, S, tS = st["s"][v]
            m = v % 8
            st["m"][v] = minus_max(MX[:, m, 0:1], S, st["b", v], st["mx"][m])

        def s_exp(v):
            m = v % 8
            r, S, _ = st["s"][v]
            kp, P, fp = PB.take()
            te = act(P, S, ACT.Exp, st["m"][v], fp, bias=MX[:, m, 0:1])
            st["mx"][m] = [te]
            st["s"][v] = (te, kp, P)
            RS.done(r, te)

        def p_mm(v):
            te, kp, P = st["s"][v]
            r, ps, free = R.take()
            for jb in range(4):
                t = TR(ps[:, jb * 128:jb * 128 + 128], P[:, jb * 128:jb * 128 + 128], te, free)
            PB.done(kp, t)
            st["s"][v] = (r, ps, t)

        def p_out(v):
            n, ib = divmod(v, 4)
            if ib == 0:
                st["ptk", n] = PTB.take()
                st["pte", n] = []
            kb, PT, fpt = st["ptk", n]
            r, ps, t = st["s"].pop(v)
            t = cp("vector" if ib in VEC_PT else "scalar", PT[:, :, ib * 128:ib * 128 + 128],
                   ps.rearrange("p (a b) -> p a b", a=4), t, fpt)
            R.done(r, t)
            st["pte", n].append(t)
            if ib == 3 and n % 4 == 3:
                later(1, lambda: emit_pv(n // 16, n % 16 // 4))

        def emit_pv(b, g, jb=0, ro=None):
            ns = [b * 16 + g * 4 + hh for hh in range(4)]
            if jb == 0:
                ro = R.take()
            r, OB, fo = ro
            for hh in range(4):
                kb, PT, _ = st["ptk", ns[hh]]
                t = M(OB[32 * hh:32 * hh + 9, :], VA[b % 2][:, jb, g * 4 + hh, :], PT[:, jb, :], jb == 0, jb == 3,
                      st["pte", ns[hh]], st["tv"][b], fo)
            if jb < 3:
                later(1, lambda: emit_pv(b, g, jb + 1, ro))
                return
            for hh in range(4):
                PTB.done(st["ptk", ns[hh]][0], t)
            if g == 3:
                st["va"][b % 2] = [t]
            later(1, lambda: pv_out(b, g, r, OB, t))

        def pv_out(b, g, r, OB, t):
            t = cp("scalar", OS, OB, t, st["ofree"])
            R.done(r, t)
            later(1, lambda: heads(b, g, t))

        def heads(b, g, t):
            r, ps, free = R.take()
            for q in range(4):
                t2 = TR(ps[:, q * 128:q * 128 + 128], OS[:, q * 128:q * 128 + 128], t, free)
            st["ofree"] = [t2]
            later(1, lambda: heads_out(b, g, r, ps, t2))

        def heads_out(b, g, r, ps, t2):
            v = ps.rearrange("p (q h r) -> p q h r", q=4, h=4)
            t = rec(RD, v[:, :, :, 8], t2)
            t = tt("vector", CT[:, :, g, :, :], v[:, :, :, 0:8], bc(RD.unsqueeze(3), [128, 4, 4, 8]), ALU.mult, t,
                   st["ctfree"])
            R.done(r, t)
            if g == 3:
                later(1, lambda: tail(b, t))

        def tail(b, tc):
            r, ps, free = R.take()
            for q in range(4):
                t = TR(ps[:, q * 128:q * 128 + 128], CT[:, q, :, :, :].rearrange("p g h d -> p (g h d)"), tc, free)
            st["ctfree"] = [t]
            later(1, lambda: tail_ct(b, r, ps, t))

        def tail_ct(b, r, ps, t):
            t = cp("scalar", CTT, ps, t, st["t1free"])
            R.done(r, t)
            later(1, lambda: tail_mm(b, t))

        def tail_mm(b, t):
            r, ps, free = R.take()
            for q in range(4):
                o = ps[:, q * 128:q * 128 + 128]
                i = b * 4 + q
                M(o, CTT[:, q * 128:q * 128 + 128], wo, True, False, t, free)
                t1 = M(o, XT[:, i * 128:i * 128 + 128], ident[:, :], False, True)
            later(1, lambda: tail_out(b, r, ps, t1))

        def tail_out(b, r, ps, t1):
            t = tt("vector", T1, ps.rearrange("p (q c) -> p q c", q=4), bc(bot.unsqueeze(1), [128, 4, 128]), ALU.add, t1)
            R.done(r, t)
            r, ps, free = R.take()
            for q in range(4):
                i = b * 4 + q
                t2 = M(ps[:, q * 128:q * 128 + 128], XT[:, i * 128:i * 128 + 128], sw, True, True, free, t_sw)
            later(1, lambda: tail_sw(b, r, ps, t2, t))

        def tail_sw(b, r, ps, t2, t):
            xs = slice(b * 4, b * 4 + 4)
            tx = tt("vector", X[:, xs, :], ps.rearrange("p (q c) -> p q c", q=4), X[:, xs, :], ALU.add, t2)
            R.done(r, tx)
            later(1, lambda: tail_norm(b, t, tx))

        def tail_norm(b, t, tx):
            xs = slice(b * 4, b * 4 + 4)
            t = stats(T1, 4, 1e-7, lmv, lst, ly, lv, ltmp, t)
            later(1, lambda: tail_end(b, t, tx))

        def tail_end(b, t, tx):
            xs = slice(b * 4, b * 4 + 4)
            for q in range(4):
                t3 = ts("vector", T1[:, q, :], T1[:, q, :], lmv[:, q, 0:1], ly[:, q:q + 1], ALU.subtract, ALU.mult, t)
            t = tt("vector", T1, T1, bc(lnsc.unsqueeze(1), [128, 4, 128]), ALU.mult, t3)
            t = tt("vector", T1, T1, bc(lnb.unsqueeze(1), [128, 4, 128]), ALU.add, t)
            t = tt("vector", X[:, xs, :], X[:, xs, :], T1, ALU.add, t, tx)
            st["t1free"] = [t]
            later(1, lambda: next_stats(b, nst4, t))

        NBH = NB * NH
        G_OUT = ("vector", "scalar")
        R_AT = 2
        STAGES = ((s_exp, 3), (s_soft, 1), (s_max, 2), (p_out, 6), (s_mm, 0), (p_mm, 5))

        def step(v):
            n, ib = divmod(v, 4)
            for stage, lag in STAGES:
                if 0 <= v - lag < 4 * NBH:
                    stage(v - lag)
            run_later()

        for _ in proj(0):
            pass
        load_group(0)
        for n in range(3):
            for x in range(2):
                emit_g(n, x)
                run_later()
        run_later()
        emit_r(0)
        emit_r(1)
        for v in range(-1, 4 * NBH + 8):
            n, ib = divmod(v, 4)
            if ib == 0 and v >= 0 and n % 16 == 4 and n // 16 + 1 < NB:
                spread(proj(n // 16 + 1))
            if ib == 0 and v >= 0 and n % 4 == 0 and n // 4 + 1 < NBH // 4:
                load_group(n // 4 + 1)
            if ib == R_AT and 0 <= v and n + 2 < NBH:
                emit_r(n + 2)
            if ib in (0, 2) and v >= 0 and n + 3 < NBH:
                emit_g(n + 3, ib // 2)
            step(v)
        while todo:
            run_later()

        barrier()
        names = ["wz_f", "wh_f", "wz_b", "wh_b"]
        w1 = [take(128) for _ in names]
        c1 = take(4)
        wout, bout = take(2, 128), take(128)
        router = take(8)
        trile, iota, rev = take(128), take(64), take(8)
        wi, wo2 = take(8, 512), take(8, 4, 128)
        t_w = [load(w1[k], names[k]) for k in range(4)] + [load(c1, "l1_cols"), load(wout, "l1_wout"), load(bout, "l1_bout"),
               load(router, "router"), load(trile, "trile"), load(iota, "iota"), load(rev, "rev")]
        t_wi, t_wo2 = load(wi, "wi", e="scalar"), load(wo2, "wo2", e="scalar")
        ones128 = take(128)
        t_o = memset("gpsimd", ones128, 1.0)
        c1x = take(4)
        PRI, PROB = take(NT, 8), take(NT, 8)
        big = top[0]
        t_n = norm_top()
        top[0] = big
        R = Ring([PS[:, k, :] for k in range(8)], t_n)


        t_c = None
        for k in range(4):
            t_c = ts("vector", c1x[:, k:k + 1], c1[:, k:k + 1], 1.0 if k % 2 else -1.0, 0.5 if k % 2 else 0.0, ALU.mult,
                     ALU.add, t_w)
        L, L2, E1, E2, W_ = (take(NT, 8) for _ in range(5))
        m8, s8 = take(NT), take(NT)
        full = [128, NT, 8]
        col = lambda v: bc(v.unsqueeze(2), full)
        revb = bc(rev.unsqueeze(1), full)

        def first_max(dst, src, t):
            t = red(m8, src, ALU.max, t)
            t = tt("vector", W_, src, col(m8), ALU.is_equal, t)
            t = tt("vector", W_, W_, revb, ALU.mult, t)
            t = red(m8, W_, ALU.max, t)
            return tt("vector", dst, W_, col(m8), ALU.is_equal, t)

        def route():
            r, ps, free = R.take()
            for i in range(NT):
                t = M(ps[:, i * 8:i * 8 + 8], XT[:, i * 128:i * 128 + 128], router, True, True, free, t_w)
            yield False
            t = cp("vector", L.rearrange("p a b -> p (a b)"), ps[:, 0:256], t)
            R.done(r, t)
            tL = t
            t = red(m8, L, ALU.max, tL)
            t = tt("vector", PROB, L, col(m8), ALU.subtract, t)
            yield False
            t = act(PROB, PROB, ACT.Exp, t)
            yield False
            t = red(s8, PROB, ALU.add, t)
            t = rec(s8, s8, t)
            tP = tt("vector", PROB, PROB, col(s8), ALU.mult, t)

            yield False
            t1 = first_max(E1, L, tP)
            yield False
            t = stt(L2, E1, -3.0e38, L, ALU.mult, ALU.add, t1)
            t2 = first_max(E2, L2, t)
            yield True
            v1, v2 = (E.rearrange("p (b q) e -> p b q e", q=4) for E in (E1, E2))
            r, ps, free = R.take()
            for k, (E, v) in enumerate(((E1, v1), (E2, v2))):
                o = ps[:, 256 * k:256 * k + 256]
                ov = o.rearrange("p (b q e) -> p b q e", q=4, e=8)
                for q in range(4):
                    prev = [(v, j) for j in range(q)] + ([(v1, j) for j in range(4)] if k else [])
                    t = M(ov[:, :, q, :], trile, v[:, :, q, :], True, not prev, free, t1, t2, t_w)
                    for x, (pv, j) in enumerate(prev):
                        t = M(ov[:, :, q, :], ones128, pv[:, :, j, :], False, x == len(prev) - 1, t_o)
            yield False
            ps_v = ps.rearrange("p (k n e) -> p k n e", k=2, e=8)
            ta = tt("vector", E1, E1, ps_v[:, 0], ALU.mult, t)
            tb = tt("vector", E2, E2, ps_v[:, 1], ALU.mult, t)
            R.done(r, tb)
            t = tt("vector", PRI, E1, E2, ALU.max, ta, tb)
            ts("vector", PRI, PRI, -1.0, None, ALU.add, None, t)

        A_ = Ring([take(512) for _ in range(3)])
        Z_ = Ring([take(512) for _ in range(3)])
        G_ = Ring([take(512) for _ in range(3)])
        H_ = Ring([take(512) for _ in range(4)])

        def scan_unit(b, d):
            toks = []
            for k in range(2):
                r, ps, free = R.take()
                t = M(ps, w1[2 * d + k], XT[:, b * SEQ:b * SEQ + SEQ], True, True, free, t_w)
                toks.append((r, ps, t))
            (r0, p0, tz), (r1, p1, th) = toks
            ka, A, fa = A_.take()
            kz, Z, fz = Z_.take()
            kg, G, fg = G_.take()
            kh, H, fh = H_.take()
            t_a = act(A, p0, ACT.Sigmoid, tz, fa, t_c, bias=c1x[:, 2 * d:2 * d + 1], scale=-1.0)
            t_z = act(Z, p0, ACT.Sigmoid, fz, bias=c1[:, 2 * d:2 * d + 1])
            R.done(r0, t_z)
            t_g = act(G, p1, ACT.Sigmoid, th, fg, bias=c1[:, 2 * d + 1:2 * d + 2])
            t = stt(G, p1, c1x[:, 2 * d + 1:2 * d + 2], G, ALU.add, ALU.max, t_g)
            R.done(r1, t)
            t = tt("gpsimd", G, G, Z, ALU.mult, t, t_z)
            Z_.done(kz, t)
            rv = slice(None, None, -1) if d else slice(None)
            t = Q.op("vector", lambda g: g.tensor_tensor_scan(H, A[:, rv], G[:, rv], 0.0, ALU.mult, ALU.add), t, t_a, fh)
            A_.done(ka, t)
            G_.done(kg, t)
            return kh, H, t

        def scan_out(b, hs):
            r, ps, free = R.take()
            for q in range(4):
                o = ps[:, q * 128:q * 128 + 128]
                sl = slice(q * 128, q * 128 + 128)
                M(o, hs[0][1][:, sl], wout[:, 0, :], True, False, hs[0][2], free)
                t = M(o, hs[1][1][:, sl], wout[:, 1, :], False, True, hs[1][2])
            for kh, _, _ in hs[:2]:
                H_.done(kh, t)
            xs = slice(b * 4, b * 4 + 4)
            t = tt("vector", X[:, xs, :], X[:, xs, :], ps.rearrange("p (q c) -> p q c", q=4), ALU.add, t, hs[2])
            R.done(r, t)
            return t
        hs = None
        tX = []
        for b in range(NB):
            xb = X[:, b * 4:b * 4 + 4, :]
            tb = tt("gpsimd", xb, xb, bc(bout.unsqueeze(1), [128, 4, 128]), ALU.add, t_w, t_n)
            if b == 0:
                spread(route())
            cur = [scan_unit(b, 0)]
            run_later()
            cur += [scan_unit(b, 1), tb]
            run_later()
            if b:
                tX.append(scan_out(b - 1, hs))
            hs = cur
        tX.append(scan_out(NB - 1, hs))
        while todo:
            run_later()

        for e in ("vector", "gpsimd", "scalar"):
            Q._waits(e, Q.last())
        top[0] = big
        XIN = take(8, 8, 64)
        EO = take(4, 8, 128)
        HT = Ring([take(4, 512) for _ in range(2)])
        DD = Ring([take(8, 64) for _ in range(5)])
        DR = Ring([take(8, 64) for _ in range(3)])
        XL = take(NT, 128)
        for_halves(*DR.bufs, XL, XT[:, :])
        XH = XT[:, :].rearrange("p (a b) -> p a b", b=128)
        iob = bc(iota.unsqueeze(1), [128, 8, 64])
        t_in = []
        for g in range(8):
            r, ps, free = R.take()
            for q in range(4):
                i = g * 4 + q
                kd, D, fd = DR.take()
                th = act(f32r(XH[:, i, :]), XN[:, i, :], ACT.Copy)
                tl = tt("gpsimd", f32r(XL[:, i, :]), XN[:, i, :], f32v(XH[:, i, :]), ALU.subtract, th)
                t = tt("vector", f32r(D), iob, bc(PRI[:, i, :].unsqueeze(2), [128, 8, 64]), ALU.is_equal, fd)
                Df = f32r(D.rearrange("p a b -> p (a b)"))
                M(ps, f32r(XH[:, i, :]), Df, q == 0, False, t, th, free)
                t = M(ps, f32r(XL[:, i, :]), Df, False, q == 3, tl)
                DR.done(kd, t)
            t = cp("scalar", XIN[:, :, g, :], ps.rearrange("p (e c) -> p e c", e=8), t)
            R.done(r, t)
            t_in.append(t)
        t_eo = []
        R1 = Ring([PS[:, k, :] for k in range(4)], Q.last())
        R2 = Ring([PS[:, 4:6, :], PS[:, 6:8, :]], Q.last())

        def down(e, kh, H, toks):
            r, ps, free = R2.take()
            rows = slice(64 * (e % 2), 64 * (e % 2) + 64)
            pv = ps.rearrange("p k (g c) -> p (k g) c", c=128)
            for g, f in [(g + x, f) for g in range(4) for f in range(4) for x in (0, 4)]:
                t = M(pv[rows, g, :], H[:, f, g * 64:g * 64 + 64], wo2[:, e, f, :], f == 0, f == 3, toks, free, t_wo2)
            HT.done(kh, t)
            t = cp("vector", EO[rows, e // 2, :, :], pv[rows, :, :], t)
            R2.done(r, t)
            t_eo.append(t)
        prev = None
        for e in range(8):
            kh, H, fh = HT.take()
            toks = []
            for f in range(4):
                r, ps, free = R1.take()
                t = M(ps, wi[:, e, f * 128:f * 128 + 128], XIN[:, e, :, :].rearrange("p g c -> p (g c)"), True, True,
                      t_in, free, t_wi)
                t = act(H[:, f, :], ps, ACT.Gelu_apprx_tanh, t, fh)
                R1.done(r, t)
                toks.append(t)
            if prev:
                down(*prev)
            prev = (e, kh, H, toks)
        down(*prev)
        R = Ring([PS[:, k, :] for k in range(8)], Q.last())
        CTB = Ring([take(4, 128) for _ in range(4)])
        st = {}

        def comb_d(i):
            kd, D, fd = DD.take()
            toks = []
            for e in range(8):
                toks.append(ts("gpsimd" if e in (1, 5) else "vector", D[:, e, :], iota, PRI[:, i, e:e + 1], PROB[:, i, e:e + 1],
                               ALU.is_equal, ALU.mult, fd))
            st["d", i] = kd, D, toks

        def comb_t(i):
            kd, D, toks = st["d", i]
            r, ps, free = R.take()
            Df = D.rearrange("p a b -> p (a b)")
            for c in range(4):
                t = TR(ps[:, c * 128:c * 128 + 128], Df[:, c * 128:c * 128 + 128], toks, free)
            DD.done(kd, t)
            st["t", i] = r, ps, t

        def comb_c(i):
            r, ps, t = st["t", i]
            kc, CB_, fc = CTB.take()
            t = cp("scalar", CB_, ps.rearrange("p (a b) -> p a b", a=4), t, fc)
            R.done(r, t)
            st["c", i] = kc, CB_, t

        def comb_m(i):
            if i % 2 == 0:
                return
            both = [(x, st["c", x], R.take()) for x in (i - 1, i)]
            for c in range(4):
                for x, (kc, CB_, tc), (r, ps, free) in both:
                    t = M(ps[:, 0:128], CB_[:, c, :], EO[:, c, x // 4, :], c == 0, c == 3, tc, t_eo, free)
                    st["m", x] = r, ps, t
            for x, (kc, _, _), _ in both:
                CTB.done(kc, t)

        def comb_x(i):
            r, ps, t = st["m", i]
            t = tt("vector", X[:, i, :], X[:, i, :], ps[:, 0:128], ALU.add, t)
            R.done(r, t)
        for u in range(NT + 5):
            for stage, lag in ((comb_x, 5), (comb_m, 3), (comb_c, 2), (comb_t, 1), (comb_d, 0)):
                if 0 <= u - lag < NT:
                    stage(u - lag)

        barrier()
        w3, mu, mu1, BO = take(3, 128), take(2), take(2), take(128)
        MH = [take(8, 512) for _ in range(2)]
        VW = [take(4, 8, 128) for _ in range(2)]
        XH, XL = XN[:, :, :].rearrange("p a b -> p (a b)"), take(4096)
        for_halves(*MH, *VW, XH, XL)
        base = top[0]
        ctxT = take(512, rows=96)
        wkT, wvT, wqT, wout2 = take(8, 96), take(8, 96), take(8, 128), take(8, 128)
        t_w = [load(ctxT, "ctxT"), load(wkT, "l2_wkT"), load(wqT, "l2_wqT", e="scalar"), load(wvT, "l2_wvT"),
               load(wout2, "l2_wout", e="scalar"), load(BO, "l2_bout"), load(w3, "l2_w"), load(mu, "l2_mu")]
        C = 1.5 * 128 ** -0.5
        GU = [take(1024, rows=96) for _ in range(2)]
        tn = norm_a(pool=(1, 3, 5, 7))
        R = Ring([PS[:, k, :] for k in range(8)])
        t_gu = [[], []]
        for kind, (w, u) in enumerate(((wkT, wqT), (wvT, wout2))):
            for g in range(2):
                r, ps, free = R.take()
                for x in range(4):
                    t = M(ps[0:96, x * 128:x * 128 + 128], w[:, 4 * g + x, :], u[:, 4 * g + x, :], True, True, free, t_w)
                t = act(GU[kind][:, g * 512:g * 512 + 512], ps[0:96, :], ACT.Copy, t, scale=1.0 if kind else C)
                R.done(r, t)
                t_gu[kind].append(t)
        t_v = []
        for h in range(8):
            r, ps, free = R.take()
            t = M(ps, GU[0][:, h * 128:h * 128 + 128], ctxT, True, True, free, t_gu[0], t_w)
            t_v.append(halves(MH[0][:, h, :], MH[1][:, h, :], ps, t))
            R.done(r, *t_v[-1])
            r, ps, free = R.take()
            j, g = divmod(h, 2)
            t = M(ps, ctxT[:, j * 128:j * 128 + 128], GU[1][:, g * 512:g * 512 + 512], True, True, free, t_gu[1], t_w)
            dst = [v[:, j, 4 * g:4 * g + 4, :].rearrange("p h c -> p (h c)") for v in VW]
            t_v.append(halves(dst[0], dst[1], ps, t))
            R.done(r, *t_v[-1])
        t_mu = ts("vector", mu1, mu, -1.0, 1.0, ALU.mult, ALU.add, t_w)
        t_n = norm_b(tn, Q.last())
        xp = []
        for b in range(NB):
            sl = slice(b * 512, b * 512 + 512)
            xp.append(halves(XH[:, sl], XL[:, sl], XT[:, sl], t_n[b], t_n[b]))
        for e in ("vector", "scalar", "gpsimd"):
            Q._waits(e, Q.last())
        top[0] = base
        RS = Ring([PS[:, k, :] for k in range(3)], Q.last())
        R = Ring([PS[:, k, :] for k in range(3, 8)], Q.last())
        PT = Ring([[take(4, 512), take(4, 512)] for _ in range(3)])
        for_halves(*[p for k in PT.bufs for p in k])
        PB = Ring([take(512) for _ in range(4)])
        XR, XK, KA, RG = (take(512) for _ in range(4))
        OT = take(512)
        MX, DN = take(8), take(8)
        nst4 = take(4, 6)
        st = {"f": [], "ot": []}
        XTb = XT[:, :].rearrange("p (b t) -> p b t", b=NB)

        def ffn(b):
            toks = []
            for k, dst in enumerate((XR, XK)):
                t0 = memset("gpsimd", dst[:, 0:1], 0.0, st["f"])
                t = act(dst[:, 1:], XTb[:, b, 0:SEQ - 1], ACT.Copy, t_n, t_mu, st["f"], scale=mu1[:, k:k + 1])
                toks.append(stt(dst, XTb[:, b, :], mu[:, k:k + 1], dst, ALU.mult, ALU.add, t, t0))
            later(1, lambda: ffn_k(b, toks))

        def ffn_k(b, toks):
            r, ps, free = R.take()
            t = M(ps, w3[:, 1, :], XK, True, True, toks[1], free)
            later(1, lambda: ffn_k2(b, toks, r, ps, t))

        def ffn_k2(b, toks, r, ps, t):
            t = ts("vector", KA, ps, 0.0, None, ALU.max, None, t, st["f"])
            R.done(r, t)
            t = tt("gpsimd", KA, KA, KA, ALU.mult, t)
            r, ps, free = R.take()
            for q in range(4):
                sl = slice(q * 128, q * 128 + 128)
                t2 = M(ps[:, sl], XR[:, sl], w3[:, 0, :], True, True, toks[0], free)
            later(1, lambda: ffn_r(b, t, r, ps, t2))

        def ffn_r(b, tk, r, ps, t):
            t = ts("vector", RG, ps, -87.0, None, ALU.max, None, t, st["f"])
            R.done(r, t)
            t = act(RG, RG, ACT.Exp, t, scale=-1.0)
            t = ts("vector", RG, RG, 1.0, None, ALU.add, None, t)
            tg = rec(RG, RG, t)
            r, ps, free = R.take()
            for q in range(4):
                sl = slice(q * 128, q * 128 + 128)
                t = M(ps[:, sl], KA[:, sl], w3[:, 2, :], True, True, tk, free)
            later(1, lambda: ffn_out(b, tg, r, ps, t))

        def ffn_out(b, tg, r, ps, t):
            t = tt("vector", RG, RG, ps, ALU.mult, t, tg)
            R.done(r, t)
            xs = slice(b * 4, b * 4 + 4)
            t_x = tt("gpsimd", X[:, xs, :], X[:, xs, :], bc(BO.unsqueeze(1), [128, 4, 128]), ALU.add, t_w, tn)
            st["f"] = [tt("gpsimd", X[:, xs, :], X[:, xs, :], RG.rearrange("p (q c) -> p q c", q=4), ALU.add, t, t_x)]
            st["fx", b] = st["f"]

        def s_mm(v):
            bh, q = divmod(v, 4)
            b, h = divmod(bh, 8)
            i = 4 * b + q
            r, S, free = RS.take()
            sl = slice(i * 128, i * 128 + 128)
            t = M3(S, (XH[:, sl], XL[:, sl]), (MH[0][:, h, :], MH[1][:, h, :]), True, True, free, t_v, xp[b])
            st["s", v] = (r, S, t)

        def s_soft(v):
            r, S, t = st["s", v]
            m = v % 8
            st["m", v] = minus_max(MX[:, m:m + 1], S, t, st.get(("e", v - 8)))

        def s_exp(v):
            r, S, _ = st["s", v]
            m = v % 8
            kp, P, fp = PB.take()
            te = act(P, S, ACT.Exp, st["m", v], fp, st.get(("d", v - 8)), bias=MX[:, m:m + 1], accum=DN[:, m:m + 1])
            RS.done(r, te)
            st["e", v] = te
            st["p", v] = (kp, P)

        def s_rec(v):
            m = v % 8
            st["r", v] = rec(DN[:, m:m + 1], DN[:, m:m + 1], st["e", v])

        def s_norm(v):
            kp, P = st["p", v]
            m = v % 8
            st["d", v] = ts("gpsimd" if v % 2 else "vector", P, P, DN[:, m:m + 1], None, ALU.mult, None, st["r", v])

        def p_mm(v):
            kp, P = st["p", v]
            r, ps, free = R.take()
            for jb in range(4):
                t = TR(ps[:, jb * 128:jb * 128 + 128], P[:, jb * 128:jb * 128 + 128], st["d", v], free)
            PB.done(kp, t)
            st["t", v] = (r, ps, t)

        def p_hi(v):
            bh, q = divmod(v, 4)
            if q == 0:
                st["pt", bh] = PT.take()
                st["ptt", bh] = []
            k, (PH, PL), free = st["pt", bh]
            r, ps, t = st["t", v]
            sl = slice(q * 128, q * 128 + 128)
            st["h", v] = act(f32r(PH[:, :, sl]), ps.rearrange("p (a b) -> p a b", a=4), ACT.Copy, t, free)

        def p_lo(v):
            bh, q = divmod(v, 4)
            k, (PH, PL), free = st["pt", bh]
            r, ps, t = st["t", v]
            sl = slice(q * 128, q * 128 + 128)
            t2 = tt("vector", f32r(PL[:, :, sl]), ps.rearrange("p (a b) -> p a b", a=4), f32v(PH[:, :, sl]), ALU.subtract, t,
                    st["h", v], free)
            R.done(r, t2)
            st["ptt", bh].append(t2)
            if q == 3:
                later(1, lambda: pv(bh, 0))

        def pv(bh, j):
            b, h = divmod(bh, 8)
            if h == 0 and j == 0:
                st["o", b] = R.take()
            r, O, free = st["o", b]
            k, (PH, PL), _ = st["pt", bh]
            t = M3(O, (VW[0][:, j, h, :], VW[1][:, j, h, :]), (PH[:, j, :], PL[:, j, :]), h == 0 and j == 0,
                   h == 7 and j == 3, st["ptt", bh], t_v, free)
            if j < 3:
                later(1, lambda: pv(bh, j + 1))
                return
            PT.done(k, t)
            if h == 7:
                later(1, lambda: o_copy(b, r, O, t))

        def o_copy(b, r, O, t):
            t = cp("scalar", OT, O, t, st["ot"])
            R.done(r, t)
            later(1, lambda: o_tr(b, t))

        def o_tr(b, t):
            r, ps, free = R.take()
            for q in range(4):
                t2 = TR(ps[:, q * 128:q * 128 + 128], OT[:, q * 128:q * 128 + 128], t, free)
            st["ot"] = [t2]
            later(1, lambda: o_out(b, r, ps, t2))

        def o_out(b, r, ps, t):
            xs = slice(b * 4, b * 4 + 4)
            t = tt("vector", X[:, xs, :], X[:, xs, :], ps.rearrange("p (q c) -> p q c", q=4), ALU.add, t, st["fx", b])
            R.done(r, t)
            later(1, lambda: next_stats(b, nst4, t))

        NV = NT * 8
        for v in range(NV + 7):
            if v % 32 == 2 and v < NV:
                ffn(v // 32)
            for stage, lag in ((p_lo, 7), (p_hi, 6), (s_exp, 2), (s_soft, 1), (s_rec, 3), (s_norm, 4), (p_mm, 5), (s_mm, 0)):
                if 0 <= v - lag < NV:
                    stage(v - lag)
            run_later()
        while todo:
            run_later()

        barrier()
        cols3, fb, sls = take(3), take(16, 2, 2), take(1)
        SEH, SEL3 = take(1024), take(1024)
        XL, XNH = take(4096), take(NT, 128)
        for_halves(SEH, SEL3, XL, XNH, XN[:, :, :], XT[:, :])
        SLT = take(16, NB, 64)
        base = top[0]
        wqkv, rows3 = take(384), take(384)
        gb, ab, pw, bdm = take(2, 256), take(128), take(2, 128), take(128)
        ng, nb_, sg, sbb = take(128), take(128), take(128), take(128)
        SE = take(8, 128)
        t_w = [load(wqkv, "l3_qkv"), load(rows3, "l3_rows"), load(cols3, "l3_cols"), load(gb, "l3_gb", e="scalar"),
               load(ab, "l3_ab"), load(pw, "l3_p"), load(bdm, "bdmask", e="scalar"), load(ng, "l3_ng"), load(nb_, "l3_nb"),
               load(sg, "l3_sg"), load(sbb, "l3_sb"), load(sls, "l3_scale"), load(fb, "l3_fb", e="scalar"),
               load(SE, "slots", e="scalar")]
        save = top[0]
        tn = norm_a()
        t_n = norm_b(tn)
        RS = Ring([PS[:, k, :] for k in range(2)], t_n)
        R = Ring([PS[:, k, :] for k in range(2, 8)], t_n)
        top[0] = save
        for e in ("vector", "scalar", "gpsimd"):
            Q._waits(e, tn)
        QT = Ring([take(512) for _ in range(3)])
        KV = Ring([take(4, 256) for _ in range(2)])
        SQ = Ring([take(4, 256)])
        SM = Ring([take(4, 128) for _ in range(2)])
        KVM = Ring([take(128)])
        nst, nmv, ny, nv_, ntm = take(8, 6), take(8, 2), take(8), take(8), take(8)
        t_tc = ts("vector", cols3[:, 2:3], cols3[:, 2:3], 1.0 / 512, None, ALU.mult, None, t_w)

        st = {"n": []}
        t_se = []

        def slots_in():
            ts_ = [Q.op("vector", lambda g, i=i: g.bn_stats(nst[:, i, :], SE[:, i, :]), t_w) for i in range(8)]
            for i in range(8):
                t = Q.op("vector", lambda g, i=i: g.bn_aggr(nmv[:, i, :], nst[:, i, :]), ts_[i])
            t = ts("vector", nv_, nmv[:, :, 1], 1e-5, None, ALU.add, None, t)
            yield False
            t = act(ntm, nv_, ACT.Sqrt, t)
            yield False
            t = newton(ny, nv_, ntm, t)
            for i in range(8):
                t2 = ts("vector", SE[:, i, :], SE[:, i, :], nmv[:, i, 0:1], ny[:, i:i + 1], ALU.subtract, ALU.mult, t)
            st["n"] = [t2]
            yield False
            t = tt("vector", SE, SE, bc(sg.unsqueeze(1), [128, 8, 128]), ALU.mult, t2)
            t = tt("vector", SE, SE, bc(sbb.unsqueeze(1), [128, 8, 128]), ALU.add, t)
            t = ts("vector", SE, SE, sls, None, ALU.mult, None, t)
            for k in range(2):
                yield True
                r, ps, free = R.take()
                for j in range(4):
                    tr = TR(ps[:, j * 128:j * 128 + 128], SE[:, 4 * k + j, :], t, free)
                yield False
                sl = slice(k * 512, k * 512 + 512)
                t_se.append(halves(SEH[:, sl], SEL3[:, sl], ps, tr))
                R.done(r, *t_se[-1])

        def front(b):
            sl, xs = slice(b * SEQ, b * SEQ + SEQ), slice(b * 4, b * 4 + 4)
            r, ps, free = R.take()
            t = M(ps, wqkv[:, 0:128], XT[:, sl], True, True, free, t_w, t_n[b])
            t_x = tt("gpsimd", X[:, xs, :], X[:, xs, :], XN[:, xs, :], ALU.add, tn)
            t_x = tt("gpsimd", X[:, xs, :], X[:, xs, :], bc(rows3[:, 256:384].unsqueeze(1), [128, 4, 128]), ALU.add, t_w, t_x)
            yield True
            kq, QT_, f = QT.take()
            tq = act(QT_, ps, ACT.Identity, t, f, bias=cols3[:, 0:1])
            R.done(r, tq)
            kk, KV_, f = KV.take()
            for x in range(2):
                r, ps, free = R.take()
                for y in range(2):
                    i = b * 4 + 2 * x + y
                    t = M(ps[:, y * 256:y * 256 + 256], XT[:, i * 128:i * 128 + 128], wqkv[:, 128:384], True, True, free)
                yield True
                t = tt("vector", KV_[:, 2 * x:2 * x + 2, :], ps.rearrange("p (y c) -> p y c", y=2),
                       bc(rows3[:, 0:256].unsqueeze(1), [128, 2, 256]), ALU.add, t, f)
                R.done(r, t)
            v = KV_.rearrange("p q (h d) -> p (q h) d", d=8)
            km, SM_, f = SM.take()
            s1, v1, tm, y1 = (SM_[:, k, :] for k in range(4))
            wide = lambda z: bc(z.unsqueeze(2), [128, 128, 8])
            t = red(s1, v, ALU.add, t, f)
            t = ts("vector", s1, s1, 0.125, None, ALU.mult, None, t)
            yield
            tc_ = tt("gpsimd", v, v, wide(s1), ALU.subtract, t)
            yield
            yield
            ks, SQ_, fs = SQ.take()
            t = act(SQ_, KV_, ACT.Square, tc_, fs)
            yield
            t = red(v1, SQ_.rearrange("p q (h d) -> p (q h) d", d=8), ALU.add, t)
            SQ.done(ks, t)
            t = ts("vector", v1, v1, 0.125, 1e-5, ALU.mult, ALU.add, t)
            yield
            t = act(tm, v1, ACT.Sqrt, t)
            yield
            t = newton(y1, v1, tm, t)
            t = tt("vector", v, v, wide(y1), ALU.mult, t, tc_)
            SM.done(km, t)
            yield
            t = tt("gpsimd", KV_, KV_, bc(gb[:, 0, :].unsqueeze(1), [128, 4, 256]), ALU.mult, t, t_w)
            yield
            t = tt("gpsimd", KV_, KV_, bc(gb[:, 1, :].unsqueeze(1), [128, 4, 256]), ALU.add, t)
            yield
            yield True
            r, ps, free = R.take()
            for q in range(4):
                t = M(ps[:, 0:128], KV_[:, q, 0:128], KV_[:, q, 128:256], q == 0, q == 3, t, free)
            KV.done(kk, t)
            yield
            km, KM, f = KVM.take()
            t = stt(KM, ps[:, 0:128], cols3[:, 2:3], bdm, ALU.mult, ALU.mult, t, t_tc, f)
            R.done(r, t)
            t = tt("vector", KM, KM, ab, ALU.add, t)
            yield True
            r, ps, free = R.take()
            tm_ = M(ps, KM, QT_, True, True, t, tq, free)
            KVM.done(km, tm_)
            yield
            ta = tt("vector", QT_, ps, XT[:, sl], ALU.add, tm_)
            R.done(r, ta)
            yield True
            r, ps, free = R.take()
            tp = M(ps, pw[:, 0, :], QT_, True, True, ta, free)
            yield
            ks, SQ_, fs = SQ.take()
            H = SQ_.rearrange("p a b -> p (a b)")[:, 0:512]
            t = act(H, ps, ACT.Gelu, tp, fs, bias=cols3[:, 1:2])
            QT.done(kq, tp, t)
            R.done(r, t)
            yield True
            r, ps, free = R.take()
            for q in range(4):
                t2 = M(ps[:, q * 128:q * 128 + 128], H[:, q * 128:q * 128 + 128], pw[:, 1, :], True, True, t, free)
            SQ.done(ks, t2)
            yield
            t = tt("vector", X[:, xs, :], X[:, xs, :], ps.rearrange("p (q c) -> p q c", q=4), ALU.add, t2, t_x)
            R.done(r, t)
            src = XN[:, xs, :]
            t = stats4(src, st["n"])
            yield
            t = act(ntm[:, 0:4], nv_[:, 0:4], ACT.Sqrt, t)
            yield
            t = newton(ny[:, 0:4], nv_[:, 0:4], ntm[:, 0:4], t)
            for q in range(4):
                t2 = ts("vector", src[:, q, :], src[:, q, :], nmv[:, q, 0:1], ny[:, q:q + 1], ALU.subtract, ALU.mult, t, t_x)
            st["n"] = [t2]
            yield
            t = tt("gpsimd", src, src, bc(ng.unsqueeze(1), [128, 4, 128]), ALU.mult, t2, t_w)
            t = tt("gpsimd", src, src, bc(nb_.unsqueeze(1), [128, 4, 128]), ALU.add, t)
            yield
            yield True
            r, ps, free = R.take()
            for q in range(4):
                tr = TR(ps[:, q * 128:q * 128 + 128], src[:, q, :], t, free)
            yield
            tx = halves(XT[:, sl], XL[:, sl], ps, tr, ta)
            R.done(r, *tx)
            yield
            t1 = act(f32r(XNH[:, xs, :]), src, ACT.Copy, t)
            t2 = tt("gpsimd", f32r(src), src, f32v(XNH[:, xs, :]), ALU.subtract, t1, tr)
            st["x", b] = tx + [t1, t2]

        def stats4(src, *w):
            ts_ = [Q.op("vector", lambda g, i=i: g.bn_stats(nst[:, i, :], src[:, i, :]), *w) for i in range(4)]
            for i in range(4):
                t = Q.op("vector", lambda g, i=i: g.bn_aggr(nmv[:, i, :], nst[:, i, :]), ts_[i])
            return ts("vector", nv_[:, 0:4], nmv[:, 0:4, 1], 1e-5, None, ALU.add, None, t)

        PT = Ring([[take(4, 512), take(4, 512)] for _ in range(2)])
        for_halves(*[p for k in PT.bufs for p in k])
        PB = Ring([take(512) for _ in range(4)])
        MX, DN = take(8), take(8)

        def s_mm(v):
            b, p = divmod(v, 8)
            r, S, free = RS.take()
            sl, sp = slice(b * SEQ, b * SEQ + SEQ), slice(p * 128, p * 128 + 128)
            t = M3(S, (SEH[:, sp], SEL3[:, sp]), (XT[:, sl], XL[:, sl]), True, True, free, t_se, st["x", b])
            st["s", v] = (r, S, t)

        def s_soft(v):
            r, S, t = st["s", v]
            m = v % 8
            st["m", v] = minus_max(MX[:, m:m + 1], S, t, st.get(("e", v - 8)))

        def s_exp(v):
            r, S, _ = st["s", v]
            m = v % 8
            kp, P, fp = PB.take()
            te = act(P, S, ACT.Exp, st["m", v], fp, st.get(("d", v - 8)), bias=MX[:, m:m + 1], accum=DN[:, m:m + 1])
            RS.done(r, te)
            st["e", v] = te
            st["p", v] = (kp, P)

        def s_rec(v):
            m = v % 8
            st["r", v] = rec(DN[:, m:m + 1], DN[:, m:m + 1], st["e", v])

        def s_norm(v):
            kp, P = st["p", v]
            m = v % 8
            st["d", v] = ts("gpsimd" if v % 4 == 1 else "vector", P, P, DN[:, m:m + 1], None, ALU.mult, None, st["r", v])

        def p_mm(v):
            kp, P = st["p", v]
            r, ps, free = R.take()
            for jb in range(4):
                t = TR(ps[:, jb * 128:jb * 128 + 128], P[:, jb * 128:jb * 128 + 128], st.get(("d", v), st["e", v]), free)
            PB.done(kp, t)
            st["t", v] = (r, ps, t)

        def p_hi(v):
            g, q = divmod(v, 4)
            if q == 0:
                st["pt", g] = PT.take()
                st["ptt", g] = []
            k, (PH, PL), free = st["pt", g]
            r, ps, t = st["t", v]
            sl = slice(q * 128, q * 128 + 128)
            st["h", v] = act(f32r(PH[:, :, sl]), ps.rearrange("p (a b) -> p a b", a=4), ACT.Copy, t, free)

        def p_lo(v):
            g, q = divmod(v, 4)
            k, (PH, PL), free = st["pt", g]
            r, ps, t = st["t", v]
            sl = slice(q * 128, q * 128 + 128)
            t2 = tt("vector", f32r(PL[:, :, sl]), ps.rearrange("p (a b) -> p a b", a=4), f32v(PH[:, :, sl]), ALU.subtract, t,
                    st["h", v], free)
            R.done(r, t2)
            st["ptt", g].append(t2)
            if q == 3:
                later(0, lambda: pv(g, 0))

        def pv(g, j):
            b, half = divmod(g, 2)
            if j == 0:
                st["o", g] = R.take()
            r, O, free = st["o", g]
            k, (PH, PL), _ = st["pt", g]
            i = 4 * b + j
            t = M3(O, (XNH[:, i, :], XN[:, i, :]), (PH[:, j, :], PL[:, j, :]), j == 0, j == 3, st["ptt", g], st["x", b], free)
            if j < 3:
                later(1, lambda: pv(g, j + 1))
                return
            PT.done(k, t)
            later(1, lambda: slots_out(b, half, r, O, t))

        def slots_out(b, half, r, O, t):
            t = cp("scalar", SLT[:, 8 * half:8 * half + 8, b, :], O.rearrange("p (e s) -> p e s", e=8), t)
            R.done(r, t)

        LEAD, NV = 33, 8 * NB
        for u in range(LEAD + NV + 7):
            if u % 8 == 0 and u // 8 < NB:
                spread(front(u // 8))
            if u == 2:
                spread(slots_in())
            v = u - LEAD
            for stage, lag in ((p_lo, 7), (p_hi, 6), (s_exp, 2), (s_soft, 1), (s_rec, 3), (s_norm, 4), (p_mm, 5), (s_mm, 0)):
                if 0 <= v - lag < NV:
                    stage(v - lag)
            run_later()
        while todo:
            run_later()

        for e in ("vector", "scalar", "gpsimd", "tensor", "sync"):
            Q._waits(e, Q.last())
        top[0] = base
        EO = take(8, NB, 128)
        for_halves(EO)
        bd = take(8, 128)
        base = top[0]
        EOH = [XN[:, :, :].rearrange("p (k b) c -> p k b c", k=4), XNH.rearrange("p (k b) c -> p k b c", k=4)]
        t_bd = load(bd, "l3_bd", Q.last())
        WG = Ring([take(2, 256) for _ in range(3)])
        WD = Ring([take(2, 128) for _ in range(3)])
        GB = Ring([take(2, 512) for _ in range(2)])
        HV = Ring([[take(512) for _ in range(4)] for _ in range(2)])
        for_halves(*[p for k in HV.bufs for p in k])
        now_ = Q.last()
        R1 = Ring([PS[:, k, :] for k in range(4)], now_)
        R2 = Ring([PS[:, 4:6, :], PS[:, 6:8, :]], now_)

        def prep(e):
            kw, W, fw = WG.take()
            kd, D, fd = WD.take()
            tw = Q.dma("sync", f"wg{kw}", W, a["wgu"][:, e, :, :], fw, now_)
            td = Q.dma("sync", f"wd{kd}", D, a["wd"][:, e, :, :], fd, now_)
            kh, H, fh = HV.take()
            src = SLT[:, e, :, :].rearrange("p b s -> p (b s)")
            flat = W.rearrange("p a b -> p (a b)")
            t1, t2 = act(f32r(H[0]), flat, ACT.Copy, tw, fh), act(f32r(H[2]), src, ACT.Copy, fh)
            toks = [t1, t2, tt("gpsimd", f32r(H[1]), flat, f32v(H[0]), ALU.subtract, t1, tw, fh),
                    tt("gpsimd", f32r(H[3]), src, f32v(H[2]), ALU.subtract, t2, fh)]
            WG.done(kw, *toks)
            return e, kd, D, td, kh, H, toks

        def up(e, kd, D, td, kh, H, th):
            kg, G, fg = GB.take()
            toks = []
            rhs = (H[2], H[3])
            for f in range(2):
                r, ps, free = R1.take()
                sg_, su = slice(f * 128, f * 128 + 128), slice(256 + f * 128, 384 + f * 128)
                t = M3(ps, (H[0][:, sg_], H[1][:, sg_]), rhs, True, True, th, free)
                r2, ps2, free2 = R1.take()
                t2 = M3(ps2, (H[0][:, su], H[1][:, su]), rhs, True, True, free2)
                t = act(G[:, f, :], ps, ACT.Gelu, t, fg, bias=fb[:, e, 0, f:f + 1])
                R1.done(r, t)
                t = stt(G[:, f, :], ps2, fb[:, e, 1, f:f + 1], G[:, f, :], ALU.add, ALU.mult, t, t2)
                R1.done(r2, t)
                toks.append(t)
            HV.done(kh, t2)
            return e, kd, D, td, kg, G, toks

        def dn(e, kd, D, td, kg, G, toks):
            r, ps, free = R2.take()
            rows = slice(64 * (e % 2), 64 * (e % 2) + 64)
            pv = ps.rearrange("p k (g c) -> p (k g) c", c=128)
            for g, f in [(g + x, f) for g in range(4) for f in range(2) for x in (0, 4)]:
                t = M(pv[rows, g, :], G[:, f, g * 64:g * 64 + 64], D[:, f, :], f == 0, f == 1, toks, td, free)
            WD.done(kd, t)
            GB.done(kg, t)
            t = tt("vector", EO[rows, e // 2, :, :], pv[rows, :, :], bc(bd[rows, e // 2, :].unsqueeze(1), [64, 8, 128]),
                   ALU.add, t, t_bd)
            R2.done(r, t)
            if e % 2:
                hi = EOH[e // 8][:, e // 2 % 4, :, :]
                t1 = act(f32r(hi), EO[:, e // 2, :, :], ACT.Copy, t, t_eo)
                t = tt("gpsimd", f32r(EO[:, e // 2, :, :]), EO[:, e // 2, :, :], f32v(hi), ALU.subtract, t1)
            return t
        prev = None
        t_eo = []
        ahead = prep(0)
        for e in range(16):
            mine, ahead = ahead, prep(e + 1) if e < 15 else None
            cur = up(*mine)
            if prev:
                t_eo.append(dn(*prev))
            prev = cur
        t_eo.append(dn(*prev))

        for e in ("vector", "scalar", "gpsimd", "tensor"):
            Q._waits(e, Q.last())
        top[0] = base
        RS = Ring([PS[:, k, :] for k in range(4)], Q.last())
        R = Ring([PS[:, k, :] for k in range(4, 8)], Q.last())
        SLF = SLT.rearrange("p e b s -> p (e b s)").rearrange("p (x h k t) -> p x h k t", x=2, h=2, k=8)
        PT = Ring([[SLF[:, x, 0], SLF[:, x, 1]] for x in range(2)] + [[take(8, 256), take(8, 256)]])
        for_halves(*[p for k in PT.bufs for p in k])
        PB = Ring([take(512) for _ in range(3)])
        MX, MJ = take(8), take(4)
        DN = take(NT, 2)
        OT = take(256)
        st = {"ot": []}

        def c_mm(v):
            i, x = divmod(v, 2)
            r, S, free = RS.take()
            sl, sx = slice(i * 128, i * 128 + 128), slice(x * 512, x * 512 + 512)
            t = M3(S, (XT[:, sl], XL[:, sl]), (SEH[:, sx], SEL3[:, sx]), True, True, free)
            st["s", v] = (r, S, t)

        def c_soft(v):
            i, x = divmod(v, 2)
            r, S, t = st["s", v]
            m = v % 8
            t = minus_max(MX[:, m:m + 1], S, t)
            if x:
                st["m", i] = tt("vector", MJ[:, i % 4:i % 4 + 1], MX[:, m - 1:m], MX[:, m:m + 1], ALU.min, t,
                                st.get(("e", v - 8)))

        def c_exp(v):
            i, x = divmod(v, 2)
            r, S, _ = st["s", v]
            kp, P, fp = PB.take()
            te = act(P, S, ACT.Exp, st["m", i], fp, bias=MJ[:, i % 4:i % 4 + 1], accum=DN[:, i, x:x + 1])
            RS.done(r, te)
            st["e", v] = te
            st["p", v] = (kp, P)

        def c_hi(v):
            g, q = divmod(v, 4)
            y, x = divmod(q, 2)
            if q == 0:
                st["pt", g] = PT.take()
                st["ptt", g] = []
            k, (PH, PL), free = st["pt", g]
            r, ps, t = st["t", v]
            st["h", v] = act(f32r(PH[:, 4 * x:4 * x + 4, y * 128:y * 128 + 128]), ps.rearrange("p (a b) -> p a b", a=4),
                             ACT.Copy, t, free)

        def c_lo(v):
            g, q = divmod(v, 4)
            y, x = divmod(q, 2)
            k, (PH, PL), free = st["pt", g]
            r, ps, t = st["t", v]
            hi, lo = (P[:, 4 * x:4 * x + 4, y * 128:y * 128 + 128] for P in (PH, PL))
            t2 = tt("vector", f32r(lo), ps.rearrange("p (a b) -> p a b", a=4), f32v(hi), ALU.subtract, t, st["h", v], free)
            R.done(r, t2)
            st["ptt", g].append(t2)
            if q == 3:
                later(1, lambda: c_pv(g, 0))

        def c_pv(g, j):
            if j == 0:
                st["o", g] = R.take()
            r, O, free = st["o", g]
            k, (PH, PL), _ = st["pt", g]
            for y in range(2):
                s_ = 2 * j + y
                b = g // 2
                t = M3(O[:, 0:256], (EOH[s_ // 4][:, s_ % 4, b, :], EO[:, s_, b, :]), (PH[:, s_, :], PL[:, s_, :]), s_ == 0,
                       s_ == 7, st["ptt", g], free)
            if j < 3:
                later(1, lambda: c_pv(g, j + 1))
                return
            PT.done(k, t)
            later(1, lambda: c_copy(g, r, O, t))

        def c_copy(g, r, O, t):
            t = cp("scalar", OT, O[:, 0:256], t, st["ot"])
            i = 2 * g
            t1 = tt("vector", DN[:, i:i + 2, 0], DN[:, i:i + 2, 0], DN[:, i:i + 2, 1], ALU.add, st["e", 4 * g + 3])
            t1 = rec(DN[:, i:i + 2, 0], DN[:, i:i + 2, 0], t1)
            later(1, lambda: c_tr(g, r, O, t, t1))

        def c_tr(g, r, O, t, t1):
            for y in range(2):
                t2 = TR(O[:, 256 + y * 128:384 + y * 128], OT[:, y * 128:y * 128 + 128], t)
            st["ot"] = [t2]
            later(1, lambda: c_out(g, r, O, t2, t1))

        def c_out(g, r, O, t, t1):
            for y in range(2):
                i = 2 * g + y
                t2 = stt(X[:, i, :], O[:, 256 + y * 128:384 + y * 128], DN[:, i, 0:1], X[:, i, :], ALU.mult, ALU.add, t, t1)
            R.done(r, t2)

        NV = 2 * NT
        for v in range(NV + 6):
            for stage, lag in ((c_lo, 6), (c_hi, 5), (c_exp, 3), (c_soft, 1), (p_mm, 4), (c_mm, 0)):
                if 0 <= v - lag < NV:
                    stage(v - lag)
            run_later()
        while todo:
            run_later()

        Q.dma("sync", "out", out, X[:, :, :], Q.last())
        Q._waits("sync", Q.alldma())
        block = ctx.enter_context(nc.Block())
        Q.emit(block)


def layout(inp):
    f = {k: np.asarray(v) for k, v in inp.items()}
    d = constants()

    d["x"] = f["L0_attn_hidden_states"].reshape(NT, 128, 128).transpose(1, 0, 2)
    d["l0_wq"], d["l0_wk"] = f["L0_attn_Wq"], f["L0_attn_Wk"]
    d["l0_wv"], d["l0_wo"] = f["L0_attn_Wv"], f["L0_attn_Wo"]
    d["l0_sw"] = f["L0_ffn_weight"].T
    d["relT"] = f["L0_attn_rel_embeddings"].T
    d["l0_cols"] = np.stack([f["L0_attn_bq"], f["L0_attn_bk"]], 1)
    rep = lambda v: np.tile(np.asarray(v)[None, :], (128, 1))
    d["l0_lnsc"], d["l0_lnb"] = rep(f["L0_attn_ln_scale"]), rep(f["L0_attn_ln_bias"])
    d["l0_bvt"], d["l0_bot"], d["l0_bkt"] = rep(f["L0_attn_bv"]), rep(f["L0_attn_bo"]), rep(f["L0_attn_bk"])[:64]
    for s in "fb":
        d["wz_" + s], d["wh_" + s] = f["L1_attn_Wz_" + s], f["L1_attn_Wh_" + s]
    d["l1_cols"] = np.stack([f["L1_attn_bz_f"], f["L1_attn_bh_f"], f["L1_attn_bz_b"], f["L1_attn_bh_b"]], 1)
    d["l1_wout"] = f["L1_attn_W_out"].reshape(2, 128, 128).transpose(1, 0, 2)
    d["l1_bout"] = rep(f["L1_attn_b_out"])
    d["router"] = f["L1_ffn_w_router"]
    d["wi"] = f["L1_ffn_wi"].transpose(1, 0, 2)
    d["wo2"] = f["L1_ffn_wo"].reshape(8, 4, 128, 128).transpose(2, 0, 1, 3)
    d["ctxT"] = f["L2_attn_context"].reshape(512, 96).T
    d["l2_wqT"] = f["L2_attn_Wq"].reshape(128, 8, 128).transpose(2, 1, 0)
    for s in "kv":
        d["l2_w" + s + "T"] = f["L2_attn_W" + s].reshape(96, 8, 128).transpose(2, 1, 0)
    d["l2_wout"] = f["L2_attn_Wout"].reshape(8, 128, 128).transpose(1, 0, 2)
    d["l2_bout"] = rep(f["L2_attn_bout"])
    d["l2_w"] = np.stack([f["L2_ffn_W_r"].T, f["L2_ffn_W_k"].T, f["L2_ffn_W_v"].T], 1)
    d["l2_mu"] = np.stack([f["L2_ffn_mu_r"], f["L2_ffn_mu_k"]], 1)
    qkv = f["L3_attn_qkv_w"].T
    d["l3_qkv"] = qkv
    qb = f["L3_attn_qkv_b"]
    d["l3_rows"] = rep(np.concatenate([qb[128:], f["L3_attn_p2_b"]]))
    d["l3_cols"] = np.stack([qb[:128], f["L3_attn_p1_b"], np.repeat(f["L3_attn_temperature"].reshape(16), 8)], 1)
    g = np.stack([np.tile(f["L3_attn_kn_g"], 16), np.tile(f["L3_attn_vn_g"], 16)])
    b = np.stack([np.tile(f["L3_attn_kn_b"], 16), np.tile(f["L3_attn_vn_b"], 16)])
    d["l3_gb"] = np.tile(np.stack([g, b])[None].reshape(1, 2, 256), (128, 1, 1))
    ab = np.zeros((16, 8, 16, 8), np.float32)
    for h in range(16):
        ab[h, :, h, :] = f["L3_attn_attn_bias"][h]
    d["l3_ab"] = ab.reshape(128, 128)
    d["l3_p"] = np.stack([f["L3_attn_p1_w"].T, f["L3_attn_p2_w"].T], 1)
    d["l3_ng"], d["l3_nb"] = rep(f["L3_ffn_norm_g"]), rep(f["L3_ffn_norm_b"])
    d["l3_sg"], d["l3_sb"] = rep(f["L3_ffn_slot_g"]), rep(f["L3_ffn_slot_b"])
    d["l3_scale"] = np.tile(f["L3_ffn_scale"][None], (128, 1))
    d["slots"] = f["L3_ffn_slot_embeds"].reshape(8, 128, 128).transpose(1, 0, 2)
    d["wgu"] = np.stack([f["L3_ffn_Wg"], f["L3_ffn_Wu"]], 1).transpose(2, 0, 1, 3)
    d["wd"] = f["L3_ffn_Wd"].reshape(16, 2, 128, 128).transpose(2, 0, 1, 3)
    d["l3_fb"] = np.stack([f["L3_ffn_bg"].reshape(16, 2, 128), f["L3_ffn_bu"].reshape(16, 2, 128)], 1).transpose(3, 0, 1, 2)
    d["l3_bd"] = np.repeat(f["L3_ffn_bd"].reshape(8, 2, 128).transpose(1, 0, 2), 64, axis=0)
    return {k: np.ascontiguousarray(v) for k, v in d.items()}


def kernel(**inputs):
    import concourse.bacc as bacc
    from concourse.bass_utils import run_bass_kernel_spmd

    nc = bacc.Bacc("TRN2", target_bir_lowering=False, num_devices=1)
    arrays = layout(inputs)
    a = {k: nc.dram_tensor("in_" + k, v.shape, mybir.dt.from_np(v.dtype), kind="ExternalInput").ap()
         for k, v in arrays.items()}
    out = nc.dram_tensor("out", (128, NT, 128), F32, kind="ExternalOutput").ap()
    program(nc, a, out)
    r = run_bass_kernel_spmd(nc, [{"in_" + k: v for k, v in arrays.items()}], core_ids=[0])
    y = r.results[0]["out"]
    return np.ascontiguousarray(y.transpose(1, 0, 2)).reshape(8, 512, 128)
```
